# Optimizing a Trainium2 kernel written in Bass

```python
import numpy as np
import jax
import jax.numpy as jnp

def _softmax(x, axis=-1):
    return jax.nn.softmax(x, axis=axis)

def _gelu(x):
    return jax.nn.gelu(x, approximate=True)

def _silu(x):
    return jax.nn.silu(x)

def _sigmoid(x):
    return jax.nn.sigmoid(x)

def _layernorm(x, axis=-1, eps=1e-05):
    m = jnp.mean(x, axis=axis, keepdims=True)
    v = jnp.var(x, axis=axis, keepdims=True)
    return (x - m) / jnp.sqrt(v + eps)

def _scatter_add(tgt, idx, src, axis=0):
    return tgt.at[idx].add(src)

def _segment_sum(src, seg, n):
    return jax.ops.segment_sum(src, seg, n)
kernel_name = 'mk_macaron_d4_jaxref_r8_626636'

def setup_inputs(seed: int=0):
    np.random.seed(seed)
    _w = jnp.asarray

    def _L0_attn_setup():
        import jax, jax.numpy as jnp
        import numpy as np
        B, S, D, H = (2, 256, 128, 16)
        DK = D // H
        key = jax.random.key(seed)
        ks = jax.random.split(key, 9)
        s = 0.02
        return {'embeddings': jax.random.normal(ks[0], (B, S, D), jnp.float32), 'Wq': jax.random.normal(ks[1], (H, D, DK), jnp.float32) * s, 'bq': jax.random.normal(ks[2], (H, DK), jnp.float32) * s, 'Wk': jax.random.normal(ks[3], (H, D, DK), jnp.float32) * s, 'bk': jax.random.normal(ks[4], (H, DK), jnp.float32) * s, 'Wv': jax.random.normal(ks[5], (H, D, DK), jnp.float32) * s, 'bv': jax.random.normal(ks[6], (H, DK), jnp.float32) * s, 'Wo': jax.random.normal(ks[7], (D, D), jnp.float32) * s, 'bo': jax.random.normal(ks[8], (D,), jnp.float32) * s}
    _L0_attn_in = _L0_attn_setup()

    def _L0_ffn_setup():
        import jax, jax.numpy as jnp
        import numpy as np
        B, S, D, F, E = (2, 256, 128, 512, 8)
        LN_EPS = 1e-05

        def _layer_norm(x, gamma, beta):
            mu = jnp.mean(x, axis=-1, keepdims=True)
            var = jnp.mean(jnp.square(x - mu), axis=-1, keepdims=True)
            return (x - mu) * jax.lax.rsqrt(var + LN_EPS) * gamma + beta
        key = jax.random.key(seed)
        ks = jax.random.split(key, 8)

        def xavier(k, shape):
            fan_in, fan_out = (shape[-1], shape[-2])
            a = jnp.sqrt(6.0 / (fan_in + fan_out))
            return jax.random.uniform(k, shape, jnp.float32, -a, a)
        return {'tgt': jax.random.normal(ks[0], (B, S, D), jnp.float32), 'Wr': xavier(ks[1], (E, D)), 'br': jnp.zeros((E,), jnp.float32), 'W1': xavier(ks[2], (E, F, D)), 'b1': jnp.zeros((E, F), jnp.float32), 'W2': xavier(ks[3], (E, D, F)), 'b2': jnp.zeros((E, D), jnp.float32), 'gamma': jnp.ones((D,), jnp.float32), 'beta': jnp.zeros((D,), jnp.float32)}
    _L0_ffn_in = _L0_ffn_setup()

    def _L1_attn_setup():
        import jax, jax.numpy as jnp
        import numpy as np
        B, T, C = (8, 256, 128)
        HS = 64
        H = C // HS
        LORA_R = 32
        TD_R = 64

        def _wkv6(r, k, v, w, u):
            n = r.shape[-1]
            decay = jnp.exp(-jnp.exp(w))

            def per_head(rt, kt, vt, dt, uh):

                def step(S, inp):
                    ri, ki, vi, di = inp
                    kv = ki[:, None] * vi[None, :]
                    y = ri @ (S + uh[:, None] * kv)
                    S = di[:, None] * S + kv
                    return (S, y)
                S0 = jnp.zeros((n, n), rt.dtype)
                _, ys = jax.lax.scan(step, S0, (rt, kt, vt, dt))
                return ys
            f = jax.vmap(per_head, in_axes=(0, 0, 0, 0, 0))
            f = jax.vmap(f, in_axes=(0, 0, 0, 0, None))
            return f(r, k, v, decay, u)
        key = jax.random.key(seed)
        ks = jax.random.split(key, 20)
        inp = {'x': jax.random.normal(ks[0], (B, T, C), jnp.float32), 'miu_x': jax.random.uniform(ks[1], (1, 1, C), jnp.float32), 'lambda_': jax.random.uniform(ks[2], (5, 1, 1, C), jnp.float32), 'A_lora': jax.random.normal(ks[3], (C, LORA_R * 5), jnp.float32) * 0.01, 'B_lora': jax.random.normal(ks[4], (5, LORA_R, C), jnp.float32) * 0.01, 'td_miu': -6.0 + 5.0 * jax.random.uniform(ks[5], (1, 1, C), jnp.float32), 'td_A': jax.random.normal(ks[6], (C, TD_R), jnp.float32) * 0.01, 'td_B': jax.random.normal(ks[7], (TD_R, C), jnp.float32) * 0.01, 'u': jax.random.normal(ks[8], (H, HS), jnp.float32) * 0.1, 'Wr': jax.random.normal(ks[9], (C, C), jnp.float32) * 0.02, 'Wk': jax.random.normal(ks[10], (C, C), jnp.float32) * 0.02, 'Wv': jax.random.normal(ks[11], (C, C), jnp.float32) * 0.02, 'Wg': jax.random.normal(ks[12], (C, C), jnp.float32) * 0.02, 'Wo': jax.random.normal(ks[13], (C, C), jnp.float32) * 0.02, 'gn_gamma': jnp.ones((C,), jnp.float32), 'gn_beta': jnp.zeros((C,), jnp.float32)}
        return inp
    _L1_attn_in = _L1_attn_setup()

    def _L1_ffn_setup():
        import jax, jax.numpy as jnp
        import numpy as np
        INPUT_SIZE = 128
        OUTPUT_SIZE = 128
        key = jax.random.key(seed)
        kx, kt, kp, ktn, kpn = jax.random.split(key, 5)
        x = jax.random.normal(kx, (8, 256, INPUT_SIZE), dtype=jnp.float32)
        theta = jax.random.normal(kt, (INPUT_SIZE, OUTPUT_SIZE), dtype=jnp.float32) * 0.02
        phi = jax.random.normal(kp, (INPUT_SIZE, OUTPUT_SIZE), dtype=jnp.float32) * 0.02
        theta_noise = jax.random.normal(ktn, (INPUT_SIZE, OUTPUT_SIZE), dtype=jnp.float32) * 0.01
        phi_noise = jax.random.normal(kpn, (INPUT_SIZE, OUTPUT_SIZE), dtype=jnp.float32) * 0.01
        return {'x': x, 'theta': theta, 'phi': phi, 'theta_noise': theta_noise, 'phi_noise': phi_noise}
    _L1_ffn_in = _L1_ffn_setup()

    def _L2_attn_setup():
        import jax, jax.numpy as jnp
        import numpy as np
        D_MODEL = 128
        NUM_HEADS = 16
        HEAD_DIM = D_MODEL // NUM_HEADS
        key = jax.random.key(seed)
        ks = jax.random.split(key, 7)
        B, T, C = (4, 256, D_MODEL)
        s = 1.0 / np.sqrt(C)
        return {'x': jax.random.normal(ks[0], (B, T, C), dtype=jnp.float32), 'ln_gamma': jnp.ones((C,), dtype=jnp.float32), 'ln_beta': jnp.zeros((C,), dtype=jnp.float32), 'w_qkv': jax.random.normal(ks[1], (C, 3 * C), dtype=jnp.float32) * s, 'b_qkv': jnp.zeros((3 * C,), dtype=jnp.float32), 'w_out': jax.random.normal(ks[2], (C, C), dtype=jnp.float32) * s, 'b_out': jnp.zeros((C,), dtype=jnp.float32)}
    _L2_attn_in = _L2_attn_setup()

    def _L2_ffn_setup():
        import jax, jax.numpy as jnp
        import numpy as np
        DIM = 128
        DEPTH = 6
        HEADS = 16
        DIM_HEAD = 64
        WINDOW = 32
        INNER = HEADS * DIM_HEAD
        DIM_INNER = int(DIM * 4 * 2 / 3)
        QK_SCALE = 8.0

        def shift_tokens(t):
            a, s = jnp.split(t, 2, -1)
            s = jnp.pad(s, ((0, 0), (1, 0), (0, 0)))[:, :-1]
            return jnp.concatenate([a, s], -1)

        def l2norm(t):
            return t / jnp.maximum(jnp.linalg.norm(t, axis=-1, keepdims=True), 1e-12)

        def rotate_half(x):
            x1, x2 = jnp.split(x, 2, -1)
            return jnp.concatenate([-x2, x1], -1)

        def rotary_tables(n):
            half = jnp.arange(0, DIM_HEAD, 2, dtype=jnp.float32)
            inv_freq = 1.0 / 10000.0 ** (half / DIM_HEAD)
            t = jnp.arange(n, dtype=jnp.float32)
            freqs = t[:, None] * inv_freq[None, :]
            freqs = jnp.concatenate([freqs, freqs], -1)
            base_scale = (half + 0.4 * DIM_HEAD) / (1.4 * DIM_HEAD)
            power = (t - n // 2) / (WINDOW // 2)
            scale = base_scale[None, :] ** power[:, None]
            scale = jnp.concatenate([scale, scale], -1)
            return (freqs, scale)

        def local_attention(q, k, v):
            b, h, n, d = q.shape
            w = WINDOW
            nw = n // w
            bq = q.reshape(b, h, nw, w, d)
            bk = k.reshape(b, h, nw, w, d)
            bv = v.reshape(b, h, nw, w, d)

            def look(t):
                p = jnp.pad(t, ((0, 0), (0, 0), (1, 0), (0, 0), (0, 0)))
                return jnp.concatenate([p[:, :, :nw], p[:, :, 1:]], axis=3)
            bk2, bv2 = (look(bk), look(bv))
            seq = jnp.arange(n).reshape(nw, w)
            seq_p = jnp.pad(seq, ((1, 0), (0, 0)), constant_values=-1)
            jt = jnp.concatenate([seq_p[:nw], seq_p[1:]], axis=1)
            it = seq[:, :, None]
            jb = jt[:, None, :]
            mask = (it < jb) | (it > jb + w) | (jb == -1)
            sim = jnp.einsum('bhwie,bhwje->bhwij', bq, bk2) * QK_SCALE
            sim = jnp.where(mask, -jnp.finfo(sim.dtype).max, sim)
            attn = jax.nn.softmax(sim, -1)
            out = jnp.einsum('bhwij,bhwje->bhwie', attn, bv2)
            return out.reshape(b, h, n, d)

        def attn_layer(x, Wqkv, qs, ksc, Wo):
            b, n, _ = x.shape
            qkv = x @ Wqkv
            q, k, v = jnp.split(qkv, 3, -1)
            sh = lambda t: t.reshape(b, n, HEADS, DIM_HEAD).transpose(0, 2, 1, 3)
            q, k, v = (sh(q), sh(k), sh(v))
            q = l2norm(q) * qs
            k = l2norm(k) * ksc
            freqs, scale = rotary_tables(n)
            cos, sin = (jnp.cos(freqs), jnp.sin(freqs))
            q = q * cos * scale + rotate_half(q) * sin * scale
            inv = 1.0 / scale
            k = k * cos * inv + rotate_half(k) * sin * inv
            out = local_attention(q, k, v)
            out = out.transpose(0, 2, 1, 3).reshape(b, n, INNER)
            return out @ Wo

        def ffn_layer(x, g, bln, W1, b1, W2, b2):
            mu = x.mean(-1, keepdims=True)
            var = ((x - mu) ** 2).mean(-1, keepdims=True)
            xn = (x - mu) / jnp.sqrt(var + 1e-05) * g + bln
            hg = xn @ W1 + b1
            a, gate = jnp.split(hg, 2, -1)
            return a * jax.nn.gelu(gate, approximate=False) @ W2 + b2
        key = jax.random.key(seed)
        ks = jax.random.split(key, 8)
        B, N = (2, 256)
        init = lambda k, shape: jax.random.normal(k, shape, jnp.float32) * 0.02
        return {'x': jax.random.normal(ks[0], (B, N, DIM), jnp.float32), 'Wqkv': init(ks[1], (DEPTH, DIM, 3 * INNER)), 'q_scale': jnp.ones((DEPTH, DIM_HEAD), jnp.float32), 'k_scale': jnp.ones((DEPTH, DIM_HEAD), jnp.float32), 'Wo': init(ks[2], (DEPTH, INNER, DIM)), 'ln_g': jnp.ones((DEPTH, DIM), jnp.float32), 'ln_b': jnp.zeros((DEPTH, DIM), jnp.float32), 'W1': init(ks[3], (DEPTH, DIM, 2 * DIM_INNER)), 'b1': jnp.zeros((DEPTH, 2 * DIM_INNER), jnp.float32), 'W2': init(ks[4], (DEPTH, DIM_INNER, DIM)), 'b2': jnp.zeros((DEPTH, DIM), jnp.float32)}
    _L2_ffn_in = _L2_ffn_setup()

    def _L3_attn_setup():
        import jax, jax.numpy as jnp
        import numpy as np
        N_HEADS = 16

        def _rope_tables(C, d_head):
            i = jnp.arange(d_head // 2, dtype=jnp.float32)
            theta = jnp.power(10000.0, -2.0 * (i - 1.0) / d_head)
            ang = jnp.arange(C, dtype=jnp.float32)[:, None] * theta[None, :]
            return (jnp.cos(ang), jnp.sin(ang))

        def _rotate(t, cos, sin):
            te, to = (t[..., 0::2], t[..., 1::2])
            re = te * cos - to * sin
            ro = te * sin + to * cos
            return jnp.stack([re, ro], axis=-1).reshape(t.shape)
        key = jax.random.key(seed)
        k1, k2, k3 = jax.random.split(key, 3)
        B, C, D = (2, 256, 128)
        x = jax.random.normal(k1, (B, C, D), dtype=jnp.float32)
        Wqkv = jax.random.normal(k2, (D, 3 * D), dtype=jnp.float32) * 0.02
        Wout = jax.random.normal(k3, (D, D), dtype=jnp.float32) * 0.02
        bout = jnp.zeros((D,), dtype=jnp.float32)
        return {'x': x, 'Wqkv': Wqkv, 'Wout': Wout, 'bout': bout}
    _L3_attn_in = _L3_attn_setup()

    def _L3_ffn_setup():
        import jax, jax.numpy as jnp
        import numpy as np
        NUM_EXPERTS = 8
        TOP_K = 2
        key = jax.random.key(seed)
        ks = jax.random.split(key, 5)
        B, L, E, H, N = (2, 256, 128, 256, NUM_EXPERTS)
        return {'x': jax.random.normal(ks[0], (B, L, E), dtype=jnp.float32), 'gate_kernel': jax.random.normal(ks[1], (E, N), dtype=jnp.float32) / np.sqrt(E), 'w0_kernel': jax.random.normal(ks[2], (N, E, H), dtype=jnp.float32) / np.sqrt(E), 'w1_kernel': jax.random.normal(ks[3], (N, E, H), dtype=jnp.float32) / np.sqrt(E), 'wo_kernel': jax.random.normal(ks[4], (N, H, E), dtype=jnp.float32) / np.sqrt(H)}
    _L3_ffn_in = _L3_ffn_setup()
    _d = {'L0_attn_embeddings': _L0_attn_in['embeddings'], 'L0_attn_Wq': _L0_attn_in['Wq'], 'L0_attn_bq': _L0_attn_in['bq'], 'L0_attn_Wk': _L0_attn_in['Wk'], 'L0_attn_bk': _L0_attn_in['bk'], 'L0_attn_Wv': _L0_attn_in['Wv'], 'L0_attn_bv': _L0_attn_in['bv'], 'L0_attn_Wo': _L0_attn_in['Wo'], 'L0_attn_bo': _L0_attn_in['bo'], 'L0_ffn_Wr': _L0_ffn_in['Wr'], 'L0_ffn_br': _L0_ffn_in['br'], 'L0_ffn_W1': _L0_ffn_in['W1'], 'L0_ffn_b1': _L0_ffn_in['b1'], 'L0_ffn_W2': _L0_ffn_in['W2'], 'L0_ffn_b2': _L0_ffn_in['b2'], 'L0_ffn_gamma': _L0_ffn_in['gamma'], 'L0_ffn_beta': _L0_ffn_in['beta'], 'L1_attn_miu_x': _L1_attn_in['miu_x'], 'L1_attn_lambda_': _L1_attn_in['lambda_'], 'L1_attn_A_lora': _L1_attn_in['A_lora'], 'L1_attn_B_lora': _L1_attn_in['B_lora'], 'L1_attn_td_miu': _L1_attn_in['td_miu'], 'L1_attn_td_A': _L1_attn_in['td_A'], 'L1_attn_td_B': _L1_attn_in['td_B'], 'L1_attn_u': _L1_attn_in['u'], 'L1_attn_Wr': _L1_attn_in['Wr'], 'L1_attn_Wk': _L1_attn_in['Wk'], 'L1_attn_Wv': _L1_attn_in['Wv'], 'L1_attn_Wg': _L1_attn_in['Wg'], 'L1_attn_Wo': _L1_attn_in['Wo'], 'L1_attn_gn_gamma': _L1_attn_in['gn_gamma'], 'L1_attn_gn_beta': _L1_attn_in['gn_beta'], 'L1_ffn_theta': _L1_ffn_in['theta'], 'L1_ffn_phi': _L1_ffn_in['phi'], 'L1_ffn_theta_noise': _L1_ffn_in['theta_noise'], 'L1_ffn_phi_noise': _L1_ffn_in['phi_noise'], 'L2_attn_ln_gamma': _L2_attn_in['ln_gamma'], 'L2_attn_ln_beta': _L2_attn_in['ln_beta'], 'L2_attn_w_qkv': _L2_attn_in['w_qkv'], 'L2_attn_b_qkv': _L2_attn_in['b_qkv'], 'L2_attn_w_out': _L2_attn_in['w_out'], 'L2_attn_b_out': _L2_attn_in['b_out'], 'L2_ffn_Wqkv': _L2_ffn_in['Wqkv'], 'L2_ffn_q_scale': _L2_ffn_in['q_scale'], 'L2_ffn_k_scale': _L2_ffn_in['k_scale'], 'L2_ffn_Wo': _L2_ffn_in['Wo'], 'L2_ffn_ln_g': _L2_ffn_in['ln_g'], 'L2_ffn_ln_b': _L2_ffn_in['ln_b'], 'L2_ffn_W1': _L2_ffn_in['W1'], 'L2_ffn_b1': _L2_ffn_in['b1'], 'L2_ffn_W2': _L2_ffn_in['W2'], 'L2_ffn_b2': _L2_ffn_in['b2'], 'L3_attn_Wqkv': _L3_attn_in['Wqkv'], 'L3_attn_Wout': _L3_attn_in['Wout'], 'L3_attn_bout': _L3_attn_in['bout'], 'L3_ffn_gate_kernel': _L3_ffn_in['gate_kernel'], 'L3_ffn_w0_kernel': _L3_ffn_in['w0_kernel'], 'L3_ffn_w1_kernel': _L3_ffn_in['w1_kernel'], 'L3_ffn_wo_kernel': _L3_ffn_in['wo_kernel']}
    _x0 = _d['L0_attn_embeddings']
    _d['L0_attn_embeddings'] = jax.random.normal(jax.random.fold_in(jax.random.key(seed), 1), (8, 256, 128), dtype=_x0.dtype)
    del _x0
    return _d

def reference(L0_attn_embeddings, L0_attn_Wq, L0_attn_bq, L0_attn_Wk, L0_attn_bk, L0_attn_Wv, L0_attn_bv, L0_attn_Wo, L0_attn_bo, L0_ffn_Wr, L0_ffn_br, L0_ffn_W1, L0_ffn_b1, L0_ffn_W2, L0_ffn_b2, L0_ffn_gamma, L0_ffn_beta, L1_attn_miu_x, L1_attn_lambda_, L1_attn_A_lora, L1_attn_B_lora, L1_attn_td_miu, L1_attn_td_A, L1_attn_td_B, L1_attn_u, L1_attn_Wr, L1_attn_Wk, L1_attn_Wv, L1_attn_Wg, L1_attn_Wo, L1_attn_gn_gamma, L1_attn_gn_beta, L1_ffn_theta, L1_ffn_phi, L1_ffn_theta_noise, L1_ffn_phi_noise, L2_attn_ln_gamma, L2_attn_ln_beta, L2_attn_w_qkv, L2_attn_b_qkv, L2_attn_w_out, L2_attn_b_out, L2_ffn_Wqkv, L2_ffn_q_scale, L2_ffn_k_scale, L2_ffn_Wo, L2_ffn_ln_g, L2_ffn_ln_b, L2_ffn_W1, L2_ffn_b1, L2_ffn_W2, L2_ffn_b2, L3_attn_Wqkv, L3_attn_Wout, L3_attn_bout, L3_ffn_gate_kernel, L3_ffn_w0_kernel, L3_ffn_w1_kernel, L3_ffn_wo_kernel):

    def _L0_attn_ref(embeddings, Wq, bq, Wk, bk, Wv, bv, Wo, bo):
        import jax, jax.numpy as jnp
        import numpy as np
        B, S, D, H = (2, 256, 128, 16)
        DK = D // H
        b, s, d = embeddings.shape
        dk = Wq.shape[-1]
        q = jnp.einsum('bsd,hdk->bhsk', embeddings, Wq) + bq[None, :, None, :]
        k = jnp.einsum('bsd,hdk->bhsk', embeddings, Wk) + bk[None, :, None, :]
        v = jnp.einsum('bsd,hdk->bhsk', embeddings, Wv) + bv[None, :, None, :]
        scores = jnp.einsum('bhqk,bhsk->bhqs', q, k) / jnp.sqrt(jnp.float32(dk))
        causal_mask = jnp.triu(jnp.ones((s, s), dtype=bool), k=1)
        scores = jnp.where(causal_mask, jnp.float32(-1000000000.0), scores)
        weights = jax.nn.softmax(scores, axis=-1)
        ctx = jnp.einsum('bhqs,bhsk->bhqk', weights, v)
        concat = ctx.transpose(0, 2, 1, 3).reshape(b, s, d)
        return concat @ Wo + bo

    def _L0_ffn_ref(tgt, Wr, br, W1, b1, W2, b2, gamma, beta):
        import jax, jax.numpy as jnp
        import numpy as np
        B, S, D, F, E = (2, 256, 128, 512, 8)
        LN_EPS = 1e-05

        def _layer_norm(x, gamma, beta):
            mu = jnp.mean(x, axis=-1, keepdims=True)
            var = jnp.mean(jnp.square(x - mu), axis=-1, keepdims=True)
            return (x - mu) * jax.lax.rsqrt(var + LN_EPS) * gamma + beta
        logits = jnp.einsum('bsd,ed->bse', tgt, Wr) + br
        top_v, top_i = jax.lax.top_k(logits, 2)
        top_w = jax.nn.softmax(top_v, axis=-1)
        n_exp = logits.shape[-1]
        router_w = jnp.sum(jax.nn.one_hot(top_i, n_exp, dtype=top_w.dtype) * top_w[..., None], axis=-2)
        h = jnp.einsum('bsd,efd->bsef', tgt, W1) + b1
        h = jax.nn.relu(h)
        o = jnp.einsum('bsef,edf->bsed', h, W2) + b2
        tgt2 = jnp.einsum('bsed,bse->bsd', o, router_w)
        return _layer_norm(tgt + tgt2, gamma, beta)

    def _L1_attn_ref(x, miu_x, lambda_, A_lora, B_lora, td_miu, td_A, td_B, u, Wr, Wk, Wv, Wg, Wo, gn_gamma, gn_beta):
        import jax, jax.numpy as jnp
        import numpy as np
        B, T, C = (8, 256, 128)
        HS = 64
        H = C // HS
        LORA_R = 32
        TD_R = 64

        def _wkv6(r, k, v, w, u):
            n = r.shape[-1]
            decay = jnp.exp(-jnp.exp(w))

            def per_head(rt, kt, vt, dt, uh):

                def step(S, inp):
                    ri, ki, vi, di = inp
                    kv = ki[:, None] * vi[None, :]
                    y = ri @ (S + uh[:, None] * kv)
                    S = di[:, None] * S + kv
                    return (S, y)
                S0 = jnp.zeros((n, n), rt.dtype)
                _, ys = jax.lax.scan(step, S0, (rt, kt, vt, dt))
                return ys
            f = jax.vmap(per_head, in_axes=(0, 0, 0, 0, 0))
            f = jax.vmap(f, in_axes=(0, 0, 0, 0, None))
            return f(r, k, v, decay, u)
        b, t, c = x.shape
        h, n = u.shape
        x_last = jnp.pad(x, ((0, 0), (1, 0), (0, 0)))[:, :t]
        dxa = x_last - x
        xm = x + dxa * miu_x
        lora_h = jnp.tanh(xm @ A_lora).reshape(b, t, 5, -1)
        miu = lambda_ + jnp.einsum('btfi,fic->fbtc', lora_h, B_lora)
        xx = x[None] + dxa[None] * miu
        w_in, k_in, v_in, r_in, g_in = xx
        k = k_in @ Wk.T
        v = v_in @ Wv.T
        r = r_in @ Wr.T
        g = jax.nn.silu(g_in @ Wg.T)
        w = td_miu + jnp.tanh(w_in @ td_A) @ td_B

        def to_heads(z):
            return z.reshape(b, t, h, n).transpose(0, 2, 1, 3)
        y = _wkv6(to_heads(r), to_heads(k), to_heads(v), to_heads(w), u)
        y = y.transpose(0, 2, 1, 3)
        eps = 1e-05 * h
        mean = y.mean(-1, keepdims=True)
        var = y.var(-1, keepdims=True)
        yn = (y - mean) * jax.lax.rsqrt(var + eps)
        yn = yn * gn_gamma.reshape(h, n) + gn_beta.reshape(h, n)
        yn = yn.reshape(b, t, c)
        return yn * g @ Wo.T

    def _L1_ffn_ref(x, theta, phi, theta_noise, phi_noise):
        import jax, jax.numpy as jnp
        import numpy as np
        INPUT_SIZE = 128
        OUTPUT_SIZE = 128
        real = jnp.einsum('bti,io->bto', x, jnp.cos(theta + theta_noise))
        imag = jnp.einsum('bti,io->bto', x, jnp.sin(phi + phi_noise))
        return jnp.sqrt(real * real + imag * imag)

    def _L2_attn_ref(x, ln_gamma, ln_beta, w_qkv, b_qkv, w_out, b_out):
        import jax, jax.numpy as jnp
        import numpy as np
        D_MODEL = 128
        NUM_HEADS = 16
        HEAD_DIM = D_MODEL // NUM_HEADS
        B, T, C = x.shape
        residual = x
        mu = jnp.mean(x, axis=-1, keepdims=True)
        var = jnp.var(x, axis=-1, keepdims=True)
        h = (x - mu) * jax.lax.rsqrt(var + 1e-05) * ln_gamma + ln_beta
        qkv = (h @ w_qkv + b_qkv).reshape(B, T, 3, NUM_HEADS, HEAD_DIM)
        qkv = jnp.transpose(qkv, (2, 0, 3, 1, 4))
        q, k, v = (qkv[0], qkv[1], qkv[2])
        scores = jnp.einsum('bhqd,bhkd->bhqk', q, k) / np.sqrt(HEAD_DIM)
        attn = jax.nn.softmax(scores, axis=-1)
        out = jnp.einsum('bhqk,bhkd->bhqd', attn, v)
        out = jnp.transpose(out, (0, 2, 1, 3)).reshape(B, T, C)
        out = out @ w_out + b_out
        return residual + out

    def _L2_ffn_ref(x, Wqkv, q_scale, k_scale, Wo, ln_g, ln_b, W1, b1, W2, b2):
        import jax, jax.numpy as jnp
        import numpy as np
        DIM = 128
        DEPTH = 6
        HEADS = 16
        DIM_HEAD = 64
        WINDOW = 32
        INNER = HEADS * DIM_HEAD
        DIM_INNER = int(DIM * 4 * 2 / 3)
        QK_SCALE = 8.0

        def shift_tokens(t):
            a, s = jnp.split(t, 2, -1)
            s = jnp.pad(s, ((0, 0), (1, 0), (0, 0)))[:, :-1]
            return jnp.concatenate([a, s], -1)

        def l2norm(t):
            return t / jnp.maximum(jnp.linalg.norm(t, axis=-1, keepdims=True), 1e-12)

        def rotate_half(x):
            x1, x2 = jnp.split(x, 2, -1)
            return jnp.concatenate([-x2, x1], -1)

        def rotary_tables(n):
            half = jnp.arange(0, DIM_HEAD, 2, dtype=jnp.float32)
            inv_freq = 1.0 / 10000.0 ** (half / DIM_HEAD)
            t = jnp.arange(n, dtype=jnp.float32)
            freqs = t[:, None] * inv_freq[None, :]
            freqs = jnp.concatenate([freqs, freqs], -1)
            base_scale = (half + 0.4 * DIM_HEAD) / (1.4 * DIM_HEAD)
            power = (t - n // 2) / (WINDOW // 2)
            scale = base_scale[None, :] ** power[:, None]
            scale = jnp.concatenate([scale, scale], -1)
            return (freqs, scale)

        def local_attention(q, k, v):
            b, h, n, d = q.shape
            w = WINDOW
            nw = n // w
            bq = q.reshape(b, h, nw, w, d)
            bk = k.reshape(b, h, nw, w, d)
            bv = v.reshape(b, h, nw, w, d)

            def look(t):
                p = jnp.pad(t, ((0, 0), (0, 0), (1, 0), (0, 0), (0, 0)))
                return jnp.concatenate([p[:, :, :nw], p[:, :, 1:]], axis=3)
            bk2, bv2 = (look(bk), look(bv))
            seq = jnp.arange(n).reshape(nw, w)
            seq_p = jnp.pad(seq, ((1, 0), (0, 0)), constant_values=-1)
            jt = jnp.concatenate([seq_p[:nw], seq_p[1:]], axis=1)
            it = seq[:, :, None]
            jb = jt[:, None, :]
            mask = (it < jb) | (it > jb + w) | (jb == -1)
            sim = jnp.einsum('bhwie,bhwje->bhwij', bq, bk2) * QK_SCALE
            sim = jnp.where(mask, -jnp.finfo(sim.dtype).max, sim)
            attn = jax.nn.softmax(sim, -1)
            out = jnp.einsum('bhwij,bhwje->bhwie', attn, bv2)
            return out.reshape(b, h, n, d)

        def attn_layer(x, Wqkv, qs, ksc, Wo):
            b, n, _ = x.shape
            qkv = x @ Wqkv
            q, k, v = jnp.split(qkv, 3, -1)
            sh = lambda t: t.reshape(b, n, HEADS, DIM_HEAD).transpose(0, 2, 1, 3)
            q, k, v = (sh(q), sh(k), sh(v))
            q = l2norm(q) * qs
            k = l2norm(k) * ksc
            freqs, scale = rotary_tables(n)
            cos, sin = (jnp.cos(freqs), jnp.sin(freqs))
            q = q * cos * scale + rotate_half(q) * sin * scale
            inv = 1.0 / scale
            k = k * cos * inv + rotate_half(k) * sin * inv
            out = local_attention(q, k, v)
            out = out.transpose(0, 2, 1, 3).reshape(b, n, INNER)
            return out @ Wo

        def ffn_layer(x, g, bln, W1, b1, W2, b2):
            mu = x.mean(-1, keepdims=True)
            var = ((x - mu) ** 2).mean(-1, keepdims=True)
            xn = (x - mu) / jnp.sqrt(var + 1e-05) * g + bln
            hg = xn @ W1 + b1
            a, gate = jnp.split(hg, 2, -1)
            return a * jax.nn.gelu(gate, approximate=False) @ W2 + b2
        for i in range(DEPTH):
            x = attn_layer(shift_tokens(x), Wqkv[i], q_scale[i], k_scale[i], Wo[i]) + x
            x = ffn_layer(shift_tokens(x), ln_g[i], ln_b[i], W1[i], b1[i], W2[i], b2[i]) + x
        return x

    def _L3_attn_ref(x, Wqkv, Wout, bout):
        import jax, jax.numpy as jnp
        import numpy as np
        N_HEADS = 16

        def _rope_tables(C, d_head):
            i = jnp.arange(d_head // 2, dtype=jnp.float32)
            theta = jnp.power(10000.0, -2.0 * (i - 1.0) / d_head)
            ang = jnp.arange(C, dtype=jnp.float32)[:, None] * theta[None, :]
            return (jnp.cos(ang), jnp.sin(ang))

        def _rotate(t, cos, sin):
            te, to = (t[..., 0::2], t[..., 1::2])
            re = te * cos - to * sin
            ro = te * sin + to * cos
            return jnp.stack([re, ro], axis=-1).reshape(t.shape)
        B, C, D = x.shape
        H = N_HEADS
        dh = D // H
        qkv = x @ Wqkv
        q, k, v = jnp.split(qkv, 3, axis=-1)
        q = q.reshape(B, C, H, dh).transpose(0, 2, 1, 3)
        k = k.reshape(B, C, H, dh).transpose(0, 2, 1, 3)
        v = v.reshape(B, C, H, dh).transpose(0, 2, 1, 3)
        cos, sin = _rope_tables(C, dh)
        q_rot = _rotate(q, cos, sin)
        k_rot = _rotate(k, cos, sin)
        scale = 1.0 / jnp.sqrt(jnp.asarray(dh, dtype=x.dtype))
        num = jnp.exp(jnp.einsum('bhqd,bhkd->bhqk', q_rot, k_rot) * scale)
        den = jnp.sum(jnp.exp(jnp.einsum('bhqd,bhkd->bhqk', q, k) * scale), axis=-1, keepdims=True)
        attn = num / den
        causal = jnp.tril(jnp.ones((C, C), dtype=bool))
        attn = jnp.where(causal[None, None], attn, 0.0)
        y = jnp.einsum('bhqk,bhkd->bhqd', attn, v)
        y = y.transpose(0, 2, 1, 3).reshape(B, C, D)
        return y @ Wout + bout

    def _L3_ffn_ref(x, gate_kernel, w0_kernel, w1_kernel, wo_kernel):
        import jax, jax.numpy as jnp
        import numpy as np
        NUM_EXPERTS = 8
        TOP_K = 2
        B, L, E = x.shape
        gate_logits = jnp.einsum('ble,en->bln', x, gate_kernel)
        top_k_weights, top_k_indices = jax.lax.top_k(gate_logits, TOP_K)
        softmax_probs = jax.nn.softmax(top_k_weights.astype(jnp.float32), axis=-1)
        weights = jnp.zeros_like(gate_logits)
        b_idx = jnp.arange(B)[:, None, None]
        l_idx = jnp.arange(L)[:, None]
        weights = weights.at[b_idx, l_idx, top_k_indices].set(softmax_probs)
        layer_w0 = jnp.einsum('ble,neh->blnh', x, w0_kernel)
        layer_w1 = jnp.einsum('ble,neh->blnh', x, w1_kernel)
        layer_mult = jax.nn.silu(layer_w0) * layer_w1
        intermediate = jnp.einsum('blnh,nhe->blne', layer_mult, wo_kernel)
        output = jnp.einsum('blne,bln->ble', intermediate, weights)
        return output
    x = L0_attn_embeddings
    x = x + 0.5 * _L0_ffn_ref(_layernorm(x, axis=-1), L0_ffn_Wr, L0_ffn_br, L0_ffn_W1, L0_ffn_b1, L0_ffn_W2, L0_ffn_b2, L0_ffn_gamma, L0_ffn_beta)
    x = x + _L0_attn_ref(_layernorm(x, axis=-1), L0_attn_Wq, L0_attn_bq, L0_attn_Wk, L0_attn_bk, L0_attn_Wv, L0_attn_bv, L0_attn_Wo, L0_attn_bo)
    x = x + 0.5 * _L0_ffn_ref(_layernorm(x, axis=-1), L0_ffn_Wr, L0_ffn_br, L0_ffn_W1, L0_ffn_b1, L0_ffn_W2, L0_ffn_b2, L0_ffn_gamma, L0_ffn_beta)
    x = x + 0.5 * _L1_ffn_ref(_layernorm(x, axis=-1), L1_ffn_theta, L1_ffn_phi, L1_ffn_theta_noise, L1_ffn_phi_noise)
    x = x + _L1_attn_ref(_layernorm(x, axis=-1), L1_attn_miu_x, L1_attn_lambda_, L1_attn_A_lora, L1_attn_B_lora, L1_attn_td_miu, L1_attn_td_A, L1_attn_td_B, L1_attn_u, L1_attn_Wr, L1_attn_Wk, L1_attn_Wv, L1_attn_Wg, L1_attn_Wo, L1_attn_gn_gamma, L1_attn_gn_beta)
    x = x + 0.5 * _L1_ffn_ref(_layernorm(x, axis=-1), L1_ffn_theta, L1_ffn_phi, L1_ffn_theta_noise, L1_ffn_phi_noise)
    x = x + 0.5 * _L2_ffn_ref(_layernorm(x, axis=-1), L2_ffn_Wqkv, L2_ffn_q_scale, L2_ffn_k_scale, L2_ffn_Wo, L2_ffn_ln_g, L2_ffn_ln_b, L2_ffn_W1, L2_ffn_b1, L2_ffn_W2, L2_ffn_b2)
    x = x + _L2_attn_ref(_layernorm(x, axis=-1), L2_attn_ln_gamma, L2_attn_ln_beta, L2_attn_w_qkv, L2_attn_b_qkv, L2_attn_w_out, L2_attn_b_out)
    x = x + 0.5 * _L2_ffn_ref(_layernorm(x, axis=-1), L2_ffn_Wqkv, L2_ffn_q_scale, L2_ffn_k_scale, L2_ffn_Wo, L2_ffn_ln_g, L2_ffn_ln_b, L2_ffn_W1, L2_ffn_b1, L2_ffn_W2, L2_ffn_b2)
    x = x + 0.5 * _L3_ffn_ref(_layernorm(x, axis=-1), L3_ffn_gate_kernel, L3_ffn_w0_kernel, L3_ffn_w1_kernel, L3_ffn_wo_kernel)
    x = x + _L3_attn_ref(_layernorm(x, axis=-1), L3_attn_Wqkv, L3_attn_Wout, L3_attn_bout)
    x = x + 0.5 * _L3_ffn_ref(_layernorm(x, axis=-1), L3_ffn_gate_kernel, L3_ffn_w0_kernel, L3_ffn_w1_kernel, L3_ffn_wo_kernel)
    return x

_drawn_inputs = setup_inputs


def setup_inputs(seed=0):
    import zlib

    import numpy as np

    out = dict(_drawn_inputs(seed))
    spreads = {'L0_ffn_br': (0.0, 0.1),
     'L0_ffn_b1': (0.0, 0.1),
     'L0_ffn_b2': (0.0, 0.1),
     'L0_ffn_gamma': (1.0, 0.2),
     'L0_ffn_beta': (0.0, 0.1),
     'L1_attn_gn_gamma': (1.0, 0.2),
     'L1_attn_gn_beta': (0.0, 0.1),
     'L2_attn_ln_gamma': (1.0, 0.2),
     'L2_attn_ln_beta': (0.0, 0.1),
     'L2_attn_b_qkv': (0.0, 0.1),
     'L2_attn_b_out': (0.0, 0.1),
     'L2_ffn_q_scale': (1.0, 0.2),
     'L2_ffn_k_scale': (1.0, 0.2),
     'L2_ffn_ln_g': (1.0, 0.2),
     'L2_ffn_ln_b': (0.0, 0.1),
     'L2_ffn_b1': (0.0, 0.1),
     'L2_ffn_b2': (0.0, 0.1),
     'L3_attn_bout': (0.0, 0.1)}
    factors = {}
    for name, (base, spread) in spreads.items():
        noise = np.random.default_rng([zlib.crc32(name.encode()), seed]).standard_normal(out[name].shape)
        drawn = base * np.exp(spread * noise) if base else spread * noise
        out[name] = jnp.asarray(drawn.astype(out[name].dtype))
    for name, factor in factors.items():
        out[name] = (out[name] * factor).astype(out[name].dtype)
    return out
```

```python
from contextlib import ExitStack

import numpy as np
import concourse.bass as bass
from concourse import mybir

ALU = mybir.AluOpType
ACT = mybir.ActivationFunctionType
AX = mybir.AxisListType
F32 = mybir.dt.float32
BF16 = mybir.dt.bfloat16
U32 = mybir.dt.uint32

P = 128
D = 128
B, SEQ = 8, 256
TILES = B * SEQ // P
HALVES = SEQ // P
HEADS, DK = 16, 8
EPS = 1e-5
MASKED = -1e30


class Signals:

    def __init__(self, nc, ctx, stage, seeded=False, **per):
        names = list(per) + ["apart"] * ("apart" not in per)
        self.sems = {name: ctx.enter_context(nc.semaphore(stage + "_" + name)) for name in names}
        self.per = per
        self.base = {name: int(seeded) for name in per}

    def __getitem__(self, name):
        return self.sems[name]

    def __call__(self, name, step, k=0):
        return self.sems[name], step * self.per[name] + (self.base[name] + k)

    def use(self, per):
        assert set(per) <= set(self.sems)
        self.per = per

    def seed(self, eng):
        for sem in self.sems.values():
            eng.sem_inc(sem, 1)

    def apart(self, eng, name, step, k):
        eng.wait_ge(*self(name, step, k))
        self.settle(eng)

    def settle(self, eng):
        eng.sem_inc(self.sems["apart"], 1)

    def ended(self, steps):
        for name, n in self.per.items():
            self.base[name] += n * steps


class Chain:

    def __init__(self, eng, signals, name, step):
        self.eng, self.signals, self.name, self.step, self.n = eng, signals, name, step, 0

    def __call__(self, ins):
        ins.then_inc(self.signals[self.name], 1)
        self.n += 1
        self.eng.wait_ge(*self.signals(self.name, self.step, self.n))

    def apart(self, ins):
        ins.then_inc(self.signals[self.name], 1)
        self.n += 1
        self.signals.apart(self.eng, self.name, self.step, self.n)

    def done(self):
        assert self.n == self.signals.per[self.name], (self.name, self.n)


class Chip:

    def __init__(self, nc, ctx, dram, loop_names):
        self.nc, self.ctx, self.dram = nc, ctx, dram
        self.tag = ""
        self.loop = Signals(nc, ctx, "loop", seeded=True, **dict.fromkeys(loop_names, 0))
        self.ffn = Signals(nc, ctx, "ffn", seeded=True, **STACK_FFN)
        self.once = Signals(nc, ctx, "once", **dict.fromkeys(["loaded", "set", "reduced", "chain"] + [f"experts{n}" for n in range(LOADS)], 0))
        self.layer = Signals(nc, ctx, "layer", **STACK_LAYER)
        self.x = ctx.enter_context(nc.sbuf_tensor("x_all", [P, TILES, D], F32))
        self.ident = ctx.enter_context(nc.sbuf_tensor("ident", [P, P], F32))
        self.eps = ctx.enter_context(nc.sbuf_tensor("eps", [P, 1], F32))


NORM_SIGNALS = dict(norm_chain=1, moments=1, act_norm=1, rstd=1, xn=1, xT_psum=1, xT=1)


class Norm:
    def __init__(self, chip, ctx, tiles, turned=True):
        self.tiles = tiles
        sb = lambda name, shape: ctx.enter_context(chip.nc.sbuf_tensor(chip.tag + "norm_" + name, shape, F32))
        self.stats = sb("stats", [P, tiles, 6])
        self.moments = sb("moments", [P, tiles, 2])
        self.logvar = sb("logvar", [P, tiles])
        self.rstd = sb("rstd", [P, tiles])
        if not turned:
            return
        self.xn = sb("xn", [P, tiles, D])
        self.xT = sb("xT", [P, tiles * P])
        self.psum = ctx.enter_context(chip.nc.psum_tensor(chip.tag + "norm_psum", [P, 512], F32))


def norm_vector(nc, dve, sig, m, step, source, target, used, which=""):
    T = m.tiles
    for t in range(T):
        ins = nc.vector.bn_stats(m.stats[:, t, :], source(t))
    ins.then_inc(sig["norm_chain" + which], 1)
    sig.apart(dve, "norm_chain" + which, step, 1)
    for t in range(T):
        ins = nc.vector.bn_aggr(m.moments[:, t, :], m.stats[:, t, :])
    ins.then_inc(sig["moments" + which], 1)
    dve.wait_ge(*sig("rstd" + which, step, 1))
    for name in used:
        dve.wait_ge(*sig(name, step))
    for t in range(T):
        ins = nc.vector.tensor_scalar(target(t), source(t), m.moments[:, t, 0:1], m.rstd[:, t:t + 1],
                                      ALU.subtract, ALU.mult)
    ins.then_inc(sig["xn" + which], 1)


def norm_rstd(nc, act, sig, chip, m, step, which=""):
    act.wait_ge(*sig("moments" + which, step, 1))
    nc.scalar.activation(m.logvar[:, :], m.moments[:, :, 1], ACT.Ln, bias=chip.eps[:, 0:1]).then_inc(sig["act_norm" + which], 1)
    act.wait_ge(*sig("act_norm" + which, step, 1))
    nc.scalar.activation(m.rstd[:, :], m.logvar[:, :], ACT.Exp, scale=-0.5).then_inc(sig["rstd" + which], 1)


def norm_transpose(nc, pe, sig, chip, m, step):
    pe.wait_ge(*sig("xn", step, 1))
    pe.wait_ge(*sig("xT", step))
    for t in range(m.tiles):
        ins = nc.tensor.transpose(m.psum[:, t * P:(t + 1) * P], m.xn[:, t, :], chip.ident[:, :])
    ins.then_inc(sig["xT_psum"], 1)


def norm_xT(nc, act, sig, m, step, xT_used):
    act.wait_ge(*sig("xT_psum", step, 1))
    for name in xT_used:
        act.wait_ge(*sig(name, step))
    nc.scalar.activation(m.xT[:, :], m.psum[:, 0:m.tiles * P], ACT.Copy).then_inc(sig["xT"], 1)


def x_tile(chip, step, tiles):
    return lambda t: chip.x[:, bass.ds(step * tiles + t, 1), :].rearrange("p a d -> p (a d)")


TWO_PI = 2 * np.pi
TWO_PI_1 = 6.28125
TWO_PI_2 = float(np.float32(np.round((TWO_PI - TWO_PI_1) * 2 ** 20) / 2 ** 20))
TWO_PI_3 = TWO_PI - TWO_PI_1 - TWO_PI_2
ROUNDER = 1.5 * 2 ** 23
PI_BELOW = 3.1415925


def setup_l1_angles(chip, cossin):
    nc = chip.nc
    with ExitStack() as ctx:
        sb = lambda name, shape: ctx.enter_context(nc.sbuf_tensor("angle_" + name, shape, F32))
        parts, angle, turns = sb("parts", [P, 4, D]), sb("sum", [P, 2, D]), sb("turns", [P, 2, D])
        sig = chip.once
        sig.use(dict(loaded=64, chain=10, reduced=1, set=1))
        block = ctx.enter_context(nc.Block())

        @block.sync
        def _(sp):
            for n, name in enumerate(["L1_ffn_theta", "L1_ffn_phi", "L1_ffn_theta_noise", "L1_ffn_phi_noise"]):
                sp.dma_start(parts[:, n, :], chip.dram[name]).then_inc(sig["loaded"], 16)

        @block.vector
        def _(dve):
            chain = Chain(dve, sig, "chain", 0)
            dve.wait_ge(*sig("loaded", 1))
            chain(nc.vector.tensor_tensor(angle[:, :, :], parts[:, 0:2, :], parts[:, 2:4, :], ALU.add))
            chain(nc.vector.tensor_scalar(turns[:, 0, :], angle[:, 0, :], 1 / TWO_PI, 0.25, ALU.mult, ALU.add))
            chain(nc.vector.tensor_scalar(turns[:, 1, :], angle[:, 1, :], 1 / TWO_PI, None, ALU.mult))
            chain(nc.vector.tensor_scalar(turns[:, :, :], turns[:, :, :], ROUNDER, None, ALU.add))
            chain(nc.vector.tensor_scalar(turns[:, :, :], turns[:, :, :], ROUNDER, None, ALU.subtract))
            for part in (TWO_PI_1, TWO_PI_2, TWO_PI_3):
                chain(nc.vector.scalar_tensor_tensor(angle[:, :, :], turns[:, :, :], -part, angle[:, :, :], ALU.mult, ALU.add))
            chain(nc.vector.tensor_scalar(angle[:, 0, :], angle[:, 0, :], np.pi / 2, None, ALU.add))
            chain(nc.vector.tensor_scalar(angle[:, :, :], angle[:, :, :], PI_BELOW, -PI_BELOW, ALU.min, ALU.max))
            chain.done()
            nc.vector.engine_nop().then_inc(sig["reduced"], 1)

        @block.scalar
        def _(act):
            act.wait_ge(*sig("reduced", 1))
            nc.scalar.activation(cossin[:, :, :], angle[:, :, :], ACT.Sin).then_inc(sig["set"], 1)
            act.wait_ge(*sig("set", 1))
    sig.ended(1)


def stage_l1_ffn(chip, cossin):
    nc, sig = chip.nc, chip.loop
    sig.use(L1_FFN_SIGNALS)
    T = 4
    with ExitStack() as ctx:
        m = Norm(chip, ctx, T)
        squares = ctx.enter_context(nc.sbuf_tensor(chip.tag + "squares", [P, T, 2, D], F32))
        norm2 = ctx.enter_context(nc.sbuf_tensor(chip.tag + "norm2", [P, T, D], F32))
        waves = ctx.enter_context(nc.psum_tensor(chip.tag + "waves", [P, T, 2, D], F32))
        block = ctx.enter_context(nc.Block())
        steps = TILES // T

        @block.vector
        def _(dve):
            with dve.Fori(0, steps) as step:
                norm_vector(nc, dve, sig, m, step, x_tile(chip, step, T), lambda t: m.xn[:, t, :], ["xT_psum"])
                dve.wait_ge(*sig("squares", step, 1))
                nc.vector.tensor_tensor(norm2[:, :, :], squares[:, :, 0, :], squares[:, :, 1, :], ALU.add)\
                  .then_inc(sig["norm2"], 1)
                dve.wait_ge(*sig("root", step, 1))
                x = chip.x[:, bass.ds(step * T, T), :]
                nc.vector.scalar_tensor_tensor(x, norm2[:, :, :], 0.5, x, ALU.mult, ALU.add).then_inc(sig["x"], 1)
                dve.wait_ge(*sig("x", step, 1))

        @block.scalar
        def _(act):
            with act.Fori(0, steps) as step:
                norm_rstd(nc, act, sig, chip, m, step)
                norm_xT(nc, act, sig, m, step, ["waves"])
                act.wait_ge(*sig("waves", step, 1))
                act.wait_ge(*sig("norm2", step))
                nc.scalar.activation(squares[:, :, :, :], waves[:, :, :, :], ACT.Square).then_inc(sig["squares"], 1)
                act.wait_ge(*sig("norm2", step, 1))
                nc.scalar.activation(norm2[:, :, :], norm2[:, :, :], ACT.Sqrt).then_inc(sig["root"], 1)

        @block.tensor
        def _(pe):
            with pe.Fori(0, steps) as step:
                norm_transpose(nc, pe, sig, chip, m, step)
                pe.wait_ge(*sig("xT", step, 1))
                pe.wait_ge(*sig("squares", step))
                for t in range(T):
                    ins = nc.tensor.matmul(waves[:, t, :, :], m.xT[:, t * P:(t + 1) * P], cossin[:, :, :],
                                           start=True, stop=True)
                ins.then_inc(sig["waves"], 1)
    sig.ended(steps)


L1_FFN_SIGNALS = dict(NORM_SIGNALS, waves=1, squares=1, norm2=1, root=1, x=1)


EXPERTS = 8
TOKEN_TILES = 4
LOADS = 4


def moe_signals(gated, chunks):
    per = dict(NORM_SIGNALS, logits=1, routed=1, top=1, gap=1, exp_gap=1, h_psum=EXPERTS * chunks,
               hidden=EXPERTS * chunks, o_psum=EXPERTS, mixed=EXPERTS, x=1 if gated else 2, route_chain=10)
    if gated:
        per.update(silu=EXPERTS * chunks)
    else:
        per.update(rwT_psum=1, rwT=1, bias_psum=1, moments2=1, rstd2=1, out_chain=5, act_chain2=1)
    return per


def stage_moe(chip, level):
    nc, T = chip.nc, TOKEN_TILES
    sig, loaded = chip.loop, chip.once
    gated = level == 3
    F = 256 if gated else 512
    chunks, width = F // P, T * P
    banks = 2
    steps = TILES // T
    dram = chip.dram
    sig.use(moe_signals(gated, chunks))
    loaded.use(moe_loads(level))
    with ExitStack() as ctx:
        sb = lambda name, shape, dt=F32: ctx.enter_context(nc.sbuf_tensor(chip.tag + name, shape, dt))
        ps = lambda name, shape: ctx.enter_context(nc.psum_tensor(chip.tag + name, shape, F32))
        m = Norm(chip, ctx, T)
        w_up = sb("w_up", [P, EXPERTS, F])
        w_up2 = sb("w_up2", [P, EXPERTS, F]) if gated else None
        w_down = sb("w_down", [P, EXPERTS, chunks, D])
        w_gate = sb("w_gate", [P, EXPERTS])
        iota = sb("iota", [P, EXPERTS])
        if not gated:
            b_gate, b_up, b_down = sb("b_gate", [P, EXPERTS]), sb("b_up", [P, EXPERTS, chunks]), sb("b_down", [EXPERTS, D])
            gamma, beta = sb("gamma", [P, D]), sb("beta", [P, D])
            rwT = sb("rwT", [EXPERTS, width])
            stats2, moments2, rstd2, logvar2 = sb("stats2", [P, T, 6]), sb("moments2", [P, T, 2]), sb("rstd2", [P, T]), sb("logvar2", [P, T])
        hidden = sb("hidden", [P, 2, chunks, width])
        silu = sb("silu", [P, 2, width]) if gated else None
        logits, top = sb("logits", [P, T, EXPERTS]), sb("top", [P, T, 8])
        index, indexf = sb("index", [P, T, 8], U32), sb("indexf", [P, T, 8])
        gap, weights = sb("gap", [P, T, 1]), sb("weights", [P, T, 2])
        pick, route = sb("pick", [P, T, EXPERTS]), sb("route", [P, T, EXPERTS])
        mix = sb("mix", [P, T, D])
        logits_psum = ps("logits_psum", [P, 512])
        h_psum = [ps(f"h_psum{n}", [P, width]) for n in range(banks)]
        h2_psum = [ps(f"h2_psum{n}", [P, width]) for n in range(banks)] if gated else None
        o_psum = [ps(f"o_psum{n}", [P, T, D]) for n in range(2)]
        lg = logits_psum[:, 0:T * EXPERTS].rearrange("p (t e) -> p t e", t=T)
        x_of = lambda step: chip.x[:, bass.ds(step * T, T), :]
        block = ctx.enter_context(nc.Block())

        @block.sync
        def _(sp):
            names = [("w_gate", w_gate), ("iota", iota)]
            if not gated:
                names += [("b_gate", b_gate), ("b_up", b_up), ("b_down", b_down), ("gamma", gamma), ("beta", beta)]
            for name, tile in names:
                src = dram["iota"] if name == "iota" else dram[f"L{level}_{name}"]
                sp.dma_start(tile[:], src).then_inc(loaded["loaded"], 16)
            for n in range(LOADS):
                e = slice(n * EXPERTS // LOADS, (n + 1) * EXPERTS // LOADS)
                sp.dma_start(w_up[:, e, :], dram[f"L{level}_w_up"][:, e, :]).then_inc(loaded[f"experts{n}"], 16)
                if gated:
                    sp.dma_start(w_up2[:, e, :], dram[f"L{level}_w_up2"][:, e, :]).then_inc(loaded[f"experts{n}"], 16)
                sp.dma_start(w_down[:, e, :, :], dram[f"L{level}_w_down"][:, e, :, :]).then_inc(loaded[f"experts{n}"], 16)

        @block.tensor
        def _(pe):
            pe.wait_ge(*loaded("loaded", 1))
            with pe.Fori(0, steps) as step:
                if not gated:
                    pe.wait_ge(*sig("rwT", step))
                norm_transpose(nc, pe, sig, chip, m, step)
                pe.wait_ge(*sig("xT", step, 1))
                pe.wait_ge(*sig("top", step))
                for t in range(T):
                    ins = nc.tensor.matmul(lg[:, t, :], m.xT[:, t * P:(t + 1) * P], w_gate[:, :], start=True, stop=True)
                ins.then_inc(sig["logits"], 1)

                def down(e):
                    pe.wait_ge(*sig("hidden", step, (e + 1) * chunks))
                    pe.wait_ge(*sig("mixed", step, max(e - 1, 0)))
                    for t in range(T):
                        for c in range(chunks):
                            ins = nc.tensor.matmul(o_psum[e % 2][:, t, :], hidden[:, e % 2, c, t * P:(t + 1) * P],
                                                   w_down[:, e, c, :], start=c == 0, stop=c == chunks - 1)
                    ins.then_inc(sig["o_psum"], 1)

                for e in range(EXPERTS):
                    pe.wait_ge(*loaded(f"experts{e * LOADS // EXPERTS}", 1))
                    for c in range(chunks):
                        n = e * chunks + c
                        pe.wait_ge(*sig("hidden", step, max(n - banks + 1, 0)))
                        ins = nc.tensor.matmul(h_psum[n % banks][:, :], w_up[:, e, c * P:(c + 1) * P], m.xT[:, :],
                                               start=True, stop=True)
                        if gated:
                            ins = nc.tensor.matmul(h2_psum[n % banks][:, :], w_up2[:, e, c * P:(c + 1) * P], m.xT[:, :],
                                                   start=True, stop=True)
                        ins.then_inc(sig["h_psum"], 1)
                    if e:
                        down(e - 1)
                down(EXPERTS - 1)
                if not gated:
                    pe.wait_ge(*sig("routed", step, 1))
                    for t in range(T):
                        ins = nc.tensor.transpose(m.psum[0:EXPERTS, t * P:(t + 1) * P], route[:, t, :], chip.ident[:, :])
                    ins.then_inc(sig["rwT_psum"], 1)
                    pe.wait_ge(*sig("rwT", step, 1))
                    pe.wait_ge(*sig("mixed", step, EXPERTS - 1))
                    for t in range(T):
                        ins = nc.tensor.matmul(o_psum[0][:, t, :], rwT[:, t * P:(t + 1) * P], b_down[:, :], start=True, stop=True)
                    ins.then_inc(sig["bias_psum"], 1)

        @block.scalar
        def _(act):
            act.wait_ge(*loaded("loaded", 1))
            with act.Fori(0, steps) as step:
                norm_rstd(nc, act, sig, chip, m, step)
                norm_xT(nc, act, sig, m, step, ["h_psum", "logits"])
                act.wait_ge(*sig("gap", step, 1))
                nc.scalar.activation(weights[:, :, 1:2], gap[:, :, :], ACT.Exp).then_inc(sig["exp_gap"], 1)
                for e in range(EXPERTS):
                    if not gated:
                        act.wait_ge(*sig("o_psum", step, max(e - 1, 0)))
                    for c in range(chunks):
                        n = e * chunks + c
                        act.wait_ge(*sig("h_psum", step, n + 1))
                        if gated:
                            act.wait_ge(*sig("hidden", step, max(n - 1, 0)))
                            nc.scalar.activation(silu[:, n % 2, :], h_psum[n % banks][:, :], ACT.Silu)\
                              .then_inc(sig["silu"], 1)
                        else:
                            nc.scalar.activation(hidden[:, e % 2, c, :], h_psum[n % banks][:, :], ACT.Relu,
                                                 bias=b_up[:, e, c:c + 1]).then_inc(sig["hidden"], 1)
                if not gated:
                    act.wait_ge(*sig("rwT_psum", step, 1))
                    act.wait_ge(*sig("bias_psum", step))
                    nc.scalar.activation(rwT[:, :], m.psum[0:EXPERTS, :], ACT.Copy).then_inc(sig["rwT"], 1)
                    act.wait_ge(*sig("moments2", step, 1))
                    nc.scalar.activation(logvar2[:, :], moments2[:, :, 1], ACT.Ln, bias=chip.eps[:, 0:1]).then_inc(sig["act_chain2"], 1)
                    act.wait_ge(*sig("act_chain2", step, 1))
                    nc.scalar.activation(rstd2[:, :], logvar2[:, :], ACT.Exp, scale=-0.5).then_inc(sig["rstd2"], 1)

        @block.vector
        def _(dve):
            dve.wait_ge(*loaded("loaded", 1))
            with dve.Fori(0, steps) as step:
                norm_vector(nc, dve, sig, m, step, x_tile(chip, step, T), lambda t: m.xn[:, t, :], ["xT_psum"])
                chain = Chain(dve, sig, "route_chain", step)
                dve.wait_ge(*sig("logits", step, 1))
                if gated:
                    ins = nc.vector.tensor_copy(logits[:, :, :], lg)
                else:
                    ins = nc.vector.tensor_tensor(logits[:, :, :], lg, b_gate[:, :].rearrange("p (a e) -> p a e", a=1).to_broadcast([P, T, EXPERTS]), ALU.add)
                ins.then_inc(sig["top"], 1)
                sig.apart(dve, "top", step, 1)
                for t in range(T):
                    ins = nc.vector.max(top[:, t, :], logits[:, t, :])
                chain.apart(ins)
                for t in range(T):
                    ins = nc.vector.max_index(index[:, t, :], top[:, t, :], logits[:, t, :])
                chain(ins)
                nc.vector.tensor_tensor(gap[:, :, :], top[:, :, 1:2], top[:, :, 0:1], ALU.subtract).then_inc(sig["gap"], 1)
                chain(nc.vector.tensor_copy(indexf[:, :, :], index[:, :, :]))
                dve.wait_ge(*sig("exp_gap", step, 1))
                chain(nc.vector.tensor_scalar(weights[:, :, 0:1], weights[:, :, 1:2], 1.0, None, ALU.add))
                chain(nc.vector.reciprocal(weights[:, :, 0:1], weights[:, :, 0:1]))
                chain(nc.vector.tensor_tensor(weights[:, :, 1:2], weights[:, :, 1:2], weights[:, :, 0:1], ALU.mult))
                every = [P, T, EXPERTS]
                ids = iota[:, :].rearrange("p (a e) -> p a e", a=1).to_broadcast(every)
                chain(nc.vector.tensor_tensor(route[:, :, :], ids, indexf[:, :, 0:1].to_broadcast(every), ALU.is_equal))
                chain(nc.vector.tensor_tensor(pick[:, :, :], ids, indexf[:, :, 1:2].to_broadcast(every), ALU.is_equal))
                chain(nc.vector.tensor_tensor(route[:, :, :], route[:, :, :], weights[:, :, 0:1].to_broadcast(every), ALU.mult))
                chain(nc.vector.tensor_tensor(pick[:, :, :], pick[:, :, :], weights[:, :, 1:2].to_broadcast(every), ALU.mult))
                nc.vector.tensor_tensor(route[:, :, :], route[:, :, :], pick[:, :, :], ALU.add).then_inc(sig["routed"], 1)
                dve.wait_ge(*sig("routed", step, 1))

                def mix_in(e):
                    dve.wait_ge(*sig("o_psum", step, e + 1))
                    if e:
                        dve.wait_ge(*sig("mixed", step, e))
                    for t in range(T):
                        if e == 0:
                            ins = nc.vector.tensor_scalar(mix[:, t, :], o_psum[0][:, t, :], route[:, t, e:e + 1], None, ALU.mult)
                        else:
                            ins = nc.vector.scalar_tensor_tensor(mix[:, t, :], o_psum[e % 2][:, t, :], route[:, t, e:e + 1],
                                                                 mix[:, t, :], ALU.mult, ALU.add)
                    ins.then_inc(sig["mixed"], 1)

                for e in range(EXPERTS):
                    if gated:
                        dve.wait_ge(*sig("o_psum", step, max(e - 1, 0)))
                        for c in range(chunks):
                            n = e * chunks + c
                            dve.wait_ge(*sig("silu", step, n + 1))
                            nc.vector.tensor_tensor(hidden[:, e % 2, c, :], silu[:, n % 2, :], h2_psum[n % banks][:, :],
                                                    ALU.mult).then_inc(sig["hidden"], 1)
                        if e:
                            mix_in(e - 1)
                    else:
                        mix_in(e)
                if gated:
                    mix_in(EXPERTS - 1)
                    dve.wait_ge(*sig("mixed", step, EXPERTS))
                    nc.vector.scalar_tensor_tensor(x_of(step), mix[:, :, :], 0.5, x_of(step), ALU.mult, ALU.add).then_inc(sig["x"], 1)
                else:
                    out = Chain(dve, sig, "out_chain", step)
                    row = [P, T, D]
                    dve.wait_ge(*sig("mixed", step, EXPERTS))
                    dve.wait_ge(*sig("bias_psum", step, 1))
                    out(nc.vector.tensor_tensor(mix[:, :, :], mix[:, :, :], o_psum[0][:, :, :], ALU.add))
                    out(nc.vector.tensor_tensor(mix[:, :, :], mix[:, :, :], m.xn[:, :, :], ALU.add))
                    for t in range(T):
                        ins = nc.vector.bn_stats(stats2[:, t, :], mix[:, t, :])
                    out.apart(ins)
                    for t in range(T):
                        ins = nc.vector.bn_aggr(moments2[:, t, :], stats2[:, t, :])
                    ins.then_inc(sig["moments2"], 1)
                    dve.wait_ge(*sig("rstd2", step, 1))
                    for t in range(T):
                        ins = nc.vector.tensor_scalar(mix[:, t, :], mix[:, t, :], moments2[:, t, 0:1], rstd2[:, t:t + 1],
                                                      ALU.subtract, ALU.mult)
                    out(ins)
                    out(nc.vector.tensor_tensor(mix[:, :, :], mix[:, :, :], gamma[:, :].rearrange("p (a d) -> p a d", a=1).to_broadcast(row), ALU.mult))
                    nc.vector.tensor_tensor(mix[:, :, :], mix[:, :, :], beta[:, :].rearrange("p (a d) -> p a d", a=1).to_broadcast(row), ALU.add)\
                      .then_inc(sig["x"], 1)
                    dve.wait_ge(*sig("x", step, 1))
                    nc.vector.scalar_tensor_tensor(x_of(step), mix[:, :, :], 0.5, x_of(step), ALU.mult, ALU.add).then_inc(sig["x"], 1)
                    out.done()
                dve.wait_ge(*sig("x", step, 1 if gated else 2))
                chain.done()
    sig.ended(steps)
    loaded.ended(1)


def moe_loads(level):
    small = 2 if level == 3 else 7
    return dict(loaded=16 * small, **{f"experts{n}": 16 * (3 if level == 3 else 2) for n in range(LOADS)})


GROUPS, BAND = 4, 32
AUG = DK + 1
PAIRS = HEADS // 2
ATTN_LOADS = {0: 11, 2: 13, 3: 11}


def attention_signals(level):
    per = dict(NORM_SIGNALS, proj=GROUPS, proj_read=GROUPS, v_psum=1, v=1, probs=PAIRS,
               ctx_psum=1, context=1, ctxT_psum=1, ctxT=1, out_psum=1, x=2, ctx_chain=1)
    if level == 3:
        per.update(rope=GROUPS, rope_chain=2 * GROUPS, den_scores=PAIRS, den_probs=PAIRS, scores=PAIRS)
    else:
        per.update(scores=PAIRS, max_scores=PAIRS, negmax=PAIRS, negmaxT=2, q_aug=2)
    if level == 2:
        per.update(norm_chain_a=1, moments_a=1, act_norm_a=1, rstd_a=1, xn_a=1, residual=1)
    return per


def stage_attention(chip, level):
    nc, sig, once = chip.nc, chip.loop, chip.once
    causal, softmax = level != 2, level != 3
    scale = float(DK) ** -0.5
    dram = chip.dram
    T = HALVES
    sig.use(attention_signals(level))
    once.use(dict(loaded=16 * ATTN_LOADS[level], set=2 if softmax else 1))
    with ExitStack() as ctx:
        sb = lambda name, shape, dt=F32: ctx.enter_context(nc.sbuf_tensor(chip.tag + name, shape, dt))
        ps = lambda name, shape: ctx.enter_context(nc.psum_tensor(chip.tag + name, shape, F32))
        m = Norm(chip, ctx, T)
        tiles = {"wq": sb("wq", [P, GROUPS, P]), "wk": sb("wk", [P, GROUPS, P]), "wv": sb("wv", [P, D]), "wo": sb("wo", [P, D]),
                 "bo": sb("bo", [P, D]), "ident_bf": sb("ident_bf", [P, P], BF16), "mask": sb("mask", [P, P], BF16),
                 "maskT": sb("maskT", [P, P], BF16)}
        if softmax:
            tiles.update(bq=sb("bq", [P, GROUPS]), bk=sb("bk", [P, GROUPS]), bv=sb("bv", [P, D]))
        else:
            tiles.update(wq_swap=sb("wq_swap", [P, GROUPS, P]), wk_swap=sb("wk_swap", [P, GROUPS, P]),
                         rope=sb("rope", [P, 2, SEQ]))
        if level == 2:
            tiles.update(gamma=sb("gamma", [P, 1]), beta=sb("beta", [P, 1]))
            x1 = sb("x1", [P, T, D])
        assert len(tiles) == ATTN_LOADS[level]
        wq, wk, wv, wo, bo, ident_bf, mask, maskT = (tiles[n] for n in ("wq", "wk", "wv", "wo", "bo", "ident_bf", "mask", "maskT"))
        qk = sb("qk", [P, 2, GROUPS, SEQ])
        turned = None if softmax else sb("turned", [P, 2, GROUPS, SEQ])
        turn = None if softmax else sb("turn", [P, 2, 2, SEQ])
        v = sb("v", [P, T, HEADS, AUG])
        negmax = sb("negmax", [P, T, GROUPS, P]) if softmax else None
        probs = sb("probs", [P, T, HEADS, SEQ])
        den_probs = None if softmax else sb("den_probs", [P, T, HEADS, SEQ])
        rden, context, ctxT = sb("rden", [P, T, HEADS, 1]), sb("context", [P, T, D]), sb("ctxT", [P, SEQ])
        scores = ps("scores", [P, GROUPS, T, SEQ])
        pv = ps("pv", [P, T, HEADS, AUG])
        vo = ps("vo", [P, T, D])
        banks = lambda n: slice(2 * (n % 2), 2 * (n % 2) + 2)
        of_pair = lambda tile, n: tile[:, :, 2 * n:2 * n + 2, :].rearrange("p t h s -> p h t s")
        block = ctx.enter_context(nc.Block())

        @block.sync
        def _(sp):
            for name, tile in tiles.items():
                src = dram[name] if name in ("ident_bf", "mask", "maskT") else dram[f"A{level}_{name}"]
                sp.dma_start(tile[:], src).then_inc(once["loaded"], 16)

        @block.tensor
        def _(pe):
            pe.wait_ge(*once("loaded", 1))
            pe.wait_ge(*once("set", 1))
            with pe.Fori(0, B) as step:
                pe.wait_ge(*sig("ctxT", step))
                norm_transpose(nc, pe, sig, chip, m, step)
                pe.wait_ge(*sig("xT", step, 1))
                pe.wait_ge(*sig("x", step))
                for t in range(T):
                    ins = nc.tensor.matmul(vo[:, t, :], m.xT[:, t * P:(t + 1) * P], wv[:, :], start=True, stop=True)
                ins.then_inc(sig["v_psum"], 1)
                pe.wait_ge(*sig("probs", step))
                for g in range(GROUPS):
                    pe.wait_ge(*sig("proj_read", step, max(g - 1, 0)))
                    if not softmax:
                        pe.wait_ge(*sig("rope", step, max(g - 1, 0)))
                    projections = [wq, wk] if softmax else [wq, wk, tiles["wq_swap"], tiles["wk_swap"]]
                    for n, w in enumerate(projections):
                        ins = nc.tensor.matmul(scores[:, 2 * (g % 2) + n // 2, n % 2, :], w[:, g, :], m.xT[:, :],
                                               start=True, stop=True)
                    ins.then_inc(sig["proj"], 1)

                def score(n, stationary, moving, rows_of, mask_of):
                    g = n // 2
                    for j in (2 * (n % 2), 2 * (n % 2) + 1):
                        rows = slice(BAND * j, BAND * j + rows_of)
                        for t in range(T):
                            first, end = span(t, mask_of)
                            ins = nc.tensor.matmul(scores[:, j, t, first:end], stationary[rows, g, t * P:(t + 1) * P],
                                                   moving[rows, g, first:end], start=True, stop=mask_of is None,
                                                   skip_group_check=True)
                            if mask_of is not None:
                                ins = nc.tensor.matmul(scores[:, j, t, t * P:(t + 1) * P], ident_bf[:, :], mask_of[:, :],
                                                       start=False, stop=True, skip_group_check=True)
                    return ins

                def span(t, mask_of):
                    if mask_of is None:
                        return 0, SEQ
                    return (0, (t + 1) * P) if mask_of is mask else (t * P, SEQ)

                q_rows, k_rows = qk[:, 0], qk[:, 1]
                pe.wait_ge(*sig("proj_read", step, GROUPS))
                if softmax:
                    for n in range(PAIRS):
                        pe.wait_ge(*sig("negmax", step, max(n - 1, 0)))
                        score(n, q_rows, k_rows, DK, mask if causal else None).then_inc(sig["max_scores"], 1)
                    pe.wait_ge(*sig("negmax", step, PAIRS))
                    for half in range(2):
                        pe.wait_ge(*sig("q_aug", step, half))
                        for g in (2 * half, 2 * half + 1):
                            for t in range(T):
                                at = (g % 2) * SEQ + t * P
                                ins = nc.tensor.transpose(m.psum[:, at:at + P], negmax[:, t, g, :], chip.ident[:, :])
                        ins.then_inc(sig["negmaxT"], 1)
                    pe.wait_ge(*sig("q_aug", step, 2))
                else:
                    pe.wait_ge(*sig("rope", step, GROUPS))
                    for n in range(PAIRS):
                        pe.wait_ge(*sig("den_probs", step, max(n - 1, 0)))
                        score(n, k_rows, q_rows, DK, None).then_inc(sig["den_scores"], 1)
                    pe.wait_ge(*sig("den_probs", step, PAIRS))

                def weigh(g):
                    pe.wait_ge(*sig("probs", step, 2 * g + 2))
                    for h in range(4 * g, 4 * g + 4):
                        for qt in range(T):
                            for kt in range(qt + 1 if causal else T):
                                last = kt == (qt if causal else T - 1)
                                ins = nc.tensor.matmul(pv[:, qt, h, 0:AUG if softmax else DK], probs[:, kt, h, qt * P:(qt + 1) * P],
                                                       v[:, kt, h, 0:AUG if softmax else DK], start=kt == 0, stop=last)
                            if not softmax:
                                for kt in range(T):
                                    ins = nc.tensor.matmul(pv[:, qt, h, DK:AUG], den_probs[:, kt, h, qt * P:(qt + 1) * P],
                                                           v[:, kt, h, DK:AUG], start=kt == 0, stop=kt == T - 1)
                    return ins

                pe.wait_ge(*sig("v", step, 1))
                pe.wait_ge(*sig("context", step))
                source, rows_of = (qk, AUG) if softmax else (turned, DK)
                for n in range(PAIRS):
                    pe.wait_ge(*sig("probs", step, max(n - 1, 0)))
                    score(n, source[:, 1], source[:, 0], rows_of, maskT if causal else None).then_inc(sig["scores"], 1)
                    if n % 2 == 1 and n > 1:
                        weigh(n // 2 - 1)
                weigh(GROUPS - 1).then_inc(sig["ctx_psum"], 1)

                pe.wait_ge(*sig("context", step, 1))
                for t in range(T):
                    ins = nc.tensor.transpose(m.psum[:, t * P:(t + 1) * P], context[:, t, :], chip.ident[:, :])
                ins.then_inc(sig["ctxT_psum"], 1)
                pe.wait_ge(*sig("ctxT", step, 1))
                for t in range(T):
                    ins = nc.tensor.matmul(vo[:, t, :], ctxT[:, t * P:(t + 1) * P], wo[:, :], start=True, stop=True)
                ins.then_inc(sig["out_psum"], 1)

        @block.scalar
        def _(act):
            act.wait_ge(*once("loaded", 1))
            with act.Fori(0, B) as step:
                if level == 2:
                    norm_rstd(nc, act, sig, chip, m, step, "_a")
                norm_rstd(nc, act, sig, chip, m, step)
                act.wait_ge(*sig("xT_psum", step, 1))
                act.wait_ge(*sig("proj", step))
                if level == 2:
                    ins = nc.scalar.activation(m.xT[:, :], m.psum[:, 0:SEQ], ACT.Identity, bias=tiles["beta"][:, 0:1],
                                               scale=tiles["gamma"][:, 0:1])
                else:
                    ins = nc.scalar.activation(m.xT[:, :], m.psum[:, 0:SEQ], ACT.Copy)
                ins.then_inc(sig["xT"], 1)
                act.wait_ge(*sig("scores", step))
                for g in range(GROUPS):
                    act.wait_ge(*sig("proj", step, g + 1))
                    for n in range(2):
                        if softmax:
                            ins = nc.scalar.activation(qk[:, n, g, :], scores[:, 2 * (g % 2), n, :], ACT.Identity,
                                                       bias=tiles["bq" if n == 0 else "bk"][:, g:g + 1])
                        else:
                            ins = nc.scalar.activation(qk[:, n, g, :], scores[:, 2 * (g % 2), n, :], ACT.Copy)
                    ins.then_inc(sig["proj_read"], 1)
                act.wait_ge(*sig("ctx_psum", step))
                if not softmax:
                    for n in range(PAIRS):
                        act.wait_ge(*sig("den_scores", step, n + 1))
                        nc.scalar.activation(of_pair(den_probs, n), scores[:, banks(n), :, :], ACT.Exp, scale=scale)\
                          .then_inc(sig["den_probs"], 1)
                for n in range(PAIRS):
                    act.wait_ge(*sig("scores", step, n + 1))
                    for t in range(T) if causal else [slice(0, T)]:
                        first = t * P if causal else 0
                        ins = nc.scalar.activation(of_pair(probs, n)[:, :, t, first:SEQ], scores[:, banks(n), t, first:SEQ],
                                                   ACT.Exp, scale=scale)
                    ins.then_inc(sig["probs"], 1)
                act.wait_ge(*sig("ctxT_psum", step, 1))
                act.wait_ge(*sig("out_psum", step))
                nc.scalar.activation(ctxT[:, :], m.psum[:, 0:SEQ], ACT.Copy).then_inc(sig["ctxT"], 1)

        @block.vector
        def _(dve):
            nc.vector.memset(v[:, :, :, :], 1.0).then_inc(once["set"], 1)
            if softmax:
                nc.vector.memset(negmax[:, :, :, :], 0.0).then_inc(once["set"], 1)
            dve.wait_ge(*once("set", 1))
            dve.wait_ge(*once("loaded", 1))
            with dve.Fori(0, B) as step:
                tile = x_tile(chip, step, T)
                if level == 2:
                    norm_vector(nc, dve, sig, m, step, tile, lambda t: x1[:, t, :], ["x"], "_a")
                    dve.wait_ge(*sig("xn_a", step, 1))
                    tile = lambda t: x1[:, t, :]
                norm_vector(nc, dve, sig, m, step, tile, lambda t: m.xn[:, t, :], ["xT_psum"])
                dve.wait_ge(*sig("v_psum", step, 1))
                dve.wait_ge(*sig("ctx_psum", step))
                vh = vo[:, :, :].rearrange("p t (h c) -> p t h c", c=DK)
                for t in range(T):
                    if softmax:
                        ins = nc.vector.tensor_tensor(v[:, t, :, 0:DK], vh[:, t], tiles["bv"][:, :].rearrange("p (h c) -> p h c", c=DK), ALU.add)
                    else:
                        ins = nc.vector.tensor_copy(v[:, t, :, 0:DK], vh[:, t])
                ins.then_inc(sig["v"], 1)
                if softmax:
                    dve.wait_ge(*sig("negmaxT", step))
                    for n in range(PAIRS):
                        dve.wait_ge(*sig("max_scores", step, n + 1))
                        places = negmax[:, :, n // 2, :].rearrange("p t (j r) -> p j t r", r=BAND)[:, banks(n), :, DK]
                        for t in range(T) if causal else [slice(0, T)]:
                            keys = (t + 1) * P if causal else SEQ
                            ins = nc.vector.tensor_reduce(places[:, :, t], scores[:, banks(n), t, 0:keys], AX.X, ALU.max,
                                                          negate=True)
                        ins.then_inc(sig["negmax"], 1)
                    for half in range(2):
                        dve.wait_ge(*sig("negmaxT", step, half + 1))
                        q2 = qk[:, 0, 2 * half:2 * half + 2, :]
                        nc.vector.tensor_tensor(q2, m.psum[:, :].rearrange("p (g s) -> p g s", g=2), q2, ALU.add)\
                          .then_inc(sig["q_aug"], 1)
                else:
                    chain = Chain(dve, sig, "rope_chain", step)
                    rope = tiles["rope"]
                    cos, sin = (rope[:, n:n + 1, :].to_broadcast([P, 2, SEQ]) for n in range(2))
                    dve.wait_ge(*sig("scores", step))
                    for g in range(GROUPS):
                        dve.wait_ge(*sig("proj", step, g + 1))
                        dve.wait_ge(*sig("proj_read", step, g + 1))
                        dve.wait_ge(*sig("rope", step, g))
                        chain(nc.vector.tensor_tensor(turn[:, 0, :, :], scores[:, 2 * (g % 2), :, :], cos, ALU.mult))
                        chain(nc.vector.tensor_tensor(turn[:, 1, :, :], scores[:, 2 * (g % 2) + 1, :, :], sin, ALU.mult))
                        nc.vector.tensor_tensor(turned[:, :, g, :], turn[:, 0, :, :], turn[:, 1, :, :], ALU.add)\
                          .then_inc(sig["rope"], 1)
                    chain.done()
                dve.wait_ge(*sig("ctx_psum", step, 1))
                nc.vector.reciprocal(rden[:, :, :, :], pv[:, :, :, DK:AUG]).then_inc(sig["ctx_chain"], 1)
                dve.wait_ge(*sig("ctx_chain", step, 1))
                dve.wait_ge(*sig("ctxT_psum", step))
                ch = context[:, :, :].rearrange("p t (h c) -> p t h c", c=DK)
                for t in range(T):
                    ins = nc.vector.tensor_tensor(ch[:, t], pv[:, t, :, 0:DK], rden[:, t].to_broadcast([P, HEADS, DK]), ALU.mult)
                ins.then_inc(sig["context"], 1)
                dve.wait_ge(*sig("out_psum", step, 1))
                xs = chip.x[:, bass.ds(step * T, T), :]
                nc.vector.tensor_tensor(xs, vo[:, :, :], xs, ALU.add).then_inc(sig["x"], 1)
                dve.wait_ge(*sig("x", step, 1))
                if level == 2:
                    nc.vector.tensor_tensor(xs, xs, x1[:, :, :], ALU.add).then_inc(sig["residual"], 1)
                    dve.wait_ge(*sig("residual", step, 1))
                nc.vector.tensor_tensor(xs, xs, bo[:, :].rearrange("p (a d) -> p a d", a=1).to_broadcast([P, T, D]), ALU.add)\
                  .then_inc(sig["x"], 1)
                dve.wait_ge(*sig("x", step, 2))
    sig.ended(B)
    once.ended(1)


RW_HEADS, HS = 2, 64
LORA_R, TD_R = 32, 64
MIXES = 5
PAIR = 2
ROUNDS = HS // PAIR
RW_SIGNALS = dict(NORM_SIGNALS, mix_chain=3 + MIXES, lora_psum=1, lora=1, miu_psum=1, mixed=1, td_psum=1, kvrg_psum=1,
                  td_tanh=1, w_psum=1, act_chain=1, decay=1, kvr=1, g_exp=1, ruk=1, bonus_psum=1, gate=1, gate_chain=2,
                  bonus=1, vb=ROUNDS, kv=ROUNDS, scan=ROUNDS, prod=ROUNDS, y_acc=ROUNDS, yT=1, y_tok=1, yn_stats=1,
                  yn_moments=1, act_yn=1, yn_rstd=1, yn=1, ynT_psum=1, ynT=1, gated=1, out_psum=1, x=1)
RW_LOADS = 16


def stage_rwkv(chip):
    nc, dram, sig, once = chip.nc, chip.dram, chip.loop, chip.once
    sig.use(RW_SIGNALS)
    once.use(dict(loaded=16 * (RW_LOADS + 1), set=4))
    T = HALVES
    with ExitStack() as ctx:
        sb = lambda name, shape, dt=F32: ctx.enter_context(nc.sbuf_tensor(chip.tag + name, shape, dt))
        ps = lambda name, shape: ctx.enter_context(nc.psum_tensor(chip.tag + name, shape, F32))
        m = Norm(chip, ctx, T)
        tiles = {"miu_x": sb("miu_x", [P, 1]), "lambda": sb("lambda", [P, MIXES]), "A": sb("A", [P, MIXES * LORA_R]),
                 "B": sb("B", [LORA_R, MIXES, D]), "td_miu": sb("td_miu", [P, 1]), "td_A": sb("td_A", [P, TD_R]),
                 "td_B": sb("td_B", [TD_R, D]), "u": sb("u", [P, 1]), "wr": sb("wr", [P, D]), "wk": sb("wk", [P, D]),
                 "wv": sb("wv", [P, D]), "wg": sb("wg", [P, D]), "wo": sb("wo", [P, D]), "gamma": sb("gamma", [P, 1]),
                 "beta": sb("beta", [P, 1]), "head_ones": sb("head_ones", [P, P])}
        assert len(tiles) == RW_LOADS
        spread = sb("spread", [P, HS, P])
        gather = sb("gather", [P, P + HS - 1])
        delta, xm, lora = sb("delta", [P, SEQ]), sb("xm", [P, SEQ]), sb("lora", [LORA_R, MIXES, SEQ])
        mix, td = sb("mix", [P, MIXES, SEQ]), sb("td", [TD_R, SEQ])
        expw, decay = sb("expw", [P, SEQ]), sb("decay", [P, PAIR, SEQ])
        kT, vT, rT, r_next = sb("kT", [P, SEQ]), sb("vT", [P, SEQ]), sb("rT", [P, SEQ]), sb("r_next", [P, SEQ])
        ruk, bonus, gate, expg = sb("ruk", [P, SEQ]), sb("bonus", [P, SEQ]), sb("gate", [P, SEQ]), sb("expg", [P, SEQ])
        kv, state, prod = sb("kv", [P, 2, PAIR, SEQ]), sb("state", [P, 2, PAIR, SEQ]), sb("prod", [P, 2, PAIR, SEQ])
        yT, yn, ynT, gated = sb("yT", [P, SEQ]), sb("yn", [P, T, D]), sb("ynT", [P, SEQ]), sb("gated", [P, SEQ])
        y_stats, y_moments = sb("y_stats", [P, T * RW_HEADS, 6]), sb("y_moments", [P, T * RW_HEADS, 2])
        y_logvar, y_rstd, eps2 = sb("y_logvar", [P, T * RW_HEADS]), sb("y_rstd", [P, T * RW_HEADS]), sb("eps2", [P, 1])
        work = ps("work", [P, 4, 2, SEQ])
        vb = [ps(f"vb{n}", [P, PAIR, SEQ]) for n in range(2)]
        y_psum = ps("y", [P, 512])
        block = ctx.enter_context(nc.Block())
        lora_psum = work[0:LORA_R, 0:3, :, :].rearrange("p b a s -> p (b a) s")[:, 0:MIXES, :]
        miu_psum = work[:, 0:3, :, :].rearrange("p b a s -> p (b a) s")[:, 0:MIXES, :]
        one = lambda v: v.rearrange("p (a s) -> p a s", a=1)

        @block.sync
        def _(sp):
            for name, tile in tiles.items():
                sp.dma_start(tile[:], dram["RW_" + name]).then_inc(once["loaded"], 16)
            sp.dma_start(gather[:, :], dram["RW_gather"]).then_inc(once["loaded"], 16)

        @block.tensor
        def _(pe):
            pe.wait_ge(*once("loaded", 1))
            pe.wait_ge(*once("set", 1))
            with pe.Fori(0, B) as step:
                norm_transpose(nc, pe, sig, chip, m, step)
                pe.wait_ge(*sig("mixed", step))
                pe.wait_ge(*sig("x", step))
                pe.wait_ge(*sig("ynT", step))
                pe.wait_ge(*sig("mix_chain", step, 3))
                for f in range(MIXES):
                    ins = nc.tensor.matmul(lora_psum[:, f, :], tiles["A"][:, f * LORA_R:(f + 1) * LORA_R], xm[:, :],
                                           start=True, stop=True)
                ins.then_inc(sig["lora_psum"], 1)
                pe.wait_ge(*sig("lora", step, 1))
                for f in range(MIXES):
                    ins = nc.tensor.matmul(miu_psum[:, f, :], tiles["B"][:, f, :], lora[:, f, :], start=True, stop=True)
                ins.then_inc(sig["miu_psum"], 1)
                pe.wait_ge(*sig("mixed", step, 1))
                nc.tensor.matmul(work[0:TD_R, 0, 0, :], tiles["td_A"][:, :], mix[:, 0, :], start=True, stop=True)\
                  .then_inc(sig["td_psum"], 1)
                for n, name in enumerate(("wk", "wv", "wr", "wg")):
                    ins = nc.tensor.matmul(work[:, 1 + n // 2, n % 2, :], tiles[name][:, :], mix[:, 1 + n, :], start=True, stop=True)
                ins.then_inc(sig["kvrg_psum"], 1)
                pe.wait_ge(*sig("td_tanh", step, 1))
                pe.wait_ge(*sig("bonus", step))
                nc.tensor.matmul(work[:, 3, 0, :], tiles["td_B"][:, :], td[:, :], start=True, stop=True).then_inc(sig["w_psum"], 1)
                pe.wait_ge(*sig("ruk", step, 1))
                pe.wait_ge(*sig("act_chain", step, 1))
                nc.tensor.matmul(work[:, 3, 1, :], tiles["head_ones"][:, :], ruk[:, :], start=True, stop=True)\
                  .then_inc(sig["bonus_psum"], 1)

                def spread_v(n):
                    pe.wait_ge(*sig("kv", step, max(n - 1, 0)))
                    for a in range(PAIR):
                        ins = nc.tensor.matmul(vb[n % 2][:, a, :], spread[:, PAIR * n + a, :], vT[:, :], start=True, stop=True)
                    ins.then_inc(sig["vb"], 1)

                spread_v(0)
                spread_v(1)
                pe.wait_ge(*sig("yT", step))
                for n in range(ROUNDS):
                    pe.wait_ge(*sig("prod", step, n + 1))
                    for a in range(PAIR):
                        at = HS - 1 - (PAIR * n + a)
                        ins = nc.tensor.matmul(y_psum[:, 0:SEQ], gather[:, at:at + P], prod[:, n % 2, a, :],
                                               start=n == 0 and a == 0, stop=n == ROUNDS - 1 and a == PAIR - 1)
                    ins.then_inc(sig["y_acc"], 1)
                    if n + 2 < ROUNDS:
                        spread_v(n + 2)
                pe.wait_ge(*sig("yT", step, 1))
                for t in range(T):
                    ins = nc.tensor.transpose(work[:, 0, t, 0:P], yT[:, t * P:(t + 1) * P], chip.ident[:, :])
                ins.then_inc(sig["y_tok"], 1)
                pe.wait_ge(*sig("yn", step, 1))
                pe.wait_ge(*sig("kvr", step, 1))
                for t in range(T):
                    ins = nc.tensor.transpose(work[:, 1, 0, t * P:(t + 1) * P], yn[:, t, :], chip.ident[:, :])
                ins.then_inc(sig["ynT_psum"], 1)
                pe.wait_ge(*sig("gated", step, 1))
                for t in range(T):
                    ins = nc.tensor.matmul(work[:, 0, t, 0:D], gated[:, t * P:(t + 1) * P], tiles["wo"][:, :], start=True, stop=True)
                ins.then_inc(sig["out_psum"], 1)

        @block.scalar
        def _(act):
            act.wait_ge(*once("loaded", 1))
            act.wait_ge(*once("set", 1))
            with act.Fori(0, B) as step:
                norm_rstd(nc, act, sig, chip, m, step)
                norm_xT(nc, act, sig, m, step, ["mixed"])
                act.wait_ge(*sig("lora_psum", step, 1))
                nc.scalar.activation(lora[:, :, :], lora_psum, ACT.Tanh).then_inc(sig["lora"], 1)
                act.wait_ge(*sig("td_psum", step, 1))
                nc.scalar.activation(td[:, :], work[0:TD_R, 0, 0, :], ACT.Tanh).then_inc(sig["td_tanh"], 1)
                act.wait_ge(*sig("kvrg_psum", step, 1))
                act.wait_ge(*sig("y_acc", step))
                nc.scalar.activation(kT[:, :], work[:, 1, 0, :], ACT.Copy)
                nc.scalar.activation(vT[:, :], work[:, 1, 1, :], ACT.Copy)
                nc.scalar.activation(r_next[:, 0:SEQ - 1], work[:, 2, 0, 1:SEQ], ACT.Copy)
                nc.scalar.activation(rT[:, :], work[:, 2, 0, :], ACT.Copy).then_inc(sig["kvr"], 1)
                act.wait_ge(*sig("gate", step))
                nc.scalar.activation(expg[:, :], work[:, 2, 1, :], ACT.Exp, scale=-1.0).then_inc(sig["g_exp"], 1)
                act.wait_ge(*sig("w_psum", step, 1))
                nc.scalar.activation(expw[:, :], work[:, 3, 0, :], ACT.Exp, bias=tiles["td_miu"][:, 0:1]).then_inc(sig["act_chain"], 1)
                act.wait_ge(*sig("act_chain", step, 1))
                for a in range(PAIR):
                    ins = nc.scalar.activation(decay[:, a, 1:SEQ], expw[:, 1:SEQ], ACT.Exp, scale=-1.0)
                ins.then_inc(sig["decay"], 1)
                act.wait_ge(*sig("yn_moments", step, 1))
                nc.scalar.activation(y_logvar[:, :], y_moments[:, :, 1], ACT.Ln, bias=eps2[:, 0:1]).then_inc(sig["act_yn"], 1)
                act.wait_ge(*sig("act_yn", step, 1))
                nc.scalar.activation(y_rstd[:, :], y_logvar[:, :], ACT.Exp, scale=-0.5).then_inc(sig["yn_rstd"], 1)
                act.wait_ge(*sig("ynT_psum", step, 1))
                act.wait_ge(*sig("gated", step))
                nc.scalar.activation(ynT[:, :], work[:, 1, 0, :], ACT.Identity, bias=tiles["beta"][:, 0:1],
                                     scale=tiles["gamma"][:, 0:1]).then_inc(sig["ynT"], 1)

        @block.gpsimd
        def _(pool):
            with pool.Fori(0, B) as step:
                pool.wait_ge(*sig("kvr", step, 1))
                for n in range(ROUNDS):
                    pool.wait_ge(*sig("scan", step, n + 1))
                    pool.wait_ge(*sig("y_acc", step, max(n - 1, 0)))
                    nc.gpsimd.tensor_tensor(prod[:, n % 2, :, :], state[:, n % 2, :, :],
                                            one(r_next[:, :]).to_broadcast([P, PAIR, SEQ]), ALU.mult).then_inc(sig["prod"], 1)

        @block.vector
        def _(dve):
            dve.wait_ge(*once("loaded", 1))
            nc.vector.memset(eps2[:, :], EPS * RW_HEADS).then_inc(once["set"], 1)
            nc.vector.memset(r_next[:, SEQ - 1:SEQ], 0.0).then_inc(once["set"], 1)
            nc.vector.memset(decay[:, :, 0:1], 0.0).then_inc(once["set"], 1)
            nc.vector.tensor_copy(spread[:, :, :].rearrange("p v (h k) -> p v h k", h=RW_HEADS),
                                  chip.ident[:, :].rearrange("p (h v o) -> p v h o", h=RW_HEADS, o=1).to_broadcast([P, HS, RW_HEADS, HS]))\
              .then_inc(once["set"], 1)
            with dve.Fori(0, B) as step:
                chain = Chain(dve, sig, "mix_chain", step)
                norm_vector(nc, dve, sig, m, step, x_tile(chip, step, T), lambda t: m.xn[:, t, :], ["xT_psum"])
                dve.wait_ge(*sig("xT", step, 1))
                nc.vector.tensor_scalar(delta[:, 0:1], m.xT[:, 0:1], -1.0, None, ALU.mult).then_inc(sig["mix_chain"], 1)
                chain.n += 1
                chain(nc.vector.tensor_tensor(delta[:, 1:SEQ], m.xT[:, 0:SEQ - 1], m.xT[:, 1:SEQ], ALU.subtract))
                chain(nc.vector.scalar_tensor_tensor(xm[:, :], delta[:, :], tiles["miu_x"][:, 0:1], m.xT[:, :], ALU.mult, ALU.add))
                dve.wait_ge(*sig("miu_psum", step, 1))
                dve.wait_ge(*sig("kvrg_psum", step))
                for f in range(MIXES):
                    chain(nc.vector.scalar_tensor_tensor(mix[:, f, :], miu_psum[:, f, :], tiles["lambda"][:, f:f + 1], delta[:, :],
                                                         ALU.add, ALU.mult))
                nc.vector.tensor_tensor(mix[:, :, :], mix[:, :, :], one(m.xT[:, :]).to_broadcast([P, MIXES, SEQ]), ALU.add)\
                  .then_inc(sig["mixed"], 1)
                chain.done()
                dve.wait_ge(*sig("kvr", step, 1))
                nc.vector.scalar_tensor_tensor(ruk[:, :], rT[:, :], tiles["u"][:, 0:1], kT[:, :], ALU.mult, ALU.mult)\
                  .then_inc(sig["ruk"], 1)
                gates = Chain(dve, sig, "gate_chain", step)
                dve.wait_ge(*sig("g_exp", step, 1))
                gates(nc.vector.tensor_scalar(gate[:, :], expg[:, :], 1.0, None, ALU.add))
                gates(nc.vector.reciprocal(gate[:, :], gate[:, :]))
                nc.vector.tensor_tensor(gate[:, :], work[:, 2, 1, :], gate[:, :], ALU.mult).then_inc(sig["gate"], 1)
                gates.done()
                dve.wait_ge(*sig("bonus_psum", step, 1))
                nc.vector.tensor_tensor(bonus[:, :], work[:, 3, 1, :], vT[:, :], ALU.mult).then_inc(sig["bonus"], 1)
                dve.wait_ge(*sig("decay", step, 1))
                for n in range(ROUNDS):
                    dve.wait_ge(*sig("vb", step, n + 1))
                    dve.wait_ge(*sig("scan", step, max(n - 1, 0)))
                    nc.vector.tensor_tensor(kv[:, n % 2, :, :], vb[n % 2][:, :, :], one(kT[:, :]).to_broadcast([P, PAIR, SEQ]), ALU.mult)\
                      .then_inc(sig["kv"], 1)
                    dve.wait_ge(*sig("kv", step, n + 1))
                    dve.wait_ge(*sig("prod", step, max(n - 1, 0)))
                    flat = lambda tile: tile.rearrange("p a s -> p (a s)")
                    nc.vector.tensor_tensor_scan(flat(state[:, n % 2, :, :]), flat(decay[:, :, :]), flat(kv[:, n % 2, :, :]), 0.0,
                                                 ALU.mult, ALU.add).then_inc(sig["scan"], 1)
                dve.wait_ge(*sig("y_acc", step, ROUNDS))
                dve.wait_ge(*sig("bonus", step, 1))
                nc.vector.tensor_copy(yT[:, 0:1], bonus[:, 0:1])
                nc.vector.tensor_tensor(yT[:, 1:SEQ], y_psum[:, 0:SEQ - 1], bonus[:, 1:SEQ], ALU.add).then_inc(sig["yT"], 1)
                dve.wait_ge(*sig("y_tok", step, 1))
                for n in range(T * RW_HEADS):
                    ins = nc.vector.bn_stats(y_stats[:, n, :], work[:, 0, n // 2, (n % 2) * HS:(n % 2 + 1) * HS])
                ins.then_inc(sig["yn_stats"], 1)
                sig.apart(dve, "yn_stats", step, 1)
                for n in range(T * RW_HEADS):
                    ins = nc.vector.bn_aggr(y_moments[:, n, :], y_stats[:, n, :])
                ins.then_inc(sig["yn_moments"], 1)
                dve.wait_ge(*sig("yn_rstd", step, 1))
                for n in range(T * RW_HEADS):
                    half = slice((n % 2) * HS, (n % 2 + 1) * HS)
                    ins = nc.vector.tensor_scalar(yn[:, n // 2, half], work[:, 0, n // 2, half], y_moments[:, n, 0:1],
                                                  y_rstd[:, n:n + 1], ALU.subtract, ALU.mult)
                ins.then_inc(sig["yn"], 1)
                dve.wait_ge(*sig("ynT", step, 1))
                dve.wait_ge(*sig("gate", step, 1))
                nc.vector.tensor_tensor(gated[:, :], ynT[:, :], gate[:, :], ALU.mult).then_inc(sig["gated"], 1)
                dve.wait_ge(*sig("out_psum", step, 1))
                xs = chip.x[:, bass.ds(step * T, T), :]
                nc.vector.tensor_tensor(xs, work[:, 0, :, 0:D], xs, ALU.add).then_inc(sig["x"], 1)
                dve.wait_ge(*sig("x", step, 1))
    sig.ended(B)
    once.ended(1)


DEPTH = 6
LH, LD = 16, 64
INNER = LH * LD
WINDOW = 32
REACH = P + WINDOW
LPAIRS = LH // 2
FF = 341
FF_CHUNKS = 3
FF_TILES = 4
FF_STEPS = TILES // FF_TILES
CHUNKS = 4
LIFT = 2.0 ** 20

STACK_ATTENTION = dict(z_copy=1, zT_psum=1, xsT=1, proj=CHUNKS + HALVES, square=CHUNKS, norm2=CHUNKS, half_turns=CHUNKS,
                       turn_sum=CHUNKS, clamped=1, log2=1, rnorm=1, qk=CHUNKS, qkT_psum=2 * CHUNKS, qkT=2 * CHUNKS,
                       v=HALVES, scores=LPAIRS, negmax=LPAIRS, shifted=LPAIRS, probs=LPAIRS, probsT_psum=LPAIRS,
                       probsT=LPAIRS, near=LPAIRS, pv=LPAIRS, rsum=LPAIRS, context=LPAIRS, ctxT_psum=4, ctxT=4,
                       out_psum=1, z=1)
STACK_FFN = dict(f_copy=1, fzT_psum=1, fxsT=1, fxs_psum=1, norm_chain=1, moments=1, act_norm=1, rstd=1, xn=1,
                 fxnT_psum=1, fxnT=1, h_psum=FF_CHUNKS, gelu=FF_CHUNKS, hidden=FF_CHUNKS, f_psum=1, zf=2)
STACK_LAYER = dict(tables=1, attention_weights=48, ffn_weights=64)


def stage_stack(chip):
    nc, dram, att, ffn, layer_sig, once = chip.nc, chip.dram, chip.loop, chip.ffn, chip.layer, chip.once
    att.use(STACK_ATTENTION)
    once.use(dict(set=4, loaded=48))
    with ExitStack() as ctx:
        sb = lambda name, shape, dt=F32: ctx.enter_context(nc.sbuf_tensor(chip.tag + name, shape, dt))
        z = sb("z", [P, TILES, D])
        wqkv, wo = sb("wqkv", [P, 3 * INNER]), sb("wo", [P, LPAIRS, D])
        rows, base, tables = sb("rows", [P, 4, 1, LD]), sb("base", [P, 4, HALVES, LD]), sb("tables", [P, 4, HALVES, LD])
        w1, w2, b2 = sb("w1", [P, 2 * FF]), sb("w2", [P, FF_CHUNKS, D]), sb("b2", [P, 1, D])
        cols = sb("cols", [P, 2 * FF_CHUNKS + 2])
        ident_bf, band = sb("ident_bf", [P, P], BF16), sb("band", [P, HALVES, REACH], BF16)
        lift = sb("lift", [P, 1])
        zc, xsT = sb("zc", [P, HALVES, D]), sb("xsT", [P, SEQ])
        square = sb("square", [P, 2, INNER])
        halves = sb("halves", [P, 2, 2, INNER])
        qk = sb("qk", [P, CHUNKS, INNER])
        norm2, clamped = sb("norm2", [P, CHUNKS, LH, 1]), sb("clamped", [P, CHUNKS, LH, 1])
        log2, rnorm = sb("log2", [P, CHUNKS, LH, 1]), sb("rnorm", [P, CHUNKS, LH, 1])
        qkT = sb("qkT", [P, 2, LPAIRS, SEQ])
        v, v_near = sb("v", [P, HALVES, LH, LD + 1]), sb("v_near", [WINDOW, LH, LD + 1])
        negmax = sb("negmax", [P, 2, 2, HALVES, 1])
        shifted, probs = sb("shifted", [P, 2, 2, HALVES, REACH]), sb("probs", [P, 2, 2, HALVES, REACH])
        probsT, near = sb("probsT", [P, 2, 2, HALVES, P]), sb("near", [WINDOW, 2, 2, P])
        rsum = sb("rsum", [P, 2, 2, HALVES, 1])
        context, ctxT = sb("context", [P, HALVES, INNER]), sb("ctxT", [P, LPAIRS, SEQ])
        fz, fxsT = sb("fz", [P, FF_TILES, D]), sb("fxsT", [P, 2, SEQ])
        stats, moments = sb("stats", [P, FF_TILES, 6]), sb("moments", [P, FF_TILES, 2])
        logvar, rstd = sb("logvar", [P, FF_TILES]), sb("rstd", [P, FF_TILES])
        fxn, fxnT = sb("fxn", [P, FF_TILES, D]), sb("fxnT", [P, FF_TILES * P])
        gelu, hidden = sb("gelu", [P, 2, FF_TILES * P]), sb("hidden", [P, FF_CHUNKS, FF_TILES * P])
        big = [ctx.enter_context(nc.psum_tensor(f"{chip.tag}big{n}", [P, 2, 512], F32)) for n in range(2)]
        flip = [ctx.enter_context(nc.psum_tensor(f"{chip.tag}flip{n}", [P, 512], F32)) for n in range(2)]
        acc = [ctx.enter_context(nc.psum_tensor(f"{chip.tag}acc{n}", [P, 512], F32)) for n in range(2)]
        tiles4 = lambda bank: bank[:, :].rearrange("p (t d) -> p t d", d=D)
        pv_of = lambda n: acc[n % 2][:, 0:4 * (LD + 1)].rearrange("p (h t c) -> p h t c", h=2, t=HALVES)
        near_psum = lambda n: big[n % 2][0:WINDOW, :, HALVES * REACH:HALVES * REACH + P]
        scores_of = lambda n: big[n % 2][:, :, 0:HALVES * REACH].rearrange("p h (t k) -> p h t k", t=HALVES)

        m = Norm(chip, ctx, FF_TILES, turned=False)
        first = chip.ffn
        first.use(dict(norm_chain=1, moments=1, act_norm=1, rstd=1, xn=1))
        with nc.Block() as block:
            @block.scalar
            def _(act):
                with act.Fori(0, FF_STEPS) as step:
                    norm_rstd(nc, act, first, chip, m, step)

            @block.vector
            def _(dve):
                with dve.Fori(0, FF_STEPS) as step:
                    norm_vector(nc, dve, first, m, step, x_tile(chip, step, FF_TILES),
                                lambda t: z[:, bass.ds(step * FF_TILES + t, 1), :].rearrange("p a d -> p (a d)"), [])
                    dve.wait_ge(*first("xn", step, 1))
                nc.vector.memset(xsT[64:P, 0:1], 0.0).then_inc(once["set"], 1)
                nc.vector.memset(fxsT[64:P, :, 0:1], 0.0).then_inc(once["set"], 1)
                nc.vector.memset(v[:, :, :, LD:LD + 1], 1.0).then_inc(once["set"], 1)
                nc.vector.memset(v_near[:, :, LD:LD + 1], 1.0)
                nc.vector.memset(lift[:, :], 0.5 * float(np.log(LIFT))).then_inc(once["set"], 1)
                dve.wait_ge(*once("set", 1))

            @block.sync
            def _(sp):
                sp.dma_start(base[:, :, :, :], dram["T_base"]).then_inc(once["loaded"], 16)
                sp.dma_start(ident_bf[:, :], dram["ident_bf"]).then_inc(once["loaded"], 16)
                sp.dma_start(band[:, :, :], dram["T_band"]).then_inc(once["loaded"], 16)
                sp.wait_ge(*once("loaded", 1))

        first.ended(FF_STEPS)
        once.ended(1)
        ffn.use(STACK_FFN)
        block = ctx.enter_context(nc.Block())

        @block.sync
        def _(sp):
            def load_attention(layer):
                for tile, name in ((wqkv, "wqkv"), (wo, "wo"), (rows, "rows")):
                    sp.dma_start(tile[:], layer_view(dram["T_" + name], layer)).then_inc(layer_sig["attention_weights"], 16)

            def load_ffn(layer):
                for tile, name in ((w1, "w1"), (w2, "w2"), (cols, "cols"), (b2, "b2")):
                    sp.dma_start(tile[:], layer_view(dram["T_" + name], layer)).then_inc(layer_sig["ffn_weights"], 16)

            load_attention(0)
            load_ffn(0)
            if DEPTH > 1:
                with sp.Fori(0, DEPTH - 1) as layer:
                    sp.wait_ge(*att("out_psum", (layer + 1) * B))
                    att.settle(sp)
                    sp.wait_ge(*layer_sig("tables", layer, 1))
                    att.settle(sp)
                    load_attention(layer + 1)
                    sp.wait_ge(*ffn("zf", (layer + 1) * FF_STEPS))
                    att.settle(sp)
                    load_ffn(layer + 1)

        @block.tensor
        def _(pe):
            with pe.Fori(0, DEPTH) as layer:
                pe.wait_ge(*layer_sig("attention_weights", layer, 48))
                pe.wait_ge(*ffn("zf", layer * FF_STEPS))
                att.settle(pe)
                with pe.Fori(0, B) as b:
                    step = layer * B + b
                    pe.wait_ge(*att("z_copy", step, 1))
                    pe.wait_ge(*att("context", step))
                    for t in range(HALVES):
                        ins = nc.tensor.transpose(acc[1][:, t * P:(t + 1) * P], zc[:, t, :], chip.ident[:, :])
                    ins.then_inc(att["zT_psum"], 1)
                    pe.wait_ge(*att("xsT", step, 1))
                    pe.wait_ge(*att("near", step))
                    for n in range(CHUNKS + HALVES):
                        if 2 <= n < 2 + CHUNKS:
                            pe.wait_ge(*att("half_turns", step, n - 1))
                            pe.wait_ge(*att("square", step, n - 1))
                        for c in range(2):
                            at = (n // HALVES) * INNER + c * 512
                            ins = nc.tensor.matmul(big[n % 2][:, c, :], xsT[:, (n % HALVES) * P:(n % HALVES + 1) * P],
                                                   wqkv[:, at:at + 512], start=True, stop=True)
                        ins.then_inc(att["proj"], 1)
                    pe.wait_ge(*att("ctxT", step))
                    for n in range(2 * CHUNKS):
                        c, part = n // 2, n % 2
                        pe.wait_ge(*att("qk", step, c + 1))
                        pe.wait_ge(*att("qkT", step, max(n - 1, 0)))
                        for i in range(4):
                            pair = 4 * part + i
                            ins = nc.tensor.transpose(flip[n % 2][:, i * P:(i + 1) * P], qk[:, c, pair * P:(pair + 1) * P],
                                                      chip.ident[:, :])
                        ins.then_inc(att["qkT_psum"], 1)
                    pe.wait_ge(*att("v", step, HALVES))
                    pe.wait_ge(*att("qkT", step, 2 * CHUNKS))

                    def score(n):
                        if n > 1:
                            pe.wait_ge(*att("near", step, n - 1))
                        for h in range(2):
                            nc.tensor.matmul(big[n % 2][:, h, 0:HALVES * REACH], ident_bf[:, :],
                                             band[:, :, :].rearrange("p t k -> p (t k)"), start=True, stop=False,
                                             skip_group_check=True)
                        for t in range(HALVES):
                            for h in range(2):
                                of_head = slice(h * LD, (h + 1) * LD)
                                first_key, at = (0, WINDOW) if t == 0 else (P - WINDOW, REACH)
                                ins = nc.tensor.matmul(big[n % 2][:, h, at:HALVES * REACH if t else REACH],
                                                       qkT[of_head, 0, n, t * P:(t + 1) * P],
                                                       qkT[of_head, 1, n, first_key:(t + 1) * P],
                                                       start=False, stop=t == HALVES - 1, skip_group_check=True)
                        ins.then_inc(att["scores"], 1)

                    def turn_probs(n):
                        pe.wait_ge(*att("probs", step, n + 1))
                        if n > 1:
                            pe.wait_ge(*att("probsT", step, n - 1))
                        for h in range(2):
                            for t in range(HALVES):
                                nc.tensor.transpose(flip[n % 2][:, (2 * h + t) * P:(2 * h + t + 1) * P],
                                                    probs[:, n % 2, h, t, WINDOW:REACH], chip.ident[:, :])
                            ins = nc.tensor.transpose(near_psum(n)[:, h, :], probs[:, n % 2, h, 1, 0:WINDOW], chip.ident[:, :])
                        ins.then_inc(att["probsT_psum"], 1)

                    def weigh(n):
                        pe.wait_ge(*att("probsT", step, n + 1))
                        pe.wait_ge(*att("near", step, n + 1))
                        if n == 0:
                            pe.wait_ge(*att("z", step))
                        if n > 1:
                            pe.wait_ge(*att("context", step, n - 1))
                        for h in range(2):
                            head = 2 * n + h
                            nc.tensor.matmul(pv_of(n)[:, h, 0, :], probsT[:, n % 2, h, 0, :], v[:, 0, head, :], start=True, stop=True)
                            nc.tensor.matmul(pv_of(n)[:, h, 1, :], near[:, n % 2, h, :], v_near[:, head, :], start=True, stop=False)
                            ins = nc.tensor.matmul(pv_of(n)[:, h, 1, :], probsT[:, n % 2, h, 1, :], v[:, 1, head, :], start=False, stop=True)
                        ins.then_inc(att["pv"], 1)

                    score(0)
                    for n in range(LPAIRS):
                        if n + 1 < LPAIRS:
                            score(n + 1)
                        turn_probs(n)
                        weigh(n)
                    pe.wait_ge(*att("probsT", step, LPAIRS))
                    pe.wait_ge(*att("context", step, LPAIRS))
                    for n in range(4):
                        if n > 1:
                            pe.wait_ge(*att("ctxT", step, n - 1))
                        for i in range(2):
                            for t in range(HALVES):
                                c = 2 * n + i
                                ins = nc.tensor.transpose(flip[n % 2][:, (2 * i + t) * P:(2 * i + t + 1) * P],
                                                          context[:, t, c * P:(c + 1) * P], chip.ident[:, :])
                        ins.then_inc(att["ctxT_psum"], 1)
                    pe.wait_ge(*att("ctxT", step, 4))
                    for t in range(HALVES):
                        for c in range(LPAIRS):
                            ins = nc.tensor.matmul(acc[0][:, t * P:(t + 1) * P], ctxT[:, c, t * P:(t + 1) * P], wo[:, c, :],
                                                   start=c == 0, stop=c == LPAIRS - 1)
                    ins.then_inc(att["out_psum"], 1)

                pe.wait_ge(*layer_sig("ffn_weights", layer, 64))
                pe.wait_ge(*att("z", (layer + 1) * B))
                pe.wait_ge(*att("xsT", (layer + 1) * B))
                att.settle(pe)
                with pe.Fori(0, FF_STEPS) as s:
                    step = layer * FF_STEPS + s
                    pe.wait_ge(*ffn("f_copy", step, 1))
                    for t in range(FF_TILES):
                        ins = nc.tensor.transpose(acc[0][:, t * P:(t + 1) * P], fz[:, t, :], chip.ident[:, :])
                    ins.then_inc(ffn["fzT_psum"], 1)
                    pe.wait_ge(*ffn("fxsT", step, 1))
                    for t in range(FF_TILES):
                        ins = nc.tensor.transpose(acc[1][:, t * P:(t + 1) * P], fxsT[:, t // 2, (t % 2) * P:(t % 2 + 1) * P],
                                                  chip.ident[:, :])
                    ins.then_inc(ffn["fxs_psum"], 1)
                    pe.wait_ge(*ffn("xn", step, 1))
                    for t in range(FF_TILES):
                        ins = nc.tensor.transpose(acc[0][:, t * P:(t + 1) * P], fxn[:, t, :], chip.ident[:, :])
                    ins.then_inc(ffn["fxnT_psum"], 1)
                    pe.wait_ge(*ffn("fxnT", step, 1))
                    for c in range(FF_CHUNKS):
                        width = min(P, FF - c * P)
                        pe.wait_ge(*ffn("hidden", step, max(c - 1, 0)))
                        for half in range(2):
                            at = half * FF + c * P
                            ins = nc.tensor.matmul(big[c % 2][0:width, half, :], w1[:, at:at + width], fxnT[:, :],
                                                   start=True, stop=True)
                        ins.then_inc(ffn["h_psum"], 1)
                    pe.wait_ge(*ffn("hidden", step, FF_CHUNKS))
                    pe.wait_ge(*ffn("zf", step))
                    for t in range(FF_TILES):
                        for c in range(FF_CHUNKS):
                            width = min(P, FF - c * P)
                            ins = nc.tensor.matmul(flip[0][:, t * P:(t + 1) * P], hidden[0:width, c, t * P:(t + 1) * P],
                                                   w2[0:width, c, :], start=c == 0, stop=c == FF_CHUNKS - 1)
                    ins.then_inc(ffn["f_psum"], 1)

        @block.scalar
        def _(act):
            def shifted_copy(target, bank, done):
                nc.scalar.activation(target[0:64], bank[0:64], ACT.Copy)
                tokens = len(target.shape) - 1
                if tokens == 1:
                    ins = nc.scalar.activation(target[64:P, 1:SEQ], bank[64:P, 0:SEQ - 1], ACT.Copy)
                else:
                    ins = nc.scalar.activation(target[64:P, :, 1:SEQ], bank[64:P, :, 0:SEQ - 1], ACT.Copy)
                ins.then_inc(done, 1)

            with act.Fori(0, DEPTH) as layer:
                with act.Fori(0, B) as b:
                    step = layer * B + b
                    act.wait_ge(*att("zT_psum", step, 1))
                    shifted_copy(xsT[:, :], acc[1][:, 0:SEQ], att["xsT"])
                    for n in range(CHUNKS):
                        act.wait_ge(*att("proj", step, n + 1))
                        act.wait_ge(*att("norm2", step, max(n - 1, 0)))
                        nc.scalar.activation(square[:, n % 2, :], big[n % 2][:, :, :].rearrange("p a n -> p (a n)"), ACT.Square)\
                          .then_inc(att["square"], 1)
                    for t in range(HALVES):
                        n = CHUNKS + t
                        act.wait_ge(*att("proj", step, n + 1))
                        if t == 0:
                            act.wait_ge(*att("pv", step))
                        heads = lambda rows: big[n % 2][rows, :, :].rearrange("p a (h d) -> p (a h) d", d=LD)
                        if t == 0:
                            nc.scalar.activation(v_near[:, :, 0:LD], heads(slice(P - WINDOW, P)), ACT.Copy)
                        nc.scalar.activation(v[:, t, :, 0:LD], heads(slice(0, P)), ACT.Copy).then_inc(att["v"], 1)
                    act.wait_ge(*att("clamped", step, 1))
                    nc.scalar.activation(log2[:, :, :, :], clamped[:, :, :, :], ACT.Ln).then_inc(att["log2"], 1)
                    act.wait_ge(*att("log2", step, 1))
                    nc.scalar.activation(rnorm[:, :, :, :], log2[:, :, :, :], ACT.Exp, scale=-0.5, bias=lift[:, 0:1])\
                      .then_inc(att["rnorm"], 1)
                    for n in range(2 * CHUNKS):
                        c, part = n // 2, n % 2
                        act.wait_ge(*att("qkT_psum", step, n + 1))
                        target = qkT[:, c // 2, 4 * part:4 * part + 4, (c % 2) * P:(c % 2 + 1) * P]
                        nc.scalar.activation(target, tiles4(flip[n % 2]), ACT.Copy).then_inc(att["qkT"], 1)

                    def exponential(n):
                        act.wait_ge(*att("shifted", step, n + 1))
                        act.wait_ge(*att("probsT_psum", step, max(n - 1, 0)))
                        nc.scalar.activation(probs[:, n % 2], shifted[:, n % 2], ACT.Exp).then_inc(att["probs"], 1)

                    exponential(0)
                    for n in range(LPAIRS):
                        if n + 1 < LPAIRS:
                            exponential(n + 1)
                        act.wait_ge(*att("probsT_psum", step, n + 1))
                        act.wait_ge(*att("pv", step, max(n - 1, 0)))
                        nc.scalar.activation(probsT[:, n % 2].rearrange("p h t q -> p (h t) q"), tiles4(flip[n % 2]), ACT.Copy)\
                          .then_inc(att["probsT"], 1)
                    act.wait_ge(*att("out_psum", step))
                    for n in range(4):
                        act.wait_ge(*att("ctxT_psum", step, n + 1))
                        nc.scalar.activation(ctxT[:, 2 * n:2 * n + 2, :], flip[n % 2][:, :].rearrange("p (c s) -> p c s", c=2), ACT.Copy)\
                          .then_inc(att["ctxT"], 1)
                act.wait_ge(*layer_sig("ffn_weights", layer, 64))
                with act.Fori(0, FF_STEPS) as s:
                    step = layer * FF_STEPS + s
                    act.wait_ge(*ffn("fzT_psum", step, 1))
                    shifted_copy(fxsT[:, :, :], acc[0][:, :].rearrange("p (b s) -> p b s", b=2), ffn["fxsT"])
                    act.wait_ge(*ffn("moments", step, 1))
                    nc.scalar.activation(logvar[:, :], moments[:, :, 1], ACT.Ln, bias=chip.eps[:, 0:1]).then_inc(ffn["act_norm"], 1)
                    act.wait_ge(*ffn("act_norm", step, 1))
                    nc.scalar.activation(rstd[:, :], logvar[:, :], ACT.Exp, scale=-0.5).then_inc(ffn["rstd"], 1)
                    act.wait_ge(*ffn("fxnT_psum", step, 1))
                    nc.scalar.activation(fxnT[:, :], acc[0][:, :], ACT.Identity, scale=cols[:, 2 * FF_CHUNKS:2 * FF_CHUNKS + 1],
                                         bias=cols[:, 2 * FF_CHUNKS + 1:2 * FF_CHUNKS + 2]).then_inc(ffn["fxnT"], 1)
                    for c in range(FF_CHUNKS):
                        width = min(P, FF - c * P)
                        act.wait_ge(*ffn("h_psum", step, c + 1))
                        act.wait_ge(*ffn("hidden", step, max(c - 1, 0)))
                        nc.scalar.activation(gelu[0:width, c % 2, :], big[c % 2][0:width, 1, :], ACT.Gelu,
                                             bias=cols[0:width, FF_CHUNKS + c:FF_CHUNKS + c + 1]).then_inc(ffn["gelu"], 1)

        @block.gpsimd
        def _(pool):
            with pool.Fori(0, DEPTH) as layer:
                with pool.Fori(0, B) as b:
                    step = layer * B + b
                    pool.wait_ge(*att("qkT_psum", step))
                    for n in range(CHUNKS):
                        pool.wait_ge(*att("half_turns", step, n + 1))
                        nc.gpsimd.tensor_tensor(qk[:, n, :], halves[:, n % 2, 0, :], halves[:, n % 2, 1, :], ALU.add)\
                          .then_inc(att["turn_sum"], 1)
                    pool.wait_ge(*att("rnorm", step, 1))
                    pool.wait_ge(*att("turn_sum", step, CHUNKS))
                    for n in range(CHUNKS):
                        heads = qk[:, n, :].rearrange("p (h d) -> p h d", d=LD)
                        nc.gpsimd.tensor_tensor(heads, heads, rnorm[:, n, :, :].to_broadcast([P, LH, LD]), ALU.mult)\
                          .then_inc(att["qk"], 1)

        @block.vector
        def _(dve):
            with dve.Fori(0, DEPTH) as layer:
                dve.wait_ge(*layer_sig("attention_weights", layer, 48))
                dve.wait_ge(*att("half_turns", layer * B))
                nc.vector.tensor_tensor(tables[:, :, :, :], base[:, :, :, :], rows[:, :, :, :].to_broadcast([P, 4, HALVES, LD]), ALU.mult)\
                  .then_inc(layer_sig["tables"], 1)
                dve.wait_ge(*layer_sig("tables", layer, 1))
                att.settle(dve)
                with dve.Fori(0, B) as b:
                    step = layer * B + b
                    z_of = z[:, bass.ds(b * HALVES, HALVES), :]
                    dve.wait_ge(*att("zT_psum", step))
                    nc.vector.tensor_copy(zc[:, :, :], z_of).then_inc(att["z_copy"], 1)
                    for n in range(CHUNKS):
                        dve.wait_ge(*att("proj", step, n + 1))
                        dve.wait_ge(*att("square", step, n + 1))
                        dve.wait_ge(*att("turn_sum", step, max(n - 1, 0)))
                        which, t = n // 2, n % 2
                        heads = big[n % 2][:, :, :].rearrange("p a (h d) -> p (a h) d", d=LD)
                        out = halves[:, n % 2].rearrange("p k (h d) -> p k h d", d=LD)
                        cos = tables[:, 2 * which, t:t + 1, :]
                        sin = tables[:, 2 * which + 1, t:t + 1, :]
                        nc.vector.tensor_tensor(out[:, 0], heads, cos.to_broadcast([P, LH, LD]), ALU.mult)
                        for half in range(2):
                            to, of = (slice(0, LD // 2), slice(LD // 2, LD))[::1 if half == 0 else -1]
                            ins = nc.vector.tensor_tensor(out[:, 1, :, to], heads[:, :, of], sin[:, :, to].to_broadcast([P, LH, LD // 2]),
                                                          ALU.mult)
                        ins.then_inc(att["half_turns"], 1)
                        if n == 0:
                            dve.wait_ge(*att("clamped", step))
                        nc.vector.tensor_reduce(norm2[:, n, :, 0], square[:, n % 2, :].rearrange("p (h d) -> p h d", d=LD), AX.X, ALU.add)\
                          .then_inc(att["norm2"], 1)
                    dve.wait_ge(*att("norm2", step, CHUNKS))
                    dve.wait_ge(*att("log2", step))
                    nc.vector.tensor_scalar(clamped[:, :, :, :], norm2[:, :, :, :], 1e-24, LIFT, ALU.max, ALU.mult)\
                      .then_inc(att["clamped"], 1)

                    def shift(n):
                        dve.wait_ge(*att("scores", step, n + 1))
                        dve.wait_ge(*att("shifted", step, max(n - 1, 0)))
                        nc.vector.tensor_reduce(negmax[:, n % 2, :, :, 0], scores_of(n), AX.X, ALU.max, negate=True)\
                          .then_inc(att["negmax"], 1)
                        dve.wait_ge(*att("negmax", step, n + 1))
                        dve.wait_ge(*att("probs", step, max(n - 1, 0)))
                        nc.vector.tensor_tensor(shifted[:, n % 2], scores_of(n), negmax[:, n % 2].to_broadcast([P, 2, HALVES, REACH]), ALU.add)\
                          .then_inc(att["shifted"], 1)

                    shift(0)
                    for n in range(LPAIRS):
                        if n + 1 < LPAIRS:
                            shift(n + 1)
                        dve.wait_ge(*att("probsT_psum", step, n + 1))
                        dve.wait_ge(*att("pv", step, max(n - 1, 0)))
                        nc.vector.tensor_copy(near[:, n % 2], near_psum(n)).then_inc(att["near"], 1)
                        dve.wait_ge(*att("pv", step, n + 1))
                        dve.wait_ge(*att("context", step, max(n - 1, 0)))
                        nc.vector.reciprocal(rsum[:, n % 2], pv_of(n)[:, :, :, LD:LD + 1]).then_inc(att["rsum"], 1)
                        dve.wait_ge(*att("rsum", step, n + 1))
                        if n == 0:
                            dve.wait_ge(*att("ctxT_psum", step))
                        to = context[:, :, 2 * n * LD:2 * (n + 1) * LD].rearrange("p t (h d) -> p h t d", h=2)
                        nc.vector.tensor_tensor(to, pv_of(n)[:, :, :, 0:LD], rsum[:, n % 2].to_broadcast([P, 2, HALVES, LD]), ALU.mult)\
                          .then_inc(att["context"], 1)
                    dve.wait_ge(*att("out_psum", step, 1))
                    nc.vector.tensor_tensor(z_of, tiles4(acc[0])[:, 0:HALVES, :], z_of, ALU.add).then_inc(att["z"], 1)
                    dve.wait_ge(*att("z", step, 1))
                dve.wait_ge(*layer_sig("ffn_weights", layer, 64))
                att.settle(dve)
                with dve.Fori(0, FF_STEPS) as s:
                    step = layer * FF_STEPS + s
                    z_of = z[:, bass.ds(s * FF_TILES, FF_TILES), :]
                    dve.wait_ge(*ffn("fzT_psum", step))
                    nc.vector.tensor_copy(fz[:, :, :], z_of).then_inc(ffn["f_copy"], 1)
                    dve.wait_ge(*ffn("fxs_psum", step, 1))
                    for t in range(FF_TILES):
                        ins = nc.vector.bn_stats(stats[:, t, :], acc[1][:, t * P:(t + 1) * P])
                    ins.then_inc(ffn["norm_chain"], 1)
                    ffn.apart(dve, "norm_chain", step, 1)
                    for t in range(FF_TILES):
                        ins = nc.vector.bn_aggr(moments[:, t, :], stats[:, t, :])
                    ins.then_inc(ffn["moments"], 1)
                    dve.wait_ge(*ffn("rstd", step, 1))
                    dve.wait_ge(*ffn("fxnT_psum", step))
                    for t in range(FF_TILES):
                        ins = nc.vector.tensor_scalar(fxn[:, t, :], acc[1][:, t * P:(t + 1) * P], moments[:, t, 0:1],
                                                      rstd[:, t:t + 1], ALU.subtract, ALU.mult)
                    ins.then_inc(ffn["xn"], 1)
                    dve.wait_ge(*ffn("f_psum", step))
                    for c in range(FF_CHUNKS):
                        width = min(P, FF - c * P)
                        dve.wait_ge(*ffn("gelu", step, c + 1))
                        nc.vector.scalar_tensor_tensor(hidden[0:width, c, :], big[c % 2][0:width, 0, :], cols[0:width, c:c + 1],
                                                       gelu[0:width, c % 2, :], ALU.add, ALU.mult).then_inc(ffn["hidden"], 1)
                    dve.wait_ge(*ffn("f_psum", step, 1))
                    nc.vector.tensor_tensor(z_of, tiles4(flip[0]), z_of, ALU.add).then_inc(ffn["zf"], 1)
                    dve.wait_ge(*ffn("zf", step, 1))
                    nc.vector.tensor_tensor(z_of, z_of, b2[:, :, :].to_broadcast([P, FF_TILES, D]), ALU.add).then_inc(ffn["zf"], 1)
                    dve.wait_ge(*ffn("zf", step, 2))
            nc.vector.scalar_tensor_tensor(chip.x[:, :, :], z[:, :, :], 0.5, chip.x[:, :, :], ALU.mult, ALU.add)
    att.ended(DEPTH * B)
    ffn.ended(DEPTH * FF_STEPS)
    layer_sig.ended(DEPTH)


def layer_view(a, layer):
    part = a[bass.ds(layer, 1)]
    names = " ".join("cde"[:len(a.shape) - 2])
    return part.rearrange(f"a p {names} -> (a p) {names}")


def loop_signals():
    stages = [moe_signals(gated, 1) for gated in (False, True)] + [attention_signals(level) for level in (0, 2, 3)]
    return sorted(set().union(*stages, L1_FFN_SIGNALS, RW_SIGNALS, STACK_ATTENTION))


def program(nc, dram, out, stages):
    with ExitStack() as ctx:
        chip = Chip(nc, ctx, dram, loop_signals())
        cossin = ctx.enter_context(nc.sbuf_tensor("cossin", [P, 2, D], F32))
        begin = chip.once
        begin.use(dict(loaded=32, set=1))
        with nc.Block() as block:
            @block.sync
            def _(sp):
                sp.dma_start(chip.x[:, :, :], dram["x"].rearrange("b (h p) d -> p (b h) d", p=P)).then_inc(begin["loaded"], 16)
                sp.dma_start(chip.ident[:, :], dram["ident"]).then_inc(begin["loaded"], 16)
                sp.wait_ge(*begin("loaded", 1))

            @block.gpsimd
            def _(pool):
                chip.loop.seed(pool)
                chip.ffn.seed(pool)

            @block.vector
            def _(dve):
                nc.vector.memset(chip.eps[:, :], EPS).then_inc(begin["set"], 1)
                dve.wait_ge(*begin("set", 1))
        begin.ended(1)
        setup_l1_angles(chip, cossin)
        for number, (level, part) in enumerate(stages):
            chip.tag = f"stage{number}_"
            if part == "attention" and level == 1:
                stage_rwkv(chip)
            elif part == "attention":
                stage_attention(chip, level)
            elif level == 1:
                stage_l1_ffn(chip, cossin)
            elif level == 2:
                stage_stack(chip)
            else:
                stage_moe(chip, level)
        end = chip.once
        end.use(dict(loaded=16))
        with nc.Block() as block:
            @block.sync
            def _(sp):
                sp.dma_start(out.rearrange("b (h p) d -> p (b h) d", p=P), chip.x[:, :, :]).then_inc(end["loaded"], 16)
                sp.wait_ge(*end("loaded", 1))


STAGES = [(level, part) for level in range(4) for part in ("ffn", "attention", "ffn")]


def kernel(**inputs):
    import concourse.bacc as bacc
    from concourse.bass_utils import run_bass_kernel_spmd

    nc = bacc.Bacc("TRN2", target_bir_lowering=False, num_devices=1)
    arrays, dram = {}, {}
    for name, a in layout(inputs).items():
        a = np.ascontiguousarray(a)
        arrays["in_" + name] = a
        dram[name] = nc.dram_tensor("in_" + name, a.shape, mybir.dt.from_np(a.dtype), kind="ExternalInput").ap()
    out = nc.dram_tensor("out", (B, SEQ, D), F32, kind="ExternalOutput").ap()
    program(nc, dram, out, STAGES)
    r = run_bass_kernel_spmd(nc, [arrays], core_ids=[0])
    return r.results[0]["out"]


def layout(inputs):
    w = {name: np.asarray(a) for name, a in inputs.items()}
    a = {"x": w["L0_attn_embeddings"], "ident": np.eye(P, dtype=np.float32)}
    for name in ("L1_ffn_theta", "L1_ffn_phi", "L1_ffn_theta_noise", "L1_ffn_phi_noise"):
        a[name] = w[name]
    rows = lambda v: np.broadcast_to(v, (P,) + v.shape)
    a["iota"] = rows(np.arange(EXPERTS, dtype=np.float32))
    split = lambda v: v.reshape(v.shape[0], -1, P, v.shape[-1]).transpose(2, 0, 1, 3)
    a["L0_w_gate"], a["L0_b_gate"] = w["L0_ffn_Wr"].T, rows(w["L0_ffn_br"])
    a["L0_w_up"] = w["L0_ffn_W1"].transpose(2, 0, 1)
    a["L0_b_up"] = w["L0_ffn_b1"].reshape(EXPERTS, -1, P).transpose(2, 0, 1)
    a["L0_w_down"] = split(w["L0_ffn_W2"].transpose(0, 2, 1))
    a["L0_b_down"] = w["L0_ffn_b2"]
    a["L0_gamma"], a["L0_beta"] = rows(w["L0_ffn_gamma"]), rows(w["L0_ffn_beta"])
    a["L3_w_gate"] = w["L3_ffn_gate_kernel"]
    a["L3_w_up"], a["L3_w_up2"] = (w[n].transpose(1, 0, 2) for n in ("L3_ffn_w0_kernel", "L3_ffn_w1_kernel"))
    a["L3_w_down"] = split(w["L3_ffn_wo_kernel"])
    attention_layout(w, a, rows)
    rwkv_layout(w, a)
    stack_layout(w, a)
    return a


def attention_layout(w, a, rows):
    bf16 = mybir.dt.np(BF16)
    a["ident_bf"] = np.eye(P, dtype=np.float32).astype(bf16)
    above = np.triu(np.full((P, P), MASKED, np.float32), 1)
    a["mask"], a["maskT"] = above.astype(bf16), np.ascontiguousarray(above.T).astype(bf16)

    def banded(v, ninth=0.0):
        out = np.zeros((v.shape[0], GROUPS, GROUPS, BAND), np.float32)
        out[..., :DK] = v.reshape(v.shape[0], GROUPS, GROUPS, DK)
        out[..., DK] = ninth
        return out.reshape(v.shape[0], GROUPS, P)

    pairs = np.arange(D) ^ 1
    heads = lambda v: v.transpose(1, 0, 2).reshape(D, D)
    q0, k0, v0 = (w["L0_attn_W" + n] for n in "qkv")
    a["A0_wq"], a["A0_wk"], a["A0_wv"] = banded(heads(q0)), banded(heads(k0)), heads(v0)
    a["A0_bq"] = banded(w["L0_attn_bq"].reshape(1, D))[0].T
    a["A0_bk"] = banded(w["L0_attn_bk"].reshape(1, D), 1.0)[0].T
    a["A0_bv"], a["A0_wo"], a["A0_bo"] = rows(w["L0_attn_bv"].reshape(D)), w["L0_attn_Wo"], rows(w["L0_attn_bo"])
    q2, k2, v2 = (w["L2_attn_w_qkv"][:, n * D:(n + 1) * D] for n in range(3))
    bq2, bk2, bv2 = (w["L2_attn_b_qkv"][n * D:(n + 1) * D] for n in range(3))
    a["A2_wq"], a["A2_wk"], a["A2_wv"] = banded(q2), banded(k2), v2
    a["A2_bq"], a["A2_bk"], a["A2_bv"] = banded(bq2.reshape(1, D))[0].T, banded(bk2.reshape(1, D), 1.0)[0].T, rows(bv2)
    a["A2_wo"], a["A2_bo"] = w["L2_attn_w_out"], rows(w["L2_attn_b_out"])
    a["A2_gamma"], a["A2_beta"] = w["L2_attn_ln_gamma"].reshape(D, 1), w["L2_attn_ln_beta"].reshape(D, 1)
    q3, k3, v3 = (w["L3_attn_Wqkv"][:, n * D:(n + 1) * D] for n in range(3))
    a["A3_wq"], a["A3_wk"], a["A3_wv"] = banded(q3), banded(k3), v3
    a["A3_wq_swap"], a["A3_wk_swap"] = banded(q3[:, pairs]), banded(k3[:, pairs])
    a["A3_wo"], a["A3_bo"] = w["L3_attn_Wout"], rows(w["L3_attn_bout"])
    theta = np.power(np.float32(10000.0), (-2.0 * (np.arange(DK // 2, dtype=np.float32) - 1.0) / DK).astype(np.float32))
    angle = (np.arange(SEQ, dtype=np.float32)[:, None] * theta.astype(np.float32)[None, :]).astype(np.float64)
    sign = np.tile([-1.0, 1.0], DK // 2)
    tables = [np.repeat(np.cos(angle), 2, axis=1), np.repeat(np.sin(angle), 2, axis=1) * sign]
    a["A3_rope"] = np.stack([banded(np.tile(t, HEADS).astype(np.float32))[:, 0].T for t in tables], axis=1)


def rwkv_layout(w, a):
    column = lambda v: v.reshape(D, 1)
    a["RW_miu_x"], a["RW_td_miu"], a["RW_u"] = (column(w["L1_attn_" + n]) for n in ("miu_x", "td_miu", "u"))
    a["RW_gamma"], a["RW_beta"] = column(w["L1_attn_gn_gamma"]), column(w["L1_attn_gn_beta"])
    a["RW_lambda"] = w["L1_attn_lambda_"].reshape(MIXES, D).T
    a["RW_A"], a["RW_B"] = w["L1_attn_A_lora"], w["L1_attn_B_lora"].transpose(1, 0, 2)
    a["RW_td_A"], a["RW_td_B"] = w["L1_attn_td_A"], w["L1_attn_td_B"]
    for n in "rkvgo":
        a["RW_w" + n] = w["L1_attn_W" + n].T
    head = np.arange(P) // HS
    a["RW_head_ones"] = (head[:, None] == head[None, :]).astype(np.float32)
    gather = np.zeros((P, P + HS - 1), np.float32)
    gather[np.arange(P), head * HS + HS - 1] = 1.0
    a["RW_gather"] = gather


def stack_layout(w, a):
    t = {n: w["L2_ffn_" + n] for n in ("Wqkv", "q_scale", "k_scale", "Wo", "ln_g", "ln_b", "W1", "b1", "W2", "b2")}
    depth = t["Wqkv"].shape[0]
    a["T_wqkv"] = t["Wqkv"]
    a["T_wo"] = t["Wo"].reshape(depth, LPAIRS, P, D).transpose(0, 2, 1, 3)
    a["T_w1"] = t["W1"]
    w2 = np.zeros((depth, FF_CHUNKS * P, D), np.float32)
    w2[:, :FF] = t["W2"]
    a["T_w2"] = w2.reshape(depth, FF_CHUNKS, P, D).transpose(0, 2, 1, 3)
    b1 = np.zeros((depth, 2, FF_CHUNKS * P), np.float32)
    b1[:, :, :FF] = t["b1"].reshape(depth, 2, FF)
    b1 = b1.reshape(depth, 2 * FF_CHUNKS, P).transpose(0, 2, 1)
    a["T_cols"] = np.concatenate([b1, t["ln_g"][:, :, None], t["ln_b"][:, :, None]], axis=2)
    a["T_b2"] = np.broadcast_to(t["b2"][:, None, None, :], (depth, P, 1, D))
    swap = lambda v: np.roll(v, LD // 2, axis=-1)
    scales = np.stack([t["q_scale"], swap(t["q_scale"]), t["k_scale"], swap(t["k_scale"])], axis=1)
    a["T_rows"] = np.broadcast_to(scales[:, None, :, None, :], (depth, P, 4, 1, LD))
    half = np.arange(0, LD, 2, dtype=np.float32)
    inv_freq = (1.0 / np.power(np.float32(10000.0), half / LD)).astype(np.float32)
    n = np.arange(SEQ, dtype=np.float32)
    freqs = (n[:, None] * inv_freq[None, :]).astype(np.float64)
    factor = ((half + 0.4 * LD) / (1.4 * LD)).astype(np.float64)[None, :] ** ((n - SEQ // 2) / (WINDOW // 2))[:, None]
    cos, sin, factor = (np.concatenate([v, v], axis=1) for v in (np.cos(freqs), np.sin(freqs), factor))
    sin = sin * np.where(np.arange(LD) < LD // 2, -1.0, 1.0)
    base = np.stack([8 * cos * factor, 8 * sin * factor, cos / factor, sin / factor])
    a["T_base"] = base.astype(np.float32).reshape(4, HALVES, P, LD).transpose(2, 0, 1, 3)
    q = np.arange(P)[:, None, None]
    key = np.arange(REACH)[None, None, :] - WINDOW
    seen = (key <= q) & (key >= q - WINDOW) & ((np.arange(HALVES)[None, :, None] > 0) | (key >= 0))
    a["T_band"] = np.where(seen, 0.0, MASKED).astype(mybir.dt.np(BF16))
```

```python
from contextlib import ExitStack

import numpy as np
import concourse.bass as bass
from concourse import mybir

ALU = mybir.AluOpType
ACT = mybir.ActivationFunctionType
AX = mybir.AxisListType
F32 = mybir.dt.float32
BF16 = mybir.dt.bfloat16
U32 = mybir.dt.uint32

P = 128
D = 128
B, SEQ = 8, 256
TILES = B * SEQ // P
HALVES = SEQ // P
HEADS, DK = 16, 8
EPS = 1e-5
MASKED = -1e30


class Signals:

    def __init__(self, nc, ctx, stage, seeded=False, **per):
        names = list(per) + ["apart"] * ("apart" not in per)
        self.sems = {name: ctx.enter_context(nc.semaphore(stage + "_" + name)) for name in names}
        self.per = per
        self.base = {name: int(seeded) for name in per}

    def __getitem__(self, name):
        return self.sems[name]

    def __call__(self, name, step, k=0):
        return self.sems[name], step * self.per[name] + (self.base[name] + k)

    def use(self, per):
        assert set(per) <= set(self.sems)
        self.per = per

    def seed(self, eng):
        for sem in self.sems.values():
            eng.sem_inc(sem, 1)

    def apart(self, eng, name, step, k):
        eng.wait_ge(*self(name, step, k))
        self.settle(eng)

    def settle(self, eng):
        eng.sem_inc(self.sems["apart"], 1)

    def ended(self, steps, names=None):
        for name in names or self.per:
            self.base[name] += self.per[name] * steps


class Chain:

    def __init__(self, eng, signals, name, step):
        self.eng, self.signals, self.name, self.step, self.n = eng, signals, name, step, 0

    def __call__(self, ins):
        ins.then_inc(self.signals[self.name], 1)
        self.n += 1
        self.eng.wait_ge(*self.signals(self.name, self.step, self.n))

    def apart(self, ins):
        ins.then_inc(self.signals[self.name], 1)
        self.n += 1
        self.signals.apart(self.eng, self.name, self.step, self.n)

    def done(self):
        assert self.n == self.signals.per[self.name], (self.name, self.n)


class Chip:

    def __init__(self, nc, ctx, dram, loop_names):
        self.nc, self.ctx, self.dram = nc, ctx, dram
        self.tag = ""
        self.loop = Signals(nc, ctx, "loop", seeded=True, **dict.fromkeys(loop_names, 0))
        self.ffn = Signals(nc, ctx, "ffn", seeded=True, **STACK_FFN)
        self.once = Signals(nc, ctx, "once", **dict.fromkeys(["loaded", "set", "reduced", "chain"] + [f"experts{n}" for n in range(LOADS)], 0))
        self.layer = Signals(nc, ctx, "layer", **STACK_LAYER)
        self.x = ctx.enter_context(nc.sbuf_tensor("x_all", [P, TILES, D], F32))
        self.ident = ctx.enter_context(nc.sbuf_tensor("ident", [P, P], F32))
        self.minus_half = ctx.enter_context(nc.sbuf_tensor("minus_half", [P, 1], F32))


NORM_SIGNALS = dict(norm_chain=1, moments=1, var=1, rstd=1, xn=1, xT_psum=1, xT=1)


class Norm:
    def __init__(self, chip, ctx, tiles, turned=True):
        self.tiles = tiles
        sb = lambda name, shape: ctx.enter_context(chip.nc.sbuf_tensor(chip.tag + "norm_" + name, shape, F32))
        self.stats = sb("stats", [P, tiles, 6])
        self.moments = sb("moments", [P, tiles, 2])
        self.var = sb("var", [P, tiles])
        self.rstd = sb("rstd", [P, tiles])
        if not turned:
            return
        self.xn = sb("xn", [P, tiles, D])
        self.xT = sb("xT", [P, tiles * P])
        self.psum = ctx.enter_context(chip.nc.psum_tensor(chip.tag + "norm_psum", [P, 512], F32))


def norm_vector(nc, dve, sig, m, step, source, target, used, which=""):
    T = m.tiles
    for t in range(T):
        ins = nc.vector.bn_stats(m.stats[:, t, :], source(t))
    ins.then_inc(sig["norm_chain" + which], 1)
    sig.apart(dve, "norm_chain" + which, step, 1)
    for t in range(T):
        ins = nc.vector.bn_aggr(m.moments[:, t, :], m.stats[:, t, :])
    ins.then_inc(sig["moments" + which], 1)
    dve.wait_ge(*sig("moments" + which, step, 1))
    nc.vector.tensor_scalar(m.var[:, :], m.moments[:, :, 1], EPS, None, ALU.add).then_inc(sig["var" + which], 1)
    dve.wait_ge(*sig("rstd" + which, step, 1))
    for name in used:
        dve.wait_ge(*sig(name, step))
    for t in range(T):
        ins = nc.vector.tensor_scalar(target(t), source(t), m.moments[:, t, 0:1], m.rstd[:, t:t + 1],
                                      ALU.subtract, ALU.mult)
    ins.then_inc(sig["xn" + which], 1)


def norm_rstd(nc, pool, sig, chip, m, step, which=""):
    pool.wait_ge(*sig("var" + which, step, 1))
    nc.gpsimd.tensor_tensor(m.rstd[:, :], m.var[:, :], chip.minus_half[:, :].to_broadcast([P, m.tiles]), ALU.pow)\
      .then_inc(sig["rstd" + which], 1)


def norm_transpose(nc, pe, sig, chip, m, step):
    pe.wait_ge(*sig("xn", step, 1))
    pe.wait_ge(*sig("xT", step))
    for t in range(m.tiles):
        ins = nc.tensor.transpose(m.psum[:, t * P:(t + 1) * P], m.xn[:, t, :], chip.ident[:, :])
    ins.then_inc(sig["xT_psum"], 1)


def norm_xT(nc, act, sig, m, step, xT_used):
    act.wait_ge(*sig("xT_psum", step, 1))
    for name in xT_used:
        act.wait_ge(*sig(name, step))
    nc.scalar.activation(m.xT[:, :], m.psum[:, 0:m.tiles * P], ACT.Copy).then_inc(sig["xT"], 1)


def x_tile(chip, step, tiles):
    return lambda t: chip.x[:, bass.ds(step * tiles + t, 1), :].rearrange("p a d -> p (a d)")


TWO_PI = 2 * np.pi
TWO_PI_1 = 6.28125
TWO_PI_2 = float(np.float32(np.round((TWO_PI - TWO_PI_1) * 2 ** 20) / 2 ** 20))
TWO_PI_3 = TWO_PI - TWO_PI_1 - TWO_PI_2
ROUNDER = 1.5 * 2 ** 23
PI_BELOW = 3.1415925


def setup_l1_angles(chip, cossin):
    nc = chip.nc
    with ExitStack() as ctx:
        sb = lambda name, shape: ctx.enter_context(nc.sbuf_tensor("angle_" + name, shape, F32))
        parts, angle, turns = sb("parts", [P, 4, D]), sb("sum", [P, 2, D]), sb("turns", [P, 2, D])
        sig = chip.once
        sig.use(dict(loaded=64, chain=10, reduced=1, set=1))
        block = ctx.enter_context(nc.Block())

        @block.sync
        def _(sp):
            for n, name in enumerate(["L1_ffn_theta", "L1_ffn_phi", "L1_ffn_theta_noise", "L1_ffn_phi_noise"]):
                sp.dma_start(parts[:, n, :], chip.dram[name]).then_inc(sig["loaded"], 16)

        @block.vector
        def _(dve):
            chain = Chain(dve, sig, "chain", 0)
            dve.wait_ge(*sig("loaded", 1))
            chain(nc.vector.tensor_tensor(angle[:, :, :], parts[:, 0:2, :], parts[:, 2:4, :], ALU.add))
            chain(nc.vector.tensor_scalar(turns[:, 0, :], angle[:, 0, :], 1 / TWO_PI, 0.25, ALU.mult, ALU.add))
            chain(nc.vector.tensor_scalar(turns[:, 1, :], angle[:, 1, :], 1 / TWO_PI, None, ALU.mult))
            chain(nc.vector.tensor_scalar(turns[:, :, :], turns[:, :, :], ROUNDER, None, ALU.add))
            chain(nc.vector.tensor_scalar(turns[:, :, :], turns[:, :, :], ROUNDER, None, ALU.subtract))
            for part in (TWO_PI_1, TWO_PI_2, TWO_PI_3):
                chain(nc.vector.scalar_tensor_tensor(angle[:, :, :], turns[:, :, :], -part, angle[:, :, :], ALU.mult, ALU.add))
            chain(nc.vector.tensor_scalar(angle[:, 0, :], angle[:, 0, :], np.pi / 2, None, ALU.add))
            chain(nc.vector.tensor_scalar(angle[:, :, :], angle[:, :, :], PI_BELOW, -PI_BELOW, ALU.min, ALU.max))
            chain.done()
            nc.vector.engine_nop().then_inc(sig["reduced"], 1)

        @block.scalar
        def _(act):
            act.wait_ge(*sig("reduced", 1))
            nc.scalar.activation(cossin[:, :, :], angle[:, :, :], ACT.Sin).then_inc(sig["set"], 1)
            act.wait_ge(*sig("set", 1))
    sig.ended(1)


def stage_l1_ffn(chip, cossin):
    nc, sig = chip.nc, chip.loop
    sig.use(L1_FFN_SIGNALS)
    T = 4
    with ExitStack() as ctx:
        m = Norm(chip, ctx, T)
        squares = ctx.enter_context(nc.sbuf_tensor(chip.tag + "squares", [P, T, 2, D], F32))
        norm2 = ctx.enter_context(nc.sbuf_tensor(chip.tag + "norm2", [P, T, D], F32))
        waves = ctx.enter_context(nc.psum_tensor(chip.tag + "waves", [P, T, 2, D], F32))
        block = ctx.enter_context(nc.Block())
        steps = TILES // T

        @block.vector
        def _(dve):
            with dve.Fori(0, steps) as step:
                norm_vector(nc, dve, sig, m, step, x_tile(chip, step, T), lambda t: m.xn[:, t, :], ["xT_psum"])
                dve.wait_ge(*sig("squares", step, 1))
                nc.vector.tensor_tensor(norm2[:, :, :], squares[:, :, 0, :], squares[:, :, 1, :], ALU.add)\
                  .then_inc(sig["norm2"], 1)
                dve.wait_ge(*sig("root", step, 1))
                x = chip.x[:, bass.ds(step * T, T), :]
                nc.vector.scalar_tensor_tensor(x, norm2[:, :, :], 0.5, x, ALU.mult, ALU.add).then_inc(sig["x"], 1)
                dve.wait_ge(*sig("x", step, 1))

        @block.scalar
        def _(act):
            with act.Fori(0, steps) as step:
                norm_xT(nc, act, sig, m, step, ["waves"])
                act.wait_ge(*sig("waves", step, 1))
                act.wait_ge(*sig("norm2", step))
                nc.scalar.activation(squares[:, :, :, :], waves[:, :, :, :], ACT.Square).then_inc(sig["squares"], 1)
                act.wait_ge(*sig("norm2", step, 1))
                nc.scalar.activation(norm2[:, :, :], norm2[:, :, :], ACT.Sqrt).then_inc(sig["root"], 1)

        @block.gpsimd
        def _(pool):
            with pool.Fori(0, steps) as step:
                norm_rstd(nc, pool, sig, chip, m, step)

        @block.tensor
        def _(pe):
            with pe.Fori(0, steps) as step:
                norm_transpose(nc, pe, sig, chip, m, step)
                pe.wait_ge(*sig("xT", step, 1))
                pe.wait_ge(*sig("squares", step))
                for t in range(T):
                    ins = nc.tensor.matmul(waves[:, t, :, :], m.xT[:, t * P:(t + 1) * P], cossin[:, :, :],
                                           start=True, stop=True)
                ins.then_inc(sig["waves"], 1)
    sig.ended(steps)


L1_FFN_SIGNALS = dict(NORM_SIGNALS, waves=1, squares=1, norm2=1, root=1, x=1)


EXPERTS = 8
TOKEN_TILES = 4
LOADS = 4


def moe_signals(gated, chunks):
    per = dict(NORM_SIGNALS, logits=1, routed=1, top=1, gap=1, exp_gap=1, h_psum=EXPERTS * chunks,
               hidden=EXPERTS * chunks, o_psum=EXPERTS, mixed=EXPERTS, x=1 if gated else 2, route_chain=10)
    if gated:
        per.update(silu=EXPERTS * chunks)
    else:
        per.update(rwT_psum=1, rwT=1, bias_psum=1, moments2=1, var2=1, rstd2=1, out_chain=5, )
    return per


def stage_moe(chip, level):
    nc, T = chip.nc, TOKEN_TILES
    sig, loaded = chip.loop, chip.once
    gated = level == 3
    F = 256 if gated else 512
    chunks, width = F // P, T * P
    banks = 2
    steps = TILES // T
    dram = chip.dram
    sig.use(moe_signals(gated, chunks))
    loaded.use(moe_loads(level))
    with ExitStack() as ctx:
        sb = lambda name, shape, dt=F32: ctx.enter_context(nc.sbuf_tensor(chip.tag + name, shape, dt))
        ps = lambda name, shape: ctx.enter_context(nc.psum_tensor(chip.tag + name, shape, F32))
        m = Norm(chip, ctx, T)
        w_up = sb("w_up", [P, EXPERTS, F])
        w_up2 = sb("w_up2", [P, EXPERTS, F]) if gated else None
        w_down = sb("w_down", [P, EXPERTS, chunks, D])
        w_gate = sb("w_gate", [P, EXPERTS])
        iota = sb("iota", [P, EXPERTS])
        if not gated:
            b_gate, b_up, b_down = sb("b_gate", [P, EXPERTS]), sb("b_up", [P, EXPERTS, chunks]), sb("b_down", [EXPERTS, D])
            gamma, beta = sb("gamma", [P, D]), sb("beta", [P, D])
            rwT = sb("rwT", [EXPERTS, width])
            stats2, moments2, var2, rstd2 = sb("stats2", [P, T, 6]), sb("moments2", [P, T, 2]), sb("var2", [P, T]), sb("rstd2", [P, T])
        hidden = sb("hidden", [P, 2, chunks, width])
        silu = sb("silu", [P, 2, width]) if gated else None
        logits, top = sb("logits", [P, T, EXPERTS]), sb("top", [P, T, 8])
        index, indexf = sb("index", [P, T, 8], U32), sb("indexf", [P, T, 8])
        gap, weights = sb("gap", [P, T, 1]), sb("weights", [P, T, 2])
        pick, route = sb("pick", [P, T, EXPERTS]), sb("route", [P, T, EXPERTS])
        mix = sb("mix", [P, T, D])
        logits_psum = ps("logits_psum", [P, 512])
        h_psum = [ps(f"h_psum{n}", [P, width]) for n in range(banks)]
        h2_psum = [ps(f"h2_psum{n}", [P, width]) for n in range(banks)] if gated else None
        o_psum = [ps(f"o_psum{n}", [P, T, D]) for n in range(2)]
        lg = logits_psum[:, 0:T * EXPERTS].rearrange("p (t e) -> p t e", t=T)
        x_of = lambda step: chip.x[:, bass.ds(step * T, T), :]
        block = ctx.enter_context(nc.Block())

        @block.sync
        def _(sp):
            names = [("w_gate", w_gate), ("iota", iota)]
            if not gated:
                names += [("b_gate", b_gate), ("b_up", b_up), ("b_down", b_down), ("gamma", gamma), ("beta", beta)]
            for name, tile in names:
                src = dram["iota"] if name == "iota" else dram[f"L{level}_{name}"]
                sp.dma_start(tile[:], src).then_inc(loaded["loaded"], 16)
            for n in range(LOADS):
                e = slice(n * EXPERTS // LOADS, (n + 1) * EXPERTS // LOADS)
                sp.dma_start(w_up[:, e, :], dram[f"L{level}_w_up"][:, e, :]).then_inc(loaded[f"experts{n}"], 16)
                if gated:
                    sp.dma_start(w_up2[:, e, :], dram[f"L{level}_w_up2"][:, e, :]).then_inc(loaded[f"experts{n}"], 16)
                sp.dma_start(w_down[:, e, :, :], dram[f"L{level}_w_down"][:, e, :, :]).then_inc(loaded[f"experts{n}"], 16)

        @block.tensor
        def _(pe):
            pe.wait_ge(*loaded("loaded", 1))
            with pe.Fori(0, steps) as step:
                if not gated:
                    pe.wait_ge(*sig("rwT", step))
                norm_transpose(nc, pe, sig, chip, m, step)
                pe.wait_ge(*sig("xT", step, 1))
                pe.wait_ge(*sig("top", step))
                for t in range(T):
                    ins = nc.tensor.matmul(lg[:, t, :], m.xT[:, t * P:(t + 1) * P], w_gate[:, :], start=True, stop=True)
                ins.then_inc(sig["logits"], 1)

                def down(e):
                    pe.wait_ge(*sig("hidden", step, (e + 1) * chunks))
                    pe.wait_ge(*sig("mixed", step, max(e - 1, 0)))
                    for t in range(T):
                        for c in range(chunks):
                            ins = nc.tensor.matmul(o_psum[e % 2][:, t, :], hidden[:, e % 2, c, t * P:(t + 1) * P],
                                                   w_down[:, e, c, :], start=c == 0, stop=c == chunks - 1)
                    ins.then_inc(sig["o_psum"], 1)

                for e in range(EXPERTS):
                    pe.wait_ge(*loaded(f"experts{e * LOADS // EXPERTS}", 1))
                    for c in range(chunks):
                        n = e * chunks + c
                        pe.wait_ge(*sig("hidden", step, max(n - banks + 1, 0)))
                        ins = nc.tensor.matmul(h_psum[n % banks][:, :], w_up[:, e, c * P:(c + 1) * P], m.xT[:, :],
                                               start=True, stop=True)
                        if gated:
                            ins = nc.tensor.matmul(h2_psum[n % banks][:, :], w_up2[:, e, c * P:(c + 1) * P], m.xT[:, :],
                                                   start=True, stop=True)
                        ins.then_inc(sig["h_psum"], 1)
                    if e:
                        down(e - 1)
                down(EXPERTS - 1)
                if not gated:
                    pe.wait_ge(*sig("routed", step, 1))
                    for t in range(T):
                        ins = nc.tensor.transpose(m.psum[0:EXPERTS, t * P:(t + 1) * P], route[:, t, :], chip.ident[:, :])
                    ins.then_inc(sig["rwT_psum"], 1)
                    pe.wait_ge(*sig("rwT", step, 1))
                    pe.wait_ge(*sig("mixed", step, EXPERTS - 1))
                    for t in range(T):
                        ins = nc.tensor.matmul(o_psum[0][:, t, :], rwT[:, t * P:(t + 1) * P], b_down[:, :], start=True, stop=True)
                    ins.then_inc(sig["bias_psum"], 1)

        @block.scalar
        def _(act):
            act.wait_ge(*loaded("loaded", 1))
            with act.Fori(0, steps) as step:
                norm_xT(nc, act, sig, m, step, ["h_psum", "logits"])
                act.wait_ge(*sig("gap", step, 1))
                nc.scalar.activation(weights[:, :, 1:2], gap[:, :, :], ACT.Exp).then_inc(sig["exp_gap"], 1)
                for e in range(EXPERTS):
                    if not gated:
                        act.wait_ge(*sig("o_psum", step, max(e - 1, 0)))
                    for c in range(chunks):
                        n = e * chunks + c
                        act.wait_ge(*sig("h_psum", step, n + 1))
                        if gated:
                            act.wait_ge(*sig("hidden", step, max(n - 1, 0)))
                            nc.scalar.activation(silu[:, n % 2, :], h_psum[n % banks][:, :], ACT.Silu)\
                              .then_inc(sig["silu"], 1)
                        else:
                            nc.scalar.activation(hidden[:, e % 2, c, :], h_psum[n % banks][:, :], ACT.Relu,
                                                 bias=b_up[:, e, c:c + 1]).then_inc(sig["hidden"], 1)
                if not gated:
                    act.wait_ge(*sig("rwT_psum", step, 1))
                    act.wait_ge(*sig("bias_psum", step))
                    nc.scalar.activation(rwT[:, :], m.psum[0:EXPERTS, :], ACT.Copy).then_inc(sig["rwT"], 1)

        @block.gpsimd
        def _(pool):
            with pool.Fori(0, steps) as step:
                norm_rstd(nc, pool, sig, chip, m, step)
                if not gated:
                    pool.wait_ge(*sig("var2", step, 1))
                    nc.gpsimd.tensor_tensor(rstd2[:, :], var2[:, :], chip.minus_half[:, :].to_broadcast([P, T]), ALU.pow)\
                      .then_inc(sig["rstd2"], 1)

        @block.vector
        def _(dve):
            dve.wait_ge(*loaded("loaded", 1))
            with dve.Fori(0, steps) as step:
                norm_vector(nc, dve, sig, m, step, x_tile(chip, step, T), lambda t: m.xn[:, t, :], ["xT_psum"])
                chain = Chain(dve, sig, "route_chain", step)
                dve.wait_ge(*sig("logits", step, 1))
                if gated:
                    ins = nc.vector.tensor_copy(logits[:, :, :], lg)
                else:
                    ins = nc.vector.tensor_tensor(logits[:, :, :], lg, b_gate[:, :].rearrange("p (a e) -> p a e", a=1).to_broadcast([P, T, EXPERTS]), ALU.add)
                ins.then_inc(sig["top"], 1)
                sig.apart(dve, "top", step, 1)
                for t in range(T):
                    ins = nc.vector.max(top[:, t, :], logits[:, t, :])
                chain.apart(ins)
                for t in range(T):
                    ins = nc.vector.max_index(index[:, t, :], top[:, t, :], logits[:, t, :])
                chain(ins)
                nc.vector.tensor_tensor(gap[:, :, :], top[:, :, 1:2], top[:, :, 0:1], ALU.subtract).then_inc(sig["gap"], 1)
                chain(nc.vector.tensor_copy(indexf[:, :, :], index[:, :, :]))
                dve.wait_ge(*sig("exp_gap", step, 1))
                chain(nc.vector.tensor_scalar(weights[:, :, 0:1], weights[:, :, 1:2], 1.0, None, ALU.add))
                chain(nc.vector.reciprocal(weights[:, :, 0:1], weights[:, :, 0:1]))
                chain(nc.vector.tensor_tensor(weights[:, :, 1:2], weights[:, :, 1:2], weights[:, :, 0:1], ALU.mult))
                every = [P, T, EXPERTS]
                ids = iota[:, :].rearrange("p (a e) -> p a e", a=1).to_broadcast(every)
                chain(nc.vector.tensor_tensor(route[:, :, :], ids, indexf[:, :, 0:1].to_broadcast(every), ALU.is_equal))
                chain(nc.vector.tensor_tensor(pick[:, :, :], ids, indexf[:, :, 1:2].to_broadcast(every), ALU.is_equal))
                chain(nc.vector.tensor_tensor(route[:, :, :], route[:, :, :], weights[:, :, 0:1].to_broadcast(every), ALU.mult))
                chain(nc.vector.tensor_tensor(pick[:, :, :], pick[:, :, :], weights[:, :, 1:2].to_broadcast(every), ALU.mult))
                nc.vector.tensor_tensor(route[:, :, :], route[:, :, :], pick[:, :, :], ALU.add).then_inc(sig["routed"], 1)
                dve.wait_ge(*sig("routed", step, 1))

                def mix_in(e):
                    dve.wait_ge(*sig("o_psum", step, e + 1))
                    if e:
                        dve.wait_ge(*sig("mixed", step, e))
                    for t in range(T):
                        if e == 0:
                            ins = nc.vector.tensor_scalar(mix[:, t, :], o_psum[0][:, t, :], route[:, t, e:e + 1], None, ALU.mult)
                        else:
                            ins = nc.vector.scalar_tensor_tensor(mix[:, t, :], o_psum[e % 2][:, t, :], route[:, t, e:e + 1],
                                                                 mix[:, t, :], ALU.mult, ALU.add)
                    ins.then_inc(sig["mixed"], 1)

                for e in range(EXPERTS):
                    if gated:
                        dve.wait_ge(*sig("o_psum", step, max(e - 1, 0)))
                        for c in range(chunks):
                            n = e * chunks + c
                            dve.wait_ge(*sig("silu", step, n + 1))
                            nc.vector.tensor_tensor(hidden[:, e % 2, c, :], silu[:, n % 2, :], h2_psum[n % banks][:, :],
                                                    ALU.mult).then_inc(sig["hidden"], 1)
                        if e:
                            mix_in(e - 1)
                    else:
                        mix_in(e)
                if gated:
                    mix_in(EXPERTS - 1)
                    dve.wait_ge(*sig("mixed", step, EXPERTS))
                    nc.vector.scalar_tensor_tensor(x_of(step), mix[:, :, :], 0.5, x_of(step), ALU.mult, ALU.add).then_inc(sig["x"], 1)
                else:
                    out = Chain(dve, sig, "out_chain", step)
                    row = [P, T, D]
                    dve.wait_ge(*sig("mixed", step, EXPERTS))
                    dve.wait_ge(*sig("bias_psum", step, 1))
                    out(nc.vector.tensor_tensor(mix[:, :, :], mix[:, :, :], o_psum[0][:, :, :], ALU.add))
                    out(nc.vector.tensor_tensor(mix[:, :, :], mix[:, :, :], m.xn[:, :, :], ALU.add))
                    for t in range(T):
                        ins = nc.vector.bn_stats(stats2[:, t, :], mix[:, t, :])
                    out.apart(ins)
                    for t in range(T):
                        ins = nc.vector.bn_aggr(moments2[:, t, :], stats2[:, t, :])
                    ins.then_inc(sig["moments2"], 1)
                    dve.wait_ge(*sig("moments2", step, 1))
                    nc.vector.tensor_scalar(var2[:, :], moments2[:, :, 1], EPS, None, ALU.add).then_inc(sig["var2"], 1)
                    dve.wait_ge(*sig("rstd2", step, 1))
                    for t in range(T):
                        ins = nc.vector.tensor_scalar(mix[:, t, :], mix[:, t, :], moments2[:, t, 0:1], rstd2[:, t:t + 1],
                                                      ALU.subtract, ALU.mult)
                    out(ins)
                    out(nc.vector.tensor_tensor(mix[:, :, :], mix[:, :, :], gamma[:, :].rearrange("p (a d) -> p a d", a=1).to_broadcast(row), ALU.mult))
                    nc.vector.tensor_tensor(mix[:, :, :], mix[:, :, :], beta[:, :].rearrange("p (a d) -> p a d", a=1).to_broadcast(row), ALU.add)\
                      .then_inc(sig["x"], 1)
                    dve.wait_ge(*sig("x", step, 1))
                    nc.vector.scalar_tensor_tensor(x_of(step), mix[:, :, :], 0.5, x_of(step), ALU.mult, ALU.add).then_inc(sig["x"], 1)
                    out.done()
                dve.wait_ge(*sig("x", step, 1 if gated else 2))
                chain.done()
    sig.ended(steps)
    loaded.ended(1)


def moe_loads(level):
    small = 2 if level == 3 else 7
    return dict(loaded=16 * small, **{f"experts{n}": 16 * (3 if level == 3 else 2) for n in range(LOADS)})


GROUPS, BAND = 4, 32
AUG = DK + 1
PAIRS = HEADS // 2
ATTN_LOADS = {0: 11, 2: 13, 3: 11}


def attention_signals(level):
    per = dict(NORM_SIGNALS, proj=GROUPS, proj_read=GROUPS, v_psum=1, v=1, probs=PAIRS,
               ctx_psum=1, context=1, ctxT_psum=1, ctxT=1, out_psum=1, x=2, ctx_chain=1)
    if level == 3:
        per.update(rope=GROUPS, rope_chain=2 * GROUPS, den_scores=PAIRS, den_probs=PAIRS, scores=PAIRS)
    else:
        per.update(scores=PAIRS, max_scores=PAIRS, negmax=PAIRS, negmaxT=2, q_aug=2)
    if level == 2:
        per.update(norm_chain_a=1, moments_a=1, var_a=1, rstd_a=1, xn_a=1, residual=1)
    return per


def stage_attention(chip, level):
    nc, sig, once = chip.nc, chip.loop, chip.once
    causal, softmax = level != 2, level != 3
    scale = float(DK) ** -0.5
    dram = chip.dram
    T = HALVES
    sig.use(attention_signals(level))
    once.use(dict(loaded=16 * ATTN_LOADS[level], set=2 if softmax else 1))
    with ExitStack() as ctx:
        sb = lambda name, shape, dt=F32: ctx.enter_context(nc.sbuf_tensor(chip.tag + name, shape, dt))
        ps = lambda name, shape: ctx.enter_context(nc.psum_tensor(chip.tag + name, shape, F32))
        m = Norm(chip, ctx, T)
        tiles = {"wq": sb("wq", [P, GROUPS, P]), "wk": sb("wk", [P, GROUPS, P]), "wv": sb("wv", [P, D]), "wo": sb("wo", [P, D]),
                 "bo": sb("bo", [P, D]), "ident_bf": sb("ident_bf", [P, P], BF16), "mask": sb("mask", [P, P], BF16),
                 "maskT": sb("maskT", [P, P], BF16)}
        if softmax:
            tiles.update(bq=sb("bq", [P, GROUPS]), bk=sb("bk", [P, GROUPS]), bv=sb("bv", [P, D]))
        else:
            tiles.update(wq_swap=sb("wq_swap", [P, GROUPS, P]), wk_swap=sb("wk_swap", [P, GROUPS, P]),
                         rope=sb("rope", [P, 2, SEQ]))
        if level == 2:
            tiles.update(gamma=sb("gamma", [P, 1]), beta=sb("beta", [P, 1]))
            x1 = sb("x1", [P, T, D])
        assert len(tiles) == ATTN_LOADS[level]
        wq, wk, wv, wo, bo, ident_bf, mask, maskT = (tiles[n] for n in ("wq", "wk", "wv", "wo", "bo", "ident_bf", "mask", "maskT"))
        qk = sb("qk", [P, 2, GROUPS, SEQ])
        turned = None if softmax else sb("turned", [P, 2, GROUPS, SEQ])
        turn = None if softmax else sb("turn", [P, 2, 2, SEQ])
        v = sb("v", [P, T, HEADS, AUG])
        negmax = sb("negmax", [P, T, GROUPS, P]) if softmax else None
        probs = sb("probs", [P, T, HEADS, SEQ])
        den_probs = None if softmax else sb("den_probs", [P, T, HEADS, SEQ])
        rden, context, ctxT = sb("rden", [P, T, HEADS, 1]), sb("context", [P, T, D]), sb("ctxT", [P, SEQ])
        scores = ps("scores", [P, GROUPS, T, SEQ])
        pv = ps("pv", [P, T, HEADS, AUG])
        vo = ps("vo", [P, T, D])
        banks = lambda n: slice(2 * (n % 2), 2 * (n % 2) + 2)
        of_pair = lambda tile, n: tile[:, :, 2 * n:2 * n + 2, :].rearrange("p t h s -> p h t s")
        block = ctx.enter_context(nc.Block())

        @block.sync
        def _(sp):
            for name, tile in tiles.items():
                src = dram[name] if name in ("ident_bf", "mask", "maskT") else dram[f"A{level}_{name}"]
                sp.dma_start(tile[:], src).then_inc(once["loaded"], 16)

        @block.tensor
        def _(pe):
            pe.wait_ge(*once("loaded", 1))
            pe.wait_ge(*once("set", 1))
            with pe.Fori(0, B) as step:
                pe.wait_ge(*sig("ctxT", step))
                norm_transpose(nc, pe, sig, chip, m, step)
                pe.wait_ge(*sig("xT", step, 1))
                pe.wait_ge(*sig("x", step))
                for t in range(T):
                    ins = nc.tensor.matmul(vo[:, t, :], m.xT[:, t * P:(t + 1) * P], wv[:, :], start=True, stop=True)
                ins.then_inc(sig["v_psum"], 1)
                pe.wait_ge(*sig("probs", step))
                for g in range(GROUPS):
                    pe.wait_ge(*sig("proj_read", step, max(g - 1, 0)))
                    if not softmax:
                        pe.wait_ge(*sig("rope", step, max(g - 1, 0)))
                    projections = [wq, wk] if softmax else [wq, wk, tiles["wq_swap"], tiles["wk_swap"]]
                    for n, w in enumerate(projections):
                        ins = nc.tensor.matmul(scores[:, 2 * (g % 2) + n // 2, n % 2, :], w[:, g, :], m.xT[:, :],
                                               start=True, stop=True)
                    ins.then_inc(sig["proj"], 1)

                def score(n, stationary, moving, rows_of, mask_of):
                    g = n // 2
                    for j in (2 * (n % 2), 2 * (n % 2) + 1):
                        rows = slice(BAND * j, BAND * j + rows_of)
                        for t in range(T):
                            first, end = span(t, mask_of)
                            ins = nc.tensor.matmul(scores[:, j, t, first:end], stationary[rows, g, t * P:(t + 1) * P],
                                                   moving[rows, g, first:end], start=True, stop=mask_of is None,
                                                   skip_group_check=True)
                            if mask_of is not None:
                                ins = nc.tensor.matmul(scores[:, j, t, t * P:(t + 1) * P], ident_bf[:, :], mask_of[:, :],
                                                       start=False, stop=True, skip_group_check=True)
                    return ins

                def span(t, mask_of):
                    if mask_of is None:
                        return 0, SEQ
                    return (0, (t + 1) * P) if mask_of is mask else (t * P, SEQ)

                q_rows, k_rows = qk[:, 0], qk[:, 1]
                pe.wait_ge(*sig("proj_read", step, GROUPS))
                if softmax:
                    for n in range(PAIRS):
                        pe.wait_ge(*sig("negmax", step, max(n - 1, 0)))
                        score(n, q_rows, k_rows, DK, mask if causal else None).then_inc(sig["max_scores"], 1)
                    pe.wait_ge(*sig("negmax", step, PAIRS))
                    for half in range(2):
                        pe.wait_ge(*sig("q_aug", step, half))
                        for g in (2 * half, 2 * half + 1):
                            for t in range(T):
                                at = (g % 2) * SEQ + t * P
                                ins = nc.tensor.transpose(m.psum[:, at:at + P], negmax[:, t, g, :], chip.ident[:, :])
                        ins.then_inc(sig["negmaxT"], 1)
                    pe.wait_ge(*sig("q_aug", step, 2))
                else:
                    pe.wait_ge(*sig("rope", step, GROUPS))
                    for n in range(PAIRS):
                        pe.wait_ge(*sig("den_probs", step, max(n - 1, 0)))
                        score(n, k_rows, q_rows, DK, None).then_inc(sig["den_scores"], 1)
                    pe.wait_ge(*sig("den_probs", step, PAIRS))

                def weigh(g):
                    pe.wait_ge(*sig("probs", step, 2 * g + 2))
                    for h in range(4 * g, 4 * g + 4):
                        for qt in range(T):
                            for kt in range(qt + 1 if causal else T):
                                last = kt == (qt if causal else T - 1)
                                ins = nc.tensor.matmul(pv[:, qt, h, 0:AUG if softmax else DK], probs[:, kt, h, qt * P:(qt + 1) * P],
                                                       v[:, kt, h, 0:AUG if softmax else DK], start=kt == 0, stop=last)
                            if not softmax:
                                for kt in range(T):
                                    ins = nc.tensor.matmul(pv[:, qt, h, DK:AUG], den_probs[:, kt, h, qt * P:(qt + 1) * P],
                                                           v[:, kt, h, DK:AUG], start=kt == 0, stop=kt == T - 1)
                    return ins

                pe.wait_ge(*sig("v", step, 1))
                pe.wait_ge(*sig("context", step))
                source, rows_of = (qk, AUG) if softmax else (turned, DK)
                for n in range(PAIRS):
                    pe.wait_ge(*sig("probs", step, max(n - 1, 0)))
                    score(n, source[:, 1], source[:, 0], rows_of, maskT if causal else None).then_inc(sig["scores"], 1)
                    if n % 2 == 1 and n > 1:
                        weigh(n // 2 - 1)
                weigh(GROUPS - 1).then_inc(sig["ctx_psum"], 1)

                pe.wait_ge(*sig("context", step, 1))
                for t in range(T):
                    ins = nc.tensor.transpose(m.psum[:, t * P:(t + 1) * P], context[:, t, :], chip.ident[:, :])
                ins.then_inc(sig["ctxT_psum"], 1)
                pe.wait_ge(*sig("ctxT", step, 1))
                for t in range(T):
                    ins = nc.tensor.matmul(vo[:, t, :], ctxT[:, t * P:(t + 1) * P], wo[:, :], start=True, stop=True)
                ins.then_inc(sig["out_psum"], 1)

        @block.scalar
        def _(act):
            act.wait_ge(*once("loaded", 1))
            with act.Fori(0, B) as step:
                act.wait_ge(*sig("xT_psum", step, 1))
                act.wait_ge(*sig("proj", step))
                if level == 2:
                    ins = nc.scalar.activation(m.xT[:, :], m.psum[:, 0:SEQ], ACT.Identity, bias=tiles["beta"][:, 0:1],
                                               scale=tiles["gamma"][:, 0:1])
                else:
                    ins = nc.scalar.activation(m.xT[:, :], m.psum[:, 0:SEQ], ACT.Copy)
                ins.then_inc(sig["xT"], 1)
                act.wait_ge(*sig("scores", step))
                for g in range(GROUPS):
                    act.wait_ge(*sig("proj", step, g + 1))
                    for n in range(2):
                        if softmax:
                            ins = nc.scalar.activation(qk[:, n, g, :], scores[:, 2 * (g % 2), n, :], ACT.Identity,
                                                       bias=tiles["bq" if n == 0 else "bk"][:, g:g + 1])
                        else:
                            ins = nc.scalar.activation(qk[:, n, g, :], scores[:, 2 * (g % 2), n, :], ACT.Copy)
                    ins.then_inc(sig["proj_read"], 1)
                act.wait_ge(*sig("ctx_psum", step))
                if not softmax:
                    for n in range(PAIRS):
                        act.wait_ge(*sig("den_scores", step, n + 1))
                        nc.scalar.activation(of_pair(den_probs, n), scores[:, banks(n), :, :], ACT.Exp, scale=scale)\
                          .then_inc(sig["den_probs"], 1)
                for n in range(PAIRS):
                    act.wait_ge(*sig("scores", step, n + 1))
                    for t in range(T) if causal else [slice(0, T)]:
                        first = t * P if causal else 0
                        ins = nc.scalar.activation(of_pair(probs, n)[:, :, t, first:SEQ], scores[:, banks(n), t, first:SEQ],
                                                   ACT.Exp, scale=scale)
                    ins.then_inc(sig["probs"], 1)
                act.wait_ge(*sig("ctxT_psum", step, 1))
                act.wait_ge(*sig("out_psum", step))
                nc.scalar.activation(ctxT[:, :], m.psum[:, 0:SEQ], ACT.Copy).then_inc(sig["ctxT"], 1)

        @block.gpsimd
        def _(pool):
            with pool.Fori(0, B) as step:
                if level == 2:
                    norm_rstd(nc, pool, sig, chip, m, step, "_a")
                norm_rstd(nc, pool, sig, chip, m, step)

        @block.vector
        def _(dve):
            nc.vector.memset(v[:, :, :, :], 1.0).then_inc(once["set"], 1)
            if softmax:
                nc.vector.memset(negmax[:, :, :, :], 0.0).then_inc(once["set"], 1)
            dve.wait_ge(*once("set", 1))
            dve.wait_ge(*once("loaded", 1))
            with dve.Fori(0, B) as step:
                tile = x_tile(chip, step, T)
                if level == 2:
                    norm_vector(nc, dve, sig, m, step, tile, lambda t: x1[:, t, :], ["x"], "_a")
                    dve.wait_ge(*sig("xn_a", step, 1))
                    tile = lambda t: x1[:, t, :]
                norm_vector(nc, dve, sig, m, step, tile, lambda t: m.xn[:, t, :], ["xT_psum"])
                dve.wait_ge(*sig("v_psum", step, 1))
                dve.wait_ge(*sig("ctx_psum", step))
                vh = vo[:, :, :].rearrange("p t (h c) -> p t h c", c=DK)
                for t in range(T):
                    if softmax:
                        ins = nc.vector.tensor_tensor(v[:, t, :, 0:DK], vh[:, t], tiles["bv"][:, :].rearrange("p (h c) -> p h c", c=DK), ALU.add)
                    else:
                        ins = nc.vector.tensor_copy(v[:, t, :, 0:DK], vh[:, t])
                ins.then_inc(sig["v"], 1)
                if softmax:
                    dve.wait_ge(*sig("negmaxT", step))
                    for n in range(PAIRS):
                        dve.wait_ge(*sig("max_scores", step, n + 1))
                        places = negmax[:, :, n // 2, :].rearrange("p t (j r) -> p j t r", r=BAND)[:, banks(n), :, DK]
                        for t in range(T) if causal else [slice(0, T)]:
                            keys = (t + 1) * P if causal else SEQ
                            ins = nc.vector.tensor_reduce(places[:, :, t], scores[:, banks(n), t, 0:keys], AX.X, ALU.max,
                                                          negate=True)
                        ins.then_inc(sig["negmax"], 1)
                    for half in range(2):
                        dve.wait_ge(*sig("negmaxT", step, half + 1))
                        q2 = qk[:, 0, 2 * half:2 * half + 2, :]
                        nc.vector.tensor_tensor(q2, m.psum[:, :].rearrange("p (g s) -> p g s", g=2), q2, ALU.add)\
                          .then_inc(sig["q_aug"], 1)
                else:
                    chain = Chain(dve, sig, "rope_chain", step)
                    rope = tiles["rope"]
                    cos, sin = (rope[:, n:n + 1, :].to_broadcast([P, 2, SEQ]) for n in range(2))
                    dve.wait_ge(*sig("scores", step))
                    for g in range(GROUPS):
                        dve.wait_ge(*sig("proj", step, g + 1))
                        dve.wait_ge(*sig("proj_read", step, g + 1))
                        dve.wait_ge(*sig("rope", step, g))
                        chain(nc.vector.tensor_tensor(turn[:, 0, :, :], scores[:, 2 * (g % 2), :, :], cos, ALU.mult))
                        chain(nc.vector.tensor_tensor(turn[:, 1, :, :], scores[:, 2 * (g % 2) + 1, :, :], sin, ALU.mult))
                        nc.vector.tensor_tensor(turned[:, :, g, :], turn[:, 0, :, :], turn[:, 1, :, :], ALU.add)\
                          .then_inc(sig["rope"], 1)
                    chain.done()
                dve.wait_ge(*sig("ctx_psum", step, 1))
                nc.vector.reciprocal(rden[:, :, :, :], pv[:, :, :, DK:AUG]).then_inc(sig["ctx_chain"], 1)
                dve.wait_ge(*sig("ctx_chain", step, 1))
                dve.wait_ge(*sig("ctxT_psum", step))
                ch = context[:, :, :].rearrange("p t (h c) -> p t h c", c=DK)
                for t in range(T):
                    ins = nc.vector.tensor_tensor(ch[:, t], pv[:, t, :, 0:DK], rden[:, t].to_broadcast([P, HEADS, DK]), ALU.mult)
                ins.then_inc(sig["context"], 1)
                dve.wait_ge(*sig("out_psum", step, 1))
                xs = chip.x[:, bass.ds(step * T, T), :]
                nc.vector.tensor_tensor(xs, vo[:, :, :], xs, ALU.add).then_inc(sig["x"], 1)
                dve.wait_ge(*sig("x", step, 1))
                if level == 2:
                    nc.vector.tensor_tensor(xs, xs, x1[:, :, :], ALU.add).then_inc(sig["residual"], 1)
                    dve.wait_ge(*sig("residual", step, 1))
                nc.vector.tensor_tensor(xs, xs, bo[:, :].rearrange("p (a d) -> p a d", a=1).to_broadcast([P, T, D]), ALU.add)\
                  .then_inc(sig["x"], 1)
                dve.wait_ge(*sig("x", step, 2))
    sig.ended(B)
    once.ended(1)


RW_HEADS, HS = 2, 64
LORA_R, TD_R = 32, 64
MIXES = 5
PAIR = 2
ROUNDS = HS // PAIR
RW_SIGNALS = dict(NORM_SIGNALS, mix_chain=3 + MIXES, lora_psum=1, lora=1, miu_psum=1, mixed=1, td_psum=1, kvrg_psum=1,
                  td_tanh=1, w_psum=1, act_chain=1, decay=1, kvr=1, g_exp=1, ruk=1, bonus_psum=1, gate=1, gate_chain=2,
                  bonus=1, vb=ROUNDS, kv=ROUNDS, scan=ROUNDS, prod=ROUNDS, y_acc=ROUNDS, yT=1, y_tok=1, yn_stats=1,
                  yn_moments=1, yn_var=1, yn_rstd=1, yn=1, ynT_psum=1, ynT=1, gated=1, out_psum=1, x=1)
RW_LOADS = 16


def stage_rwkv(chip):
    nc, dram, sig, once = chip.nc, chip.dram, chip.loop, chip.once
    sig.use(RW_SIGNALS)
    once.use(dict(loaded=16 * (RW_LOADS + 1), set=3))
    T = HALVES
    with ExitStack() as ctx:
        sb = lambda name, shape, dt=F32: ctx.enter_context(nc.sbuf_tensor(chip.tag + name, shape, dt))
        ps = lambda name, shape: ctx.enter_context(nc.psum_tensor(chip.tag + name, shape, F32))
        m = Norm(chip, ctx, T)
        tiles = {"miu_x": sb("miu_x", [P, 1]), "lambda": sb("lambda", [P, MIXES]), "A": sb("A", [P, MIXES * LORA_R]),
                 "B": sb("B", [LORA_R, MIXES, D]), "td_miu": sb("td_miu", [P, 1]), "td_A": sb("td_A", [P, TD_R]),
                 "td_B": sb("td_B", [TD_R, D]), "u": sb("u", [P, 1]), "wr": sb("wr", [P, D]), "wk": sb("wk", [P, D]),
                 "wv": sb("wv", [P, D]), "wg": sb("wg", [P, D]), "wo": sb("wo", [P, D]), "gamma": sb("gamma", [P, 1]),
                 "beta": sb("beta", [P, 1]), "head_ones": sb("head_ones", [P, P])}
        assert len(tiles) == RW_LOADS
        spread = sb("spread", [P, HS, P])
        gather = sb("gather", [P, P + HS - 1])
        delta, xm, lora = sb("delta", [P, SEQ]), sb("xm", [P, SEQ]), sb("lora", [LORA_R, MIXES, SEQ])
        mix, td = sb("mix", [P, MIXES, SEQ]), sb("td", [TD_R, SEQ])
        expw, decay = sb("expw", [P, SEQ]), sb("decay", [P, PAIR, SEQ])
        kT, vT, rT, r_next = sb("kT", [P, SEQ]), sb("vT", [P, SEQ]), sb("rT", [P, SEQ]), sb("r_next", [P, SEQ])
        ruk, bonus, gate, expg = sb("ruk", [P, SEQ]), sb("bonus", [P, SEQ]), sb("gate", [P, SEQ]), sb("expg", [P, SEQ])
        kv, state, prod = sb("kv", [P, 2, PAIR, SEQ]), sb("state", [P, 2, PAIR, SEQ]), sb("prod", [P, 2, PAIR, SEQ])
        yT, yn, ynT, gated = sb("yT", [P, SEQ]), sb("yn", [P, T, D]), sb("ynT", [P, SEQ]), sb("gated", [P, SEQ])
        y_stats, y_moments = sb("y_stats", [P, T * RW_HEADS, 6]), sb("y_moments", [P, T * RW_HEADS, 2])
        y_var, y_rstd = sb("y_var", [P, T * RW_HEADS]), sb("y_rstd", [P, T * RW_HEADS])
        work = ps("work", [P, 4, 2, SEQ])
        vb = [ps(f"vb{n}", [P, PAIR, SEQ]) for n in range(2)]
        y_psum = ps("y", [P, 512])
        block = ctx.enter_context(nc.Block())
        lora_psum = work[0:LORA_R, 0:3, :, :].rearrange("p b a s -> p (b a) s")[:, 0:MIXES, :]
        miu_psum = work[:, 0:3, :, :].rearrange("p b a s -> p (b a) s")[:, 0:MIXES, :]
        one = lambda v: v.rearrange("p (a s) -> p a s", a=1)

        @block.sync
        def _(sp):
            for name, tile in tiles.items():
                sp.dma_start(tile[:], dram["RW_" + name]).then_inc(once["loaded"], 16)
            sp.dma_start(gather[:, :], dram["RW_gather"]).then_inc(once["loaded"], 16)

        @block.tensor
        def _(pe):
            pe.wait_ge(*once("loaded", 1))
            pe.wait_ge(*once("set", 1))
            with pe.Fori(0, B) as step:
                norm_transpose(nc, pe, sig, chip, m, step)
                pe.wait_ge(*sig("mixed", step))
                pe.wait_ge(*sig("x", step))
                pe.wait_ge(*sig("ynT", step))
                pe.wait_ge(*sig("mix_chain", step, 3))
                for f in range(MIXES):
                    ins = nc.tensor.matmul(lora_psum[:, f, :], tiles["A"][:, f * LORA_R:(f + 1) * LORA_R], xm[:, :],
                                           start=True, stop=True)
                ins.then_inc(sig["lora_psum"], 1)
                pe.wait_ge(*sig("lora", step, 1))
                for f in range(MIXES):
                    ins = nc.tensor.matmul(miu_psum[:, f, :], tiles["B"][:, f, :], lora[:, f, :], start=True, stop=True)
                ins.then_inc(sig["miu_psum"], 1)
                pe.wait_ge(*sig("mixed", step, 1))
                nc.tensor.matmul(work[0:TD_R, 0, 0, :], tiles["td_A"][:, :], mix[:, 0, :], start=True, stop=True)\
                  .then_inc(sig["td_psum"], 1)
                for n, name in enumerate(("wk", "wv", "wr", "wg")):
                    ins = nc.tensor.matmul(work[:, 1 + n // 2, n % 2, :], tiles[name][:, :], mix[:, 1 + n, :], start=True, stop=True)
                ins.then_inc(sig["kvrg_psum"], 1)
                pe.wait_ge(*sig("td_tanh", step, 1))
                pe.wait_ge(*sig("bonus", step))
                nc.tensor.matmul(work[:, 3, 0, :], tiles["td_B"][:, :], td[:, :], start=True, stop=True).then_inc(sig["w_psum"], 1)
                pe.wait_ge(*sig("ruk", step, 1))
                pe.wait_ge(*sig("act_chain", step, 1))
                nc.tensor.matmul(work[:, 3, 1, :], tiles["head_ones"][:, :], ruk[:, :], start=True, stop=True)\
                  .then_inc(sig["bonus_psum"], 1)

                def spread_v(n):
                    pe.wait_ge(*sig("kv", step, max(n - 1, 0)))
                    for a in range(PAIR):
                        ins = nc.tensor.matmul(vb[n % 2][:, a, :], spread[:, PAIR * n + a, :], vT[:, :], start=True, stop=True)
                    ins.then_inc(sig["vb"], 1)

                spread_v(0)
                spread_v(1)
                pe.wait_ge(*sig("yT", step))
                for n in range(ROUNDS):
                    pe.wait_ge(*sig("prod", step, n + 1))
                    for a in range(PAIR):
                        at = HS - 1 - (PAIR * n + a)
                        ins = nc.tensor.matmul(y_psum[:, 0:SEQ], gather[:, at:at + P], prod[:, n % 2, a, :],
                                               start=n == 0 and a == 0, stop=n == ROUNDS - 1 and a == PAIR - 1)
                    ins.then_inc(sig["y_acc"], 1)
                    if n + 2 < ROUNDS:
                        spread_v(n + 2)
                pe.wait_ge(*sig("yT", step, 1))
                for t in range(T):
                    ins = nc.tensor.transpose(work[:, 0, t, 0:P], yT[:, t * P:(t + 1) * P], chip.ident[:, :])
                ins.then_inc(sig["y_tok"], 1)
                pe.wait_ge(*sig("yn", step, 1))
                pe.wait_ge(*sig("kvr", step, 1))
                for t in range(T):
                    ins = nc.tensor.transpose(work[:, 1, 0, t * P:(t + 1) * P], yn[:, t, :], chip.ident[:, :])
                ins.then_inc(sig["ynT_psum"], 1)
                pe.wait_ge(*sig("gated", step, 1))
                for t in range(T):
                    ins = nc.tensor.matmul(work[:, 0, t, 0:D], gated[:, t * P:(t + 1) * P], tiles["wo"][:, :], start=True, stop=True)
                ins.then_inc(sig["out_psum"], 1)

        @block.scalar
        def _(act):
            act.wait_ge(*once("loaded", 1))
            act.wait_ge(*once("set", 1))
            with act.Fori(0, B) as step:
                norm_xT(nc, act, sig, m, step, ["mixed"])
                act.wait_ge(*sig("lora_psum", step, 1))
                nc.scalar.activation(lora[:, :, :], lora_psum, ACT.Tanh).then_inc(sig["lora"], 1)
                act.wait_ge(*sig("td_psum", step, 1))
                nc.scalar.activation(td[:, :], work[0:TD_R, 0, 0, :], ACT.Tanh).then_inc(sig["td_tanh"], 1)
                act.wait_ge(*sig("kvrg_psum", step, 1))
                act.wait_ge(*sig("y_acc", step))
                nc.scalar.activation(kT[:, :], work[:, 1, 0, :], ACT.Copy)
                nc.scalar.activation(vT[:, :], work[:, 1, 1, :], ACT.Copy)
                nc.scalar.activation(r_next[:, 0:SEQ - 1], work[:, 2, 0, 1:SEQ], ACT.Copy)
                nc.scalar.activation(rT[:, :], work[:, 2, 0, :], ACT.Copy).then_inc(sig["kvr"], 1)
                act.wait_ge(*sig("gate", step))
                nc.scalar.activation(expg[:, :], work[:, 2, 1, :], ACT.Exp, scale=-1.0).then_inc(sig["g_exp"], 1)
                act.wait_ge(*sig("w_psum", step, 1))
                nc.scalar.activation(expw[:, :], work[:, 3, 0, :], ACT.Exp, bias=tiles["td_miu"][:, 0:1]).then_inc(sig["act_chain"], 1)
                act.wait_ge(*sig("act_chain", step, 1))
                for a in range(PAIR):
                    ins = nc.scalar.activation(decay[:, a, 1:SEQ], expw[:, 1:SEQ], ACT.Exp, scale=-1.0)
                ins.then_inc(sig["decay"], 1)
                act.wait_ge(*sig("ynT_psum", step, 1))
                act.wait_ge(*sig("gated", step))
                nc.scalar.activation(ynT[:, :], work[:, 1, 0, :], ACT.Identity, bias=tiles["beta"][:, 0:1],
                                     scale=tiles["gamma"][:, 0:1]).then_inc(sig["ynT"], 1)

        @block.gpsimd
        def _(pool):
            with pool.Fori(0, B) as step:
                norm_rstd(nc, pool, sig, chip, m, step)
                pool.wait_ge(*sig("kvr", step, 1))
                for n in range(ROUNDS):
                    pool.wait_ge(*sig("scan", step, n + 1))
                    pool.wait_ge(*sig("y_acc", step, max(n - 1, 0)))
                    nc.gpsimd.tensor_tensor(prod[:, n % 2, :, :], state[:, n % 2, :, :],
                                            one(r_next[:, :]).to_broadcast([P, PAIR, SEQ]), ALU.mult).then_inc(sig["prod"], 1)
                pool.wait_ge(*sig("yn_var", step, 1))
                nc.gpsimd.tensor_tensor(y_rstd[:, :], y_var[:, :], chip.minus_half[:, :].to_broadcast([P, T * RW_HEADS]), ALU.pow)\
                  .then_inc(sig["yn_rstd"], 1)

        @block.vector
        def _(dve):
            dve.wait_ge(*once("loaded", 1))
            nc.vector.memset(r_next[:, SEQ - 1:SEQ], 0.0).then_inc(once["set"], 1)
            nc.vector.memset(decay[:, :, 0:1], 0.0).then_inc(once["set"], 1)
            nc.vector.tensor_copy(spread[:, :, :].rearrange("p v (h k) -> p v h k", h=RW_HEADS),
                                  chip.ident[:, :].rearrange("p (h v o) -> p v h o", h=RW_HEADS, o=1).to_broadcast([P, HS, RW_HEADS, HS]))\
              .then_inc(once["set"], 1)
            with dve.Fori(0, B) as step:
                chain = Chain(dve, sig, "mix_chain", step)
                norm_vector(nc, dve, sig, m, step, x_tile(chip, step, T), lambda t: m.xn[:, t, :], ["xT_psum"])
                dve.wait_ge(*sig("xT", step, 1))
                nc.vector.tensor_scalar(delta[:, 0:1], m.xT[:, 0:1], -1.0, None, ALU.mult).then_inc(sig["mix_chain"], 1)
                chain.n += 1
                chain(nc.vector.tensor_tensor(delta[:, 1:SEQ], m.xT[:, 0:SEQ - 1], m.xT[:, 1:SEQ], ALU.subtract))
                chain(nc.vector.scalar_tensor_tensor(xm[:, :], delta[:, :], tiles["miu_x"][:, 0:1], m.xT[:, :], ALU.mult, ALU.add))
                dve.wait_ge(*sig("miu_psum", step, 1))
                dve.wait_ge(*sig("kvrg_psum", step))
                for f in range(MIXES):
                    chain(nc.vector.scalar_tensor_tensor(mix[:, f, :], miu_psum[:, f, :], tiles["lambda"][:, f:f + 1], delta[:, :],
                                                         ALU.add, ALU.mult))
                nc.vector.tensor_tensor(mix[:, :, :], mix[:, :, :], one(m.xT[:, :]).to_broadcast([P, MIXES, SEQ]), ALU.add)\
                  .then_inc(sig["mixed"], 1)
                chain.done()
                dve.wait_ge(*sig("kvr", step, 1))
                nc.vector.scalar_tensor_tensor(ruk[:, :], rT[:, :], tiles["u"][:, 0:1], kT[:, :], ALU.mult, ALU.mult)\
                  .then_inc(sig["ruk"], 1)
                gates = Chain(dve, sig, "gate_chain", step)
                dve.wait_ge(*sig("g_exp", step, 1))
                gates(nc.vector.tensor_scalar(gate[:, :], expg[:, :], 1.0, None, ALU.add))
                gates(nc.vector.reciprocal(gate[:, :], gate[:, :]))
                nc.vector.tensor_tensor(gate[:, :], work[:, 2, 1, :], gate[:, :], ALU.mult).then_inc(sig["gate"], 1)
                gates.done()
                dve.wait_ge(*sig("bonus_psum", step, 1))
                nc.vector.tensor_tensor(bonus[:, :], work[:, 3, 1, :], vT[:, :], ALU.mult).then_inc(sig["bonus"], 1)
                dve.wait_ge(*sig("decay", step, 1))
                for n in range(ROUNDS):
                    dve.wait_ge(*sig("vb", step, n + 1))
                    dve.wait_ge(*sig("scan", step, max(n - 1, 0)))
                    nc.vector.tensor_tensor(kv[:, n % 2, :, :], vb[n % 2][:, :, :], one(kT[:, :]).to_broadcast([P, PAIR, SEQ]), ALU.mult)\
                      .then_inc(sig["kv"], 1)
                    dve.wait_ge(*sig("kv", step, n + 1))
                    dve.wait_ge(*sig("prod", step, max(n - 1, 0)))
                    flat = lambda tile: tile.rearrange("p a s -> p (a s)")
                    nc.vector.tensor_tensor_scan(flat(state[:, n % 2, :, :]), flat(decay[:, :, :]), flat(kv[:, n % 2, :, :]), 0.0,
                                                 ALU.mult, ALU.add).then_inc(sig["scan"], 1)
                dve.wait_ge(*sig("y_acc", step, ROUNDS))
                dve.wait_ge(*sig("bonus", step, 1))
                nc.vector.tensor_copy(yT[:, 0:1], bonus[:, 0:1])
                nc.vector.tensor_tensor(yT[:, 1:SEQ], y_psum[:, 0:SEQ - 1], bonus[:, 1:SEQ], ALU.add).then_inc(sig["yT"], 1)
                dve.wait_ge(*sig("y_tok", step, 1))
                for n in range(T * RW_HEADS):
                    ins = nc.vector.bn_stats(y_stats[:, n, :], work[:, 0, n // 2, (n % 2) * HS:(n % 2 + 1) * HS])
                ins.then_inc(sig["yn_stats"], 1)
                sig.apart(dve, "yn_stats", step, 1)
                for n in range(T * RW_HEADS):
                    ins = nc.vector.bn_aggr(y_moments[:, n, :], y_stats[:, n, :])
                ins.then_inc(sig["yn_moments"], 1)
                dve.wait_ge(*sig("yn_moments", step, 1))
                nc.vector.tensor_scalar(y_var[:, :], y_moments[:, :, 1], EPS * RW_HEADS, None, ALU.add).then_inc(sig["yn_var"], 1)
                dve.wait_ge(*sig("yn_rstd", step, 1))
                for n in range(T * RW_HEADS):
                    half = slice((n % 2) * HS, (n % 2 + 1) * HS)
                    ins = nc.vector.tensor_scalar(yn[:, n // 2, half], work[:, 0, n // 2, half], y_moments[:, n, 0:1],
                                                  y_rstd[:, n:n + 1], ALU.subtract, ALU.mult)
                ins.then_inc(sig["yn"], 1)
                dve.wait_ge(*sig("ynT", step, 1))
                dve.wait_ge(*sig("gate", step, 1))
                nc.vector.tensor_tensor(gated[:, :], ynT[:, :], gate[:, :], ALU.mult).then_inc(sig["gated"], 1)
                dve.wait_ge(*sig("out_psum", step, 1))
                xs = chip.x[:, bass.ds(step * T, T), :]
                nc.vector.tensor_tensor(xs, work[:, 0, :, 0:D], xs, ALU.add).then_inc(sig["x"], 1)
                dve.wait_ge(*sig("x", step, 1))
    sig.ended(B)
    once.ended(1)


DEPTH = 6
LH, LD = 16, 64
INNER = LH * LD
WINDOW = 32
REACH = P + WINDOW
LPAIRS = LH // 2
FF = 341
FF_CHUNKS = 3
FF_TILES = 4
FF_STEPS = TILES // FF_TILES
CHUNKS = 4

STACK_ATTENTION = dict(z_copy=1, zT_psum=1, xsT=1, proj=CHUNKS + HALVES, square=CHUNKS, norm2=CHUNKS, half_turns=CHUNKS,
                       turn_sum=CHUNKS, clamped=CHUNKS, rnorm=CHUNKS, qk=CHUNKS, qkT_psum=2 * CHUNKS, qkT=2 * CHUNKS,
                       v=HALVES, scores=LPAIRS, negmax=LPAIRS, shifted=LPAIRS, probs=LPAIRS, probsT_psum=LPAIRS,
                       probsT=LPAIRS, pv=LPAIRS, rsum=LPAIRS, context=LPAIRS, ctxT_psum=4, ctxT=4, out_psum=1, z=1)
STACK_AHEAD = ("z_copy", "zT_psum", "xsT", "proj", "square", "norm2", "half_turns", "turn_sum", "clamped", "rnorm", "qk",
               "qkT_psum", "qkT", "v")
STACK_FFN = dict(f_copy=1, fzT_psum=1, fxsT=1, fxs_psum=1, norm_chain=1, moments=1, var=1, rstd=1, xn=1,
                 fxnT_psum=1, fxnT=1, h_psum=FF_CHUNKS, gelu=FF_CHUNKS, hidden=FF_CHUNKS, f_psum=1, zf=2)
STACK_LAYER = dict(tables=1, qkv_weights=32, out_weights=16, ffn_weights=64)
FF_PIECES = 3 + FF_CHUNKS + 1


def beside(n):
    total = (FF_STEPS - 1) * FF_PIECES
    return range(n * total // LPAIRS, (n + 1) * total // LPAIRS)


def stage_stack(chip):
    nc, dram, att, ffn, layer_sig, once = chip.nc, chip.dram, chip.loop, chip.ffn, chip.layer, chip.once
    att.use(STACK_ATTENTION)
    once.use(dict(set=3, loaded=48))
    with ExitStack() as ctx:
        sb = lambda name, shape, dt=F32: ctx.enter_context(nc.sbuf_tensor(chip.tag + name, shape, dt))
        z = sb("z", [P, TILES, D])
        wqkv, wo = sb("wqkv", [P, 3 * INNER]), sb("wo", [P, LPAIRS, D])
        rows, base, tables = sb("rows", [P, 4, 1, LD]), sb("base", [P, 4, HALVES, LD]), sb("tables", [P, 4, HALVES, LD])
        w1, w2, b2 = sb("w1", [P, 2 * FF]), sb("w2", [P, FF_CHUNKS, D]), sb("b2", [P, 1, D])
        cols = sb("cols", [P, 2 * FF_CHUNKS + 2])
        ident_bf, band = sb("ident_bf", [P, P], BF16), sb("band", [P, HALVES, REACH], BF16)
        zc, xsT = sb("zc", [P, HALVES, D]), sb("xsT", [P, SEQ])
        square = sb("square", [P, 2, INNER])
        halves = sb("halves", [P, 2, 2, INNER])
        qk = sb("qk", [P, CHUNKS, INNER])
        norm2, clamped, rnorm = sb("norm2", [P, CHUNKS, LH]), sb("clamped", [P, CHUNKS, LH]), sb("rnorm", [P, CHUNKS, LH])
        qkT = sb("qkT", [P, 2, LPAIRS, SEQ])
        v, v_near = sb("v", [P, HALVES, LH, LD + 1]), sb("v_near", [WINDOW, LH, LD + 1])
        negmax = sb("negmax", [P, 2, 2, HALVES, 1])
        shifted, probs = sb("shifted", [P, 2, 2, HALVES, REACH]), sb("probs", [P, 2, 2, HALVES, REACH])
        probsT, near = sb("probsT", [P, 2, 2, HALVES, P]), sb("near", [WINDOW, 2, 2, WINDOW])
        rsum = sb("rsum", [P, 2, 2, HALVES, 1])
        context, ctxT = sb("context", [P, HALVES, INNER]), sb("ctxT", [P, LPAIRS, SEQ])
        fz, fxsT = sb("fz", [P, FF_TILES, D]), sb("fxsT", [P, 2, SEQ])
        stats, moments = sb("stats", [P, FF_TILES, 6]), sb("moments", [P, FF_TILES, 2])
        var, rstd = sb("var", [P, FF_TILES]), sb("rstd", [P, FF_TILES])
        fxn, fxnT = sb("fxn", [P, FF_TILES, D]), sb("fxnT", [P, FF_TILES * P])
        gelu, hidden = sb("gelu", [P, 2, FF_TILES * P]), sb("hidden", [P, FF_CHUNKS, FF_TILES * P])
        wide = ctx.enter_context(nc.psum_tensor(chip.tag + "wide", [P, 2, 512], F32))
        score_psum = ctx.enter_context(nc.psum_tensor(chip.tag + "score_psum", [P, 2, 512], F32))
        flip = [ctx.enter_context(nc.psum_tensor(f"{chip.tag}flip{n}", [P, 512], F32)) for n in range(2)]
        acc = [ctx.enter_context(nc.psum_tensor(f"{chip.tag}acc{n}", [P, 512], F32)) for n in range(2)]
        tiles4 = lambda bank: bank[:, :].rearrange("p (t d) -> p t d", d=D)
        pv_of = lambda n: acc[n % 2][:, 0:4 * (LD + 1)].rearrange("p (h t c) -> p h t c", h=2, t=HALVES)
        near_psum = lambda n: acc[n % 2][0:WINDOW, 4 * (LD + 1):4 * (LD + 1) + 2 * WINDOW].rearrange("p (h q) -> p h q", h=2)
        scores = score_psum[:, :, 0:HALVES * REACH].rearrange("p h (t k) -> p h t k", t=HALVES)
        turn_flip = lambda n: flip[0 if n in (5, 7) else 1]
        ctx_flip = lambda n: flip[(n + 1) % 2]

        m = Norm(chip, ctx, FF_TILES, turned=False)
        first = chip.ffn
        first.use(dict(norm_chain=1, moments=1, var=1, rstd=1, xn=1))
        with nc.Block() as block:
            @block.gpsimd
            def _(pool):
                with pool.Fori(0, FF_STEPS) as step:
                    norm_rstd(nc, pool, first, chip, m, step)

            @block.vector
            def _(dve):
                with dve.Fori(0, FF_STEPS) as step:
                    norm_vector(nc, dve, first, m, step, x_tile(chip, step, FF_TILES),
                                lambda t: z[:, bass.ds(step * FF_TILES + t, 1), :].rearrange("p a d -> p (a d)"), [])
                    dve.wait_ge(*first("xn", step, 1))
                nc.vector.memset(xsT[64:P, 0:1], 0.0).then_inc(once["set"], 1)
                nc.vector.memset(fxsT[64:P, :, 0:1], 0.0).then_inc(once["set"], 1)
                nc.vector.memset(v_near[:, :, LD:LD + 1], 1.0)
                nc.vector.memset(v[:, :, :, LD:LD + 1], 1.0).then_inc(once["set"], 1)
                dve.wait_ge(*once("set", 1))

            @block.sync
            def _(sp):
                sp.dma_start(base[:, :, :, :], dram["T_base"]).then_inc(once["loaded"], 16)
                sp.dma_start(ident_bf[:, :], dram["ident_bf"]).then_inc(once["loaded"], 16)
                sp.dma_start(band[:, :, :], dram["T_band"]).then_inc(once["loaded"], 16)
                sp.wait_ge(*once("loaded", 1))

        first.ended(FF_STEPS)
        once.ended(1)
        ffn.use(STACK_FFN)
        block = ctx.enter_context(nc.Block())

        @block.sync
        def _(sp):
            def load(layer, names, done):
                tiles = dict(wqkv=wqkv, rows=rows, wo=wo, w1=w1, w2=w2, cols=cols, b2=b2)
                for name in names:
                    sp.dma_start(tiles[name][:], layer_view(dram["T_" + name], layer)).then_inc(layer_sig[done], 16)

            load(0, ("wqkv", "rows"), "qkv_weights")
            load(0, ("wo",), "out_weights")
            load(0, ("w1", "w2", "cols", "b2"), "ffn_weights")
            if DEPTH > 1:
                with sp.Fori(0, DEPTH - 1) as layer:
                    sp.wait_ge(*att("proj", (layer + 1) * B))
                    att.settle(sp)
                    sp.wait_ge(*layer_sig("tables", layer, 1))
                    att.settle(sp)
                    load(layer + 1, ("wqkv", "rows"), "qkv_weights")
                    sp.wait_ge(*att("out_psum", (layer + 1) * B))
                    att.settle(sp)
                    load(layer + 1, ("wo",), "out_weights")
                    sp.wait_ge(*ffn("zf", (layer + 1) * FF_STEPS))
                    att.settle(sp)
                    load(layer + 1, ("w1", "w2", "cols", "b2"), "ffn_weights")
            sp.wait_ge(*att("proj", DEPTH * B))
            sp.wait_ge(*layer_sig("tables", DEPTH - 1, 1))
            load(DEPTH, ("wqkv", "rows"), "qkv_weights")

        @block.tensor
        def _(pe):
            def turn_z(ahead, settled):
                pe.wait_ge(*att("z_copy", ahead, 1))
                pe.wait_ge(*att("qkT", ahead))
                pe.wait_ge(*att("ctxT", settled))
                for t in range(HALVES):
                    ins = nc.tensor.transpose(flip[1][:, t * P:(t + 1) * P], zc[:, t, :], chip.ident[:, :])
                ins.then_inc(att["zT_psum"], 1)

            def project(ahead, n):
                if n == 0:
                    pe.wait_ge(*att("xsT", ahead, 1))
                    pe.wait_ge(*att("v", ahead))
                elif n <= CHUNKS:
                    pe.wait_ge(*att("half_turns", ahead, n))
                else:
                    pe.wait_ge(*att("v", ahead, 1))
                for c in range(2):
                    at = (n // HALVES) * INNER + c * 512
                    ins = nc.tensor.matmul(wide[:, c, :], xsT[:, (n % HALVES) * P:(n % HALVES + 1) * P],
                                           wqkv[:, at:at + 512], start=True, stop=True)
                ins.then_inc(att["proj"], 1)

            def turn_qk(ahead, n):
                chunk, part = n % CHUNKS, n // CHUNKS
                pe.wait_ge(*att("qk", ahead, chunk + 1))
                if n > 0 and n != 5:
                    pe.wait_ge(*att("qkT", ahead, n if n <= CHUNKS else n - 1))
                for i in range(4):
                    pair = 4 * part + i
                    ins = nc.tensor.transpose(turn_flip(n)[:, i * P:(i + 1) * P], qk[:, chunk, pair * P:(pair + 1) * P],
                                              chip.ident[:, :])
                ins.then_inc(att["qkT_psum"], 1)

            def score(step, n):
                pe.wait_ge(*att("shifted", step, n))
                if n % 4 == 0:
                    pe.wait_ge(*att("qkT", step, n + 4))
                for h in range(2):
                    nc.tensor.matmul(score_psum[:, h, 0:HALVES * REACH], ident_bf[:, :],
                                     band[:, :, :].rearrange("p t k -> p (t k)"), start=True, stop=False,
                                     skip_group_check=True)
                for t in range(HALVES):
                    for h in range(2):
                        of_head = slice(h * LD, (h + 1) * LD)
                        first_key, at = (0, WINDOW) if t == 0 else (P - WINDOW, REACH)
                        ins = nc.tensor.matmul(score_psum[:, h, at:HALVES * REACH if t else REACH],
                                               qkT[of_head, 0, n, t * P:(t + 1) * P],
                                               qkT[of_head, 1, n, first_key:(t + 1) * P],
                                               start=False, stop=t == HALVES - 1, skip_group_check=True)
                ins.then_inc(att["scores"], 1)

            def turn_probs(step, n):
                pe.wait_ge(*att("probs", step, n + 1))
                pe.wait_ge(*att("probsT", step, n))
                if n == 0:
                    pe.wait_ge(*att("qkT", step, 2 * CHUNKS))
                    pe.wait_ge(*att("ctxT", step))
                    pe.wait_ge(*att("context", step))
                elif n == 1:
                    pe.wait_ge(*att("z", step))
                else:
                    pe.wait_ge(*att("context", step, n - 1))
                for h in range(2):
                    for t in range(HALVES):
                        nc.tensor.transpose(flip[0][:, (2 * h + t) * P:(2 * h + t + 1) * P],
                                            probs[:, n % 2, h, t, WINDOW:REACH], chip.ident[:, :])
                    ins = nc.tensor.transpose(near_psum(n)[:, h, :], probs[0:WINDOW, n % 2, h, 1, 0:WINDOW],
                                              chip.ident[0:WINDOW, 0:WINDOW])
                ins.then_inc(att["probsT_psum"], 1)

            def weigh(step, n):
                pe.wait_ge(*att("probsT", step, n + 1))
                if n == 0:
                    pe.wait_ge(*att("v", step, HALVES))
                for h in range(2):
                    head = 2 * n + h
                    for t in range(HALVES):
                        nc.tensor.matmul(pv_of(n)[:, h, t, :], probsT[:, n % 2, h, t, :], v[:, t, head, :],
                                         start=True, stop=t == 0, skip_group_check=True)
                    ins = nc.tensor.matmul(pv_of(n)[0:WINDOW, h, 1, :], near[:, n % 2, h, :], v_near[:, head, :],
                                           start=False, stop=True, skip_group_check=True)
                ins.then_inc(att["pv"], 1)

            def turn_context(step, n, ahead=None):
                pe.wait_ge(*att("context", step, 2 * n + 2))
                if n > 1:
                    pe.wait_ge(*att("ctxT", step, n - 1))
                elif ahead is not None:
                    pe.wait_ge(*att("qkT", ahead, 7 + n))
                for i in range(2):
                    for t in range(HALVES):
                        c = 2 * n + i
                        ins = nc.tensor.transpose(ctx_flip(n)[:, (2 * i + t) * P:(2 * i + t + 1) * P],
                                                  context[:, t, c * P:(c + 1) * P], chip.ident[:, :])
                ins.then_inc(att["ctxT_psum"], 1)

            def output(step):
                pe.wait_ge(*att("ctxT", step, 4))
                for t in range(HALVES):
                    for c in range(LPAIRS):
                        ins = nc.tensor.matmul(acc[1][:, t * P:(t + 1) * P], ctxT[:, c, t * P:(t + 1) * P], wo[:, c, :],
                                               start=c == 0, stop=c == LPAIRS - 1)
                ins.then_inc(att["out_psum"], 1)

            def ffn_piece(step, n, banks):
                left, right = banks[:, 0, :], banks[:, 1, :]
                if n == 0:
                    pe.wait_ge(*ffn("f_copy", step, 1))
                    pe.wait_ge(*ffn("zf", step))
                    for t in range(FF_TILES):
                        ins = nc.tensor.transpose(left[:, t * P:(t + 1) * P], fz[:, t, :], chip.ident[:, :])
                    ins.then_inc(ffn["fzT_psum"], 1)
                elif n == 1:
                    pe.wait_ge(*ffn("fxsT", step, 1))
                    for t in range(FF_TILES):
                        ins = nc.tensor.transpose(right[:, t * P:(t + 1) * P], fxsT[:, t // 2, (t % 2) * P:(t % 2 + 1) * P],
                                                  chip.ident[:, :])
                    ins.then_inc(ffn["fxs_psum"], 1)
                elif n == 2:
                    pe.wait_ge(*ffn("xn", step, 1))
                    for t in range(FF_TILES):
                        ins = nc.tensor.transpose(left[:, t * P:(t + 1) * P], fxn[:, t, :], chip.ident[:, :])
                    ins.then_inc(ffn["fxnT_psum"], 1)
                elif n < FF_PIECES - 1:
                    c = n - 3
                    width = min(P, FF - c * P)
                    if c == 0:
                        pe.wait_ge(*ffn("fxnT", step, 1))
                    else:
                        pe.wait_ge(*ffn("hidden", step, c))
                    for half in range(2):
                        at = half * FF + c * P
                        ins = nc.tensor.matmul(banks[0:width, half, :], w1[:, at:at + width], fxnT[:, :],
                                               start=True, stop=True)
                    ins.then_inc(ffn["h_psum"], 1)
                else:
                    pe.wait_ge(*ffn("hidden", step, FF_CHUNKS))
                    for t in range(FF_TILES):
                        for c in range(FF_CHUNKS):
                            width = min(P, FF - c * P)
                            ins = nc.tensor.matmul(left[:, t * P:(t + 1) * P], hidden[0:width, c, t * P:(t + 1) * P],
                                                   w2[0:width, c, :], start=c == 0, stop=c == FF_CHUNKS - 1)
                    ins.then_inc(ffn["f_psum"], 1)

            pe.wait_ge(*layer_sig("qkv_weights", 0, 32))
            turn_z(0, 0)
            for n in range(CHUNKS + HALVES):
                project(0, n)
            for n in range(2 * CHUNKS):
                turn_qk(0, n)
            with pe.Fori(0, DEPTH) as layer:
                start = layer * B
                pe.wait_ge(*layer_sig("out_weights", layer, 16))
                pe.wait_ge(*ffn("zf", layer * FF_STEPS))
                score(start, 0)
                att.settle(pe)
                with pe.Fori(0, B - 1) as b:
                    step = layer * B + b
                    ahead = step + 1
                    for n in range(LPAIRS):
                        if n + 1 < LPAIRS:
                            score(step, n + 1)
                        if n > 0:
                            weigh(step, n - 1)
                        if n == 0:
                            turn_z(ahead, step)
                        if n >= CHUNKS:
                            turn_qk(ahead, n - CHUNKS)
                        turn_probs(step, n)
                        if n <= CHUNKS:
                            project(ahead, n)
                    score(ahead, 0)
                    turn_qk(ahead, 4)
                    weigh(step, LPAIRS - 1)
                    for n in range(5, 8):
                        turn_qk(ahead, n)
                    for n in range(4):
                        turn_context(step, n, ahead)
                        if n == 1:
                            project(ahead, CHUNKS + 1)
                    output(step)
                last, ahead = start + (B - 1), start + B
                f_start = layer * FF_STEPS
                pe.wait_ge(*layer_sig("ffn_weights", layer, 64))
                pe.wait_ge(*att("v", ahead))
                for n in range(LPAIRS):
                    pieces = beside(n)
                    if n + 1 < LPAIRS:
                        score(last, n + 1)
                    ffn_piece(f_start + pieces[0] // FF_PIECES, pieces[0] % FF_PIECES, wide)
                    if n > 0:
                        weigh(last, n - 1)
                    ffn_piece(f_start + pieces[1] // FF_PIECES, pieces[1] % FF_PIECES, wide)
                    turn_probs(last, n)
                    for piece in pieces[2:]:
                        ffn_piece(f_start + piece // FF_PIECES, piece % FF_PIECES, wide)
                weigh(last, LPAIRS - 1)
                for n in range(4):
                    turn_context(last, n)
                output(last)
                f_last = f_start + (FF_STEPS - 1)
                pe.wait_ge(*layer_sig("qkv_weights", layer + 1, 32))
                pe.wait_ge(*att("shifted", ahead))
                ffn_piece(f_last, 0, score_psum)
                turn_z(ahead, ahead)
                ffn_piece(f_last, 1, score_psum)
                project(ahead, 0)
                ffn_piece(f_last, 2, score_psum)
                ffn_piece(f_last, 3, score_psum)
                project(ahead, 1)
                ffn_piece(f_last, 4, score_psum)
                ffn_piece(f_last, 5, score_psum)
                project(ahead, 2)
                ffn_piece(f_last, 6, score_psum)
                project(ahead, 3)
                project(ahead, 4)
                turn_qk(ahead, 0)
                project(ahead, 5)
                for n in range(1, 2 * CHUNKS):
                    turn_qk(ahead, n)

        @block.scalar
        def _(act):
            def shifted_copy(target, bank, done):
                nc.scalar.activation(target[0:64], bank[0:64], ACT.Copy)
                tokens = len(target.shape) - 1
                if tokens == 1:
                    ins = nc.scalar.activation(target[64:P, 1:SEQ], bank[64:P, 0:SEQ - 1], ACT.Copy)
                else:
                    ins = nc.scalar.activation(target[64:P, :, 1:SEQ], bank[64:P, :, 0:SEQ - 1], ACT.Copy)
                ins.then_inc(done, 1)

            def shifted_z(ahead):
                act.wait_ge(*att("zT_psum", ahead, 1))
                act.wait_ge(*att("proj", ahead))
                shifted_copy(xsT[:, :], flip[1][:, 0:SEQ], att["xsT"])

            def squares(ahead, n):
                act.wait_ge(*att("proj", ahead, n + 1))
                act.wait_ge(*att("norm2", ahead, max(n - 1, 0)))
                nc.scalar.activation(square[:, n % 2, :], wide[:, :, :].rearrange("p a n -> p (a n)"), ACT.Square)\
                  .then_inc(att["square"], 1)

            def copy_v(ahead, t):
                act.wait_ge(*att("proj", ahead, CHUNKS + t + 1))
                if t == 0:
                    act.wait_ge(*att("pv", ahead))
                heads = lambda rows: wide[rows, :, :].rearrange("p a (h d) -> p (a h) d", d=LD)
                if t == 0:
                    nc.scalar.activation(v_near[:, :, 0:LD], heads(slice(P - WINDOW, P)), ACT.Copy)
                nc.scalar.activation(v[:, t, :, 0:LD], heads(slice(0, P)), ACT.Copy)\
                  .then_inc(att["v"], 1)

            def copy_qkT(ahead, n, scored):
                chunk, part = n % CHUNKS, n // CHUNKS
                act.wait_ge(*att("qkT_psum", ahead, n + 1))
                act.wait_ge(*scored)
                target = qkT[:, chunk // 2, 4 * part:4 * part + 4, (chunk % 2) * P:(chunk % 2 + 1) * P]
                nc.scalar.activation(target, tiles4(turn_flip(n)), ACT.Copy).then_inc(att["qkT"], 1)

            def exponential(step, n):
                act.wait_ge(*att("shifted", step, n + 1))
                act.wait_ge(*att("probsT_psum", step, max(n - 1, 0)))
                nc.scalar.activation(probs[:, n % 2], shifted[:, n % 2], ACT.Exp).then_inc(att["probs"], 1)

            def copy_probsT(step, n):
                act.wait_ge(*att("probsT_psum", step, n + 1))
                act.wait_ge(*att("pv", step, max(n - 1, 0)))
                nc.scalar.activation(probsT[:, n % 2].rearrange("p h t q -> p (h t) q"), tiles4(flip[0]), ACT.Copy)
                nc.scalar.activation(near[:, n % 2], near_psum(n), ACT.Copy).then_inc(att["probsT"], 1)

            def copy_ctxT(step, n):
                if n == 0:
                    act.wait_ge(*att("out_psum", step))
                act.wait_ge(*att("ctxT_psum", step, n + 1))
                nc.scalar.activation(ctxT[:, 2 * n:2 * n + 2, :], ctx_flip(n)[:, :].rearrange("p (c s) -> p c s", c=2), ACT.Copy)\
                  .then_inc(att["ctxT"], 1)

            def ffn_piece(step, n, banks):
                if n == 0:
                    act.wait_ge(*ffn("fzT_psum", step, 1))
                    act.wait_ge(*ffn("fxs_psum", step))
                    shifted_copy(fxsT[:, :, :], banks[:, 0, :].rearrange("p (b s) -> p b s", b=2), ffn["fxsT"])
                elif n == 2:
                    act.wait_ge(*ffn("fxnT_psum", step, 1))
                    act.wait_ge(*ffn("h_psum", step))
                    nc.scalar.activation(fxnT[:, :], banks[:, 0, :], ACT.Identity, scale=cols[:, 2 * FF_CHUNKS:2 * FF_CHUNKS + 1],
                                         bias=cols[:, 2 * FF_CHUNKS + 1:2 * FF_CHUNKS + 2]).then_inc(ffn["fxnT"], 1)
                elif 3 <= n < FF_PIECES - 1:
                    c = n - 3
                    width = min(P, FF - c * P)
                    act.wait_ge(*ffn("h_psum", step, c + 1))
                    act.wait_ge(*ffn("hidden", step, max(c - 1, 0)))
                    nc.scalar.activation(gelu[0:width, c % 2, :], banks[0:width, 1, :], ACT.Gelu,
                                         bias=cols[0:width, FF_CHUNKS + c:FF_CHUNKS + c + 1]).then_inc(ffn["gelu"], 1)

            shifted_z(0)
            for n in range(CHUNKS):
                squares(0, n)
            for t in range(HALVES):
                copy_v(0, t)
            for n in range(2 * CHUNKS):
                copy_qkT(0, n, att("scores", 0))
            with act.Fori(0, DEPTH) as layer:
                start = layer * B
                exponential(start, 0)
                with act.Fori(0, B - 1) as b:
                    step = layer * B + b
                    ahead = step + 1
                    for n in range(LPAIRS):
                        if n == 0:
                            shifted_z(ahead)
                        if n >= CHUNKS:
                            copy_qkT(ahead, n - CHUNKS, att("scores", step, 4))
                        copy_probsT(step, n)
                        if n + 1 < LPAIRS:
                            exponential(step, n + 1)
                        if n < CHUNKS:
                            squares(ahead, n)
                    copy_qkT(ahead, 4, att("scores", step, LPAIRS))
                    exponential(ahead, 0)
                    for n in range(5, 8):
                        copy_qkT(ahead, n, att("scores", step, LPAIRS))
                    copy_v(ahead, 0)
                    for n in range(4):
                        copy_ctxT(step, n)
                        if n == 1:
                            copy_v(ahead, 1)
                last, ahead = start + (B - 1), start + B
                f_start = layer * FF_STEPS
                act.wait_ge(*layer_sig("ffn_weights", layer, 64))
                for n in range(LPAIRS):
                    pieces = beside(n)
                    for piece in pieces[:2]:
                        ffn_piece(f_start + piece // FF_PIECES, piece % FF_PIECES, wide)
                    copy_probsT(last, n)
                    if n + 1 < LPAIRS:
                        exponential(last, n + 1)
                    for piece in pieces[2:]:
                        ffn_piece(f_start + piece // FF_PIECES, piece % FF_PIECES, wide)
                for n in range(4):
                    copy_ctxT(last, n)
                f_last = f_start + (FF_STEPS - 1)
                ffn_piece(f_last, 0, score_psum)
                shifted_z(ahead)
                squares(ahead, 0)
                ffn_piece(f_last, 2, score_psum)
                ffn_piece(f_last, 3, score_psum)
                squares(ahead, 1)
                ffn_piece(f_last, 4, score_psum)
                ffn_piece(f_last, 5, score_psum)
                squares(ahead, 2)
                squares(ahead, 3)
                copy_v(ahead, 0)
                copy_qkT(ahead, 0, att("scores", ahead))
                copy_v(ahead, 1)
                for n in range(1, 2 * CHUNKS):
                    copy_qkT(ahead, n, att("scores", ahead))

        @block.gpsimd
        def _(pool):
            def rotate_and_scale(ahead):
                pool.wait_ge(*att("qkT_psum", ahead))
                for n in range(CHUNKS):
                    pool.wait_ge(*att("half_turns", ahead, n + 1))
                    nc.gpsimd.tensor_tensor(qk[:, n, :], halves[:, n % 2, 0, :], halves[:, n % 2, 1, :], ALU.add)\
                      .then_inc(att["turn_sum"], 1)
                    pool.wait_ge(*att("clamped", ahead, n + 1))
                    if n == 0:
                        pool.wait_ge(*att("qk", ahead))
                    nc.gpsimd.tensor_tensor(rnorm[:, n, :], clamped[:, n, :], chip.minus_half[:, :].to_broadcast([P, LH]), ALU.pow)\
                      .then_inc(att["rnorm"], 1)
                    pool.wait_ge(*att("rnorm", ahead, n + 1))
                    pool.wait_ge(*att("turn_sum", ahead, n + 1))
                    heads = qk[:, n, :].rearrange("p (h d) -> p h d", d=LD)
                    nc.gpsimd.tensor_tensor(heads, heads, rnorm[:, n, :].rearrange("p (h o) -> p h o", o=1).to_broadcast([P, LH, LD]),
                                            ALU.mult).then_inc(att["qk"], 1)

            rotate_and_scale(0)
            with pool.Fori(0, DEPTH) as layer:
                with pool.Fori(0, B - 1) as b:
                    rotate_and_scale(layer * B + b + 1)
                with pool.Fori(0, FF_STEPS) as s:
                    step = layer * FF_STEPS + s
                    pool.wait_ge(*ffn("var", step, 1))
                    nc.gpsimd.tensor_tensor(rstd[:, :], var[:, :], chip.minus_half[:, :].to_broadcast([P, FF_TILES]), ALU.pow)\
                      .then_inc(ffn["rstd"], 1)
                rotate_and_scale(layer * B + B)

        @block.vector
        def _(dve):
            def copy_z(ahead, b):
                dve.wait_ge(*att("zT_psum", ahead))
                nc.vector.tensor_copy(zc[:, :, :], z[:, bass.ds(b * HALVES, HALVES), :]).then_inc(att["z_copy"], 1)

            def rotate(ahead, n):
                dve.wait_ge(*att("proj", ahead, n + 1))
                if n == 0:
                    dve.wait_ge(*att("rnorm", ahead))
                dve.wait_ge(*att("square", ahead, n + 1))
                dve.wait_ge(*att("turn_sum", ahead, max(n - 1, 0)))
                which, t = n // 2, n % 2
                heads = wide[:, :, :].rearrange("p a (h d) -> p (a h) d", d=LD)
                out = halves[:, n % 2].rearrange("p k (h d) -> p k h d", d=LD)
                cos = tables[:, 2 * which, t:t + 1, :]
                sin = tables[:, 2 * which + 1, t:t + 1, :]
                nc.vector.tensor_tensor(out[:, 0], heads, cos.to_broadcast([P, LH, LD]), ALU.mult)
                for half in range(2):
                    to, of = (slice(0, LD // 2), slice(LD // 2, LD))[::1 if half == 0 else -1]
                    ins = nc.vector.tensor_tensor(out[:, 1, :, to], heads[:, :, of], sin[:, :, to].to_broadcast([P, LH, LD // 2]),
                                                  ALU.mult)
                ins.then_inc(att["half_turns"], 1)

            def norms(ahead, n):
                nc.vector.tensor_reduce(norm2[:, n, :], square[:, n % 2, :].rearrange("p (h d) -> p h d", d=LD), AX.X, ALU.add)\
                  .then_inc(att["norm2"], 1)
                dve.wait_ge(*att("norm2", ahead, n + 1))
                nc.vector.tensor_scalar(clamped[:, n, :], norm2[:, n, :], 1e-24, None, ALU.max).then_inc(att["clamped"], 1)

            def shift(step, n):
                dve.wait_ge(*att("scores", step, n + 1))
                dve.wait_ge(*att("shifted", step, max(n - 1, 0)))
                nc.vector.tensor_reduce(negmax[:, n % 2, :, :, 0], scores, AX.X, ALU.max, negate=True)\
                  .then_inc(att["negmax"], 1)
                dve.wait_ge(*att("negmax", step, n + 1))
                dve.wait_ge(*att("probs", step, max(n - 1, 0)))
                nc.vector.tensor_tensor(shifted[:, n % 2], scores, negmax[:, n % 2].to_broadcast([P, 2, HALVES, REACH]), ALU.add)\
                  .then_inc(att["shifted"], 1)

            def divide(step, n):
                dve.wait_ge(*att("pv", step, n + 1))
                dve.wait_ge(*att("context", step, max(n - 1, 0)))
                nc.vector.reciprocal(rsum[:, n % 2], pv_of(n)[:, :, :, LD:LD + 1]).then_inc(att["rsum"], 1)
                dve.wait_ge(*att("rsum", step, n + 1))
                if n == 0:
                    dve.wait_ge(*att("ctxT_psum", step))
                to = context[:, :, 2 * n * LD:2 * (n + 1) * LD].rearrange("p t (h d) -> p h t d", h=2)
                nc.vector.tensor_tensor(to, pv_of(n)[:, :, :, 0:LD], rsum[:, n % 2].to_broadcast([P, 2, HALVES, LD]), ALU.mult)\
                  .then_inc(att["context"], 1)

            def add_output(step, b):
                z_of = z[:, bass.ds(b * HALVES, HALVES), :]
                dve.wait_ge(*att("out_psum", step, 1))
                nc.vector.tensor_tensor(z_of, tiles4(acc[1])[:, 0:HALVES, :], z_of, ALU.add).then_inc(att["z"], 1)
                dve.wait_ge(*att("z", step, 1))

            def scale_tables(layer):
                dve.wait_ge(*layer_sig("qkv_weights", layer, 32))
                dve.wait_ge(*att("half_turns", layer * B))
                nc.vector.tensor_tensor(tables[:, :, :, :], base[:, :, :, :], rows[:, :, :, :].to_broadcast([P, 4, HALVES, LD]), ALU.mult)\
                  .then_inc(layer_sig["tables"], 1)
                dve.wait_ge(*layer_sig("tables", layer, 1))

            def copy_ff(step, s):
                dve.wait_ge(*ffn("fzT_psum", step))
                nc.vector.tensor_copy(fz[:, :, :], z[:, s * FF_TILES:(s + 1) * FF_TILES, :]).then_inc(ffn["f_copy"], 1)

            def ffn_piece(step, s, n, banks):
                left, right = banks[:, 0, :], banks[:, 1, :]
                if n == 1:
                    dve.wait_ge(*ffn("fxs_psum", step, 1))
                    for t in range(FF_TILES):
                        ins = nc.vector.bn_stats(stats[:, t, :], right[:, t * P:(t + 1) * P])
                    ins.then_inc(ffn["norm_chain"], 1)
                    ffn.apart(dve, "norm_chain", step, 1)
                    for t in range(FF_TILES):
                        ins = nc.vector.bn_aggr(moments[:, t, :], stats[:, t, :])
                    ins.then_inc(ffn["moments"], 1)
                    dve.wait_ge(*ffn("moments", step, 1))
                    nc.vector.tensor_scalar(var[:, :], moments[:, :, 1], EPS, None, ALU.add).then_inc(ffn["var"], 1)
                    dve.wait_ge(*ffn("rstd", step, 1))
                    dve.wait_ge(*ffn("fxnT_psum", step))
                    for t in range(FF_TILES):
                        ins = nc.vector.tensor_scalar(fxn[:, t, :], right[:, t * P:(t + 1) * P], moments[:, t, 0:1],
                                                      rstd[:, t:t + 1], ALU.subtract, ALU.mult)
                    ins.then_inc(ffn["xn"], 1)
                elif 3 <= n < FF_PIECES - 1:
                    c = n - 3
                    width = min(P, FF - c * P)
                    if c == 0:
                        dve.wait_ge(*ffn("f_psum", step))
                    dve.wait_ge(*ffn("gelu", step, c + 1))
                    nc.vector.scalar_tensor_tensor(hidden[0:width, c, :], left[0:width, :], cols[0:width, c:c + 1],
                                                   gelu[0:width, c % 2, :], ALU.add, ALU.mult).then_inc(ffn["hidden"], 1)
                elif n == FF_PIECES - 1:
                    z_of = z[:, s * FF_TILES:(s + 1) * FF_TILES, :]
                    dve.wait_ge(*ffn("f_psum", step, 1))
                    nc.vector.tensor_tensor(z_of, tiles4(left), z_of, ALU.add).then_inc(ffn["zf"], 1)
                    dve.wait_ge(*ffn("zf", step, 1))
                    nc.vector.tensor_tensor(z_of, z_of, b2[:, :, :].to_broadcast([P, FF_TILES, D]), ALU.add).then_inc(ffn["zf"], 1)
                    dve.wait_ge(*ffn("zf", step, 2))
                    if s + 1 < FF_STEPS - 1:
                        copy_ff(step + 1, s + 1)

            copy_z(0, 0)
            scale_tables(0)
            for n in range(CHUNKS):
                rotate(0, n)
                norms(0, n)
            with dve.Fori(0, DEPTH) as layer:
                start = layer * B
                shift(start, 0)
                att.settle(dve)
                with dve.Fori(0, B - 1) as b:
                    step = layer * B + b
                    ahead = step + 1
                    copy_z(ahead, b + 1)
                    for n in range(LPAIRS):
                        if 1 <= n <= CHUNKS:
                            rotate(ahead, n - 1)
                        if n + 1 < LPAIRS:
                            shift(step, n + 1)
                        if n > 0:
                            divide(step, n - 1)
                        if 1 <= n <= CHUNKS:
                            norms(ahead, n - 1)
                    shift(ahead, 0)
                    divide(step, LPAIRS - 1)
                    add_output(step, b)
                last, ahead = start + (B - 1), start + B
                f_start = layer * FF_STEPS
                dve.wait_ge(*layer_sig("ffn_weights", layer, 64))
                copy_ff(f_start, 0)
                for n in range(LPAIRS):
                    pieces = beside(n)
                    if n + 1 < LPAIRS:
                        shift(last, n + 1)
                    ffn_piece(f_start + pieces[0] // FF_PIECES, pieces[0] // FF_PIECES, pieces[0] % FF_PIECES, wide)
                    if n > 0:
                        divide(last, n - 1)
                    for piece in pieces[1:]:
                        ffn_piece(f_start + piece // FF_PIECES, piece // FF_PIECES, piece % FF_PIECES, wide)
                divide(last, LPAIRS - 1)
                add_output(last, B - 1)
                f_last = f_start + (FF_STEPS - 1)
                copy_ff(f_last, FF_STEPS - 1)
                copy_z(ahead, 0)
                scale_tables(layer + 1)
                for n in range(CHUNKS):
                    ffn_piece(f_last, FF_STEPS - 1, (1, 3, 5, 6)[n], score_psum)
                    rotate(ahead, n)
                    norms(ahead, n)
                    if n == 1:
                        ffn_piece(f_last, FF_STEPS - 1, 4, score_psum)
            nc.vector.scalar_tensor_tensor(chip.x[:, :, :], z[:, :, :], 0.5, chip.x[:, :, :], ALU.mult, ALU.add)
    att.ended(DEPTH * B)
    att.ended(1, STACK_AHEAD)
    ffn.ended(DEPTH * FF_STEPS)
    layer_sig.ended(DEPTH)
    layer_sig.ended(1, ("qkv_weights", "tables"))


def layer_view(a, layer):
    part = a[bass.ds(layer, 1)]
    names = " ".join("cde"[:len(a.shape) - 2])
    return part.rearrange(f"a p {names} -> (a p) {names}")


def loop_signals():
    stages = [moe_signals(gated, 1) for gated in (False, True)] + [attention_signals(level) for level in (0, 2, 3)]
    return sorted(set().union(*stages, L1_FFN_SIGNALS, RW_SIGNALS, STACK_ATTENTION))


def program(nc, dram, out, stages):
    with ExitStack() as ctx:
        chip = Chip(nc, ctx, dram, loop_signals())
        cossin = ctx.enter_context(nc.sbuf_tensor("cossin", [P, 2, D], F32))
        begin = chip.once
        begin.use(dict(loaded=32, set=1))
        with nc.Block() as block:
            @block.sync
            def _(sp):
                sp.dma_start(chip.x[:, :, :], dram["x"].rearrange("b (h p) d -> p (b h) d", p=P)).then_inc(begin["loaded"], 16)
                sp.dma_start(chip.ident[:, :], dram["ident"]).then_inc(begin["loaded"], 16)
                sp.wait_ge(*begin("loaded", 1))

            @block.gpsimd
            def _(pool):
                chip.loop.seed(pool)
                chip.ffn.seed(pool)

            @block.vector
            def _(dve):
                nc.vector.memset(chip.minus_half[:, :], -0.5).then_inc(begin["set"], 1)
                dve.wait_ge(*begin("set", 1))
        begin.ended(1)
        setup_l1_angles(chip, cossin)
        for number, (level, part) in enumerate(stages):
            chip.tag = f"stage{number}_"
            if part == "attention" and level == 1:
                stage_rwkv(chip)
            elif part == "attention":
                stage_attention(chip, level)
            elif level == 1:
                stage_l1_ffn(chip, cossin)
            elif level == 2:
                stage_stack(chip)
            else:
                stage_moe(chip, level)
        end = chip.once
        end.use(dict(loaded=16))
        with nc.Block() as block:
            @block.sync
            def _(sp):
                sp.dma_start(out.rearrange("b (h p) d -> p (b h) d", p=P), chip.x[:, :, :]).then_inc(end["loaded"], 16)
                sp.wait_ge(*end("loaded", 1))


STAGES = [(level, part) for level in range(4) for part in ("ffn", "attention", "ffn")]


def kernel(**inputs):
    import concourse.bacc as bacc
    from concourse.bass_utils import run_bass_kernel_spmd

    nc = bacc.Bacc("TRN2", target_bir_lowering=False, num_devices=1)
    arrays, dram = {}, {}
    for name, a in layout(inputs).items():
        a = np.ascontiguousarray(a)
        arrays["in_" + name] = a
        dram[name] = nc.dram_tensor("in_" + name, a.shape, mybir.dt.from_np(a.dtype), kind="ExternalInput").ap()
    out = nc.dram_tensor("out", (B, SEQ, D), F32, kind="ExternalOutput").ap()
    program(nc, dram, out, STAGES)
    r = run_bass_kernel_spmd(nc, [arrays], core_ids=[0])
    return r.results[0]["out"]


def layout(inputs):
    w = {name: np.asarray(a) for name, a in inputs.items()}
    a = {"x": w["L0_attn_embeddings"], "ident": np.eye(P, dtype=np.float32)}
    for name in ("L1_ffn_theta", "L1_ffn_phi", "L1_ffn_theta_noise", "L1_ffn_phi_noise"):
        a[name] = w[name]
    rows = lambda v: np.broadcast_to(v, (P,) + v.shape)
    a["iota"] = rows(np.arange(EXPERTS, dtype=np.float32))
    split = lambda v: v.reshape(v.shape[0], -1, P, v.shape[-1]).transpose(2, 0, 1, 3)
    a["L0_w_gate"], a["L0_b_gate"] = w["L0_ffn_Wr"].T, rows(w["L0_ffn_br"])
    a["L0_w_up"] = w["L0_ffn_W1"].transpose(2, 0, 1)
    a["L0_b_up"] = w["L0_ffn_b1"].reshape(EXPERTS, -1, P).transpose(2, 0, 1)
    a["L0_w_down"] = split(w["L0_ffn_W2"].transpose(0, 2, 1))
    a["L0_b_down"] = w["L0_ffn_b2"]
    a["L0_gamma"], a["L0_beta"] = rows(w["L0_ffn_gamma"]), rows(w["L0_ffn_beta"])
    a["L3_w_gate"] = w["L3_ffn_gate_kernel"]
    a["L3_w_up"], a["L3_w_up2"] = (w[n].transpose(1, 0, 2) for n in ("L3_ffn_w0_kernel", "L3_ffn_w1_kernel"))
    a["L3_w_down"] = split(w["L3_ffn_wo_kernel"])
    attention_layout(w, a, rows)
    rwkv_layout(w, a)
    stack_layout(w, a)
    return a


def attention_layout(w, a, rows):
    bf16 = mybir.dt.np(BF16)
    a["ident_bf"] = np.eye(P, dtype=np.float32).astype(bf16)
    above = np.triu(np.full((P, P), MASKED, np.float32), 1)
    a["mask"], a["maskT"] = above.astype(bf16), np.ascontiguousarray(above.T).astype(bf16)

    def banded(v, ninth=0.0):
        out = np.zeros((v.shape[0], GROUPS, GROUPS, BAND), np.float32)
        out[..., :DK] = v.reshape(v.shape[0], GROUPS, GROUPS, DK)
        out[..., DK] = ninth
        return out.reshape(v.shape[0], GROUPS, P)

    pairs = np.arange(D) ^ 1
    heads = lambda v: v.transpose(1, 0, 2).reshape(D, D)
    q0, k0, v0 = (w["L0_attn_W" + n] for n in "qkv")
    a["A0_wq"], a["A0_wk"], a["A0_wv"] = banded(heads(q0)), banded(heads(k0)), heads(v0)
    a["A0_bq"] = banded(w["L0_attn_bq"].reshape(1, D))[0].T
    a["A0_bk"] = banded(w["L0_attn_bk"].reshape(1, D), 1.0)[0].T
    a["A0_bv"], a["A0_wo"], a["A0_bo"] = rows(w["L0_attn_bv"].reshape(D)), w["L0_attn_Wo"], rows(w["L0_attn_bo"])
    q2, k2, v2 = (w["L2_attn_w_qkv"][:, n * D:(n + 1) * D] for n in range(3))
    bq2, bk2, bv2 = (w["L2_attn_b_qkv"][n * D:(n + 1) * D] for n in range(3))
    a["A2_wq"], a["A2_wk"], a["A2_wv"] = banded(q2), banded(k2), v2
    a["A2_bq"], a["A2_bk"], a["A2_bv"] = banded(bq2.reshape(1, D))[0].T, banded(bk2.reshape(1, D), 1.0)[0].T, rows(bv2)
    a["A2_wo"], a["A2_bo"] = w["L2_attn_w_out"], rows(w["L2_attn_b_out"])
    a["A2_gamma"], a["A2_beta"] = w["L2_attn_ln_gamma"].reshape(D, 1), w["L2_attn_ln_beta"].reshape(D, 1)
    q3, k3, v3 = (w["L3_attn_Wqkv"][:, n * D:(n + 1) * D] for n in range(3))
    a["A3_wq"], a["A3_wk"], a["A3_wv"] = banded(q3), banded(k3), v3
    a["A3_wq_swap"], a["A3_wk_swap"] = banded(q3[:, pairs]), banded(k3[:, pairs])
    a["A3_wo"], a["A3_bo"] = w["L3_attn_Wout"], rows(w["L3_attn_bout"])
    theta = np.power(np.float32(10000.0), (-2.0 * (np.arange(DK // 2, dtype=np.float32) - 1.0) / DK).astype(np.float32))
    angle = (np.arange(SEQ, dtype=np.float32)[:, None] * theta.astype(np.float32)[None, :]).astype(np.float64)
    sign = np.tile([-1.0, 1.0], DK // 2)
    tables = [np.repeat(np.cos(angle), 2, axis=1), np.repeat(np.sin(angle), 2, axis=1) * sign]
    a["A3_rope"] = np.stack([banded(np.tile(t, HEADS).astype(np.float32))[:, 0].T for t in tables], axis=1)


def rwkv_layout(w, a):
    column = lambda v: v.reshape(D, 1)
    a["RW_miu_x"], a["RW_td_miu"], a["RW_u"] = (column(w["L1_attn_" + n]) for n in ("miu_x", "td_miu", "u"))
    a["RW_gamma"], a["RW_beta"] = column(w["L1_attn_gn_gamma"]), column(w["L1_attn_gn_beta"])
    a["RW_lambda"] = w["L1_attn_lambda_"].reshape(MIXES, D).T
    a["RW_A"], a["RW_B"] = w["L1_attn_A_lora"], w["L1_attn_B_lora"].transpose(1, 0, 2)
    a["RW_td_A"], a["RW_td_B"] = w["L1_attn_td_A"], w["L1_attn_td_B"]
    for n in "rkvgo":
        a["RW_w" + n] = w["L1_attn_W" + n].T
    head = np.arange(P) // HS
    a["RW_head_ones"] = (head[:, None] == head[None, :]).astype(np.float32)
    gather = np.zeros((P, P + HS - 1), np.float32)
    gather[np.arange(P), head * HS + HS - 1] = 1.0
    a["RW_gather"] = gather


def stack_layout(w, a):
    t = {n: w["L2_ffn_" + n] for n in ("Wqkv", "q_scale", "k_scale", "Wo", "ln_g", "ln_b", "W1", "b1", "W2", "b2")}
    depth = t["Wqkv"].shape[0]
    a["T_wqkv"] = np.concatenate([t["Wqkv"], t["Wqkv"][-1:]])
    a["T_wo"] = t["Wo"].reshape(depth, LPAIRS, P, D).transpose(0, 2, 1, 3)
    a["T_w1"] = t["W1"]
    w2 = np.zeros((depth, FF_CHUNKS * P, D), np.float32)
    w2[:, :FF] = t["W2"]
    a["T_w2"] = w2.reshape(depth, FF_CHUNKS, P, D).transpose(0, 2, 1, 3)
    b1 = np.zeros((depth, 2, FF_CHUNKS * P), np.float32)
    b1[:, :, :FF] = t["b1"].reshape(depth, 2, FF)
    b1 = b1.reshape(depth, 2 * FF_CHUNKS, P).transpose(0, 2, 1)
    a["T_cols"] = np.concatenate([b1, t["ln_g"][:, :, None], t["ln_b"][:, :, None]], axis=2)
    a["T_b2"] = np.broadcast_to(t["b2"][:, None, None, :], (depth, P, 1, D))
    swap = lambda v: np.roll(v, LD // 2, axis=-1)
    scales = np.stack([t["q_scale"], swap(t["q_scale"]), t["k_scale"], swap(t["k_scale"])], axis=1)
    a["T_rows"] = np.broadcast_to(np.concatenate([scales, scales[-1:]])[:, None, :, None, :], (depth + 1, P, 4, 1, LD))
    half = np.arange(0, LD, 2, dtype=np.float32)
    inv_freq = (1.0 / np.power(np.float32(10000.0), half / LD)).astype(np.float32)
    n = np.arange(SEQ, dtype=np.float32)
    freqs = (n[:, None] * inv_freq[None, :]).astype(np.float64)
    factor = ((half + 0.4 * LD) / (1.4 * LD)).astype(np.float64)[None, :] ** ((n - SEQ // 2) / (WINDOW // 2))[:, None]
    cos, sin, factor = (np.concatenate([v, v], axis=1) for v in (np.cos(freqs), np.sin(freqs), factor))
    sin = sin * np.where(np.arange(LD) < LD // 2, -1.0, 1.0)
    base = np.stack([8 * cos * factor, 8 * sin * factor, cos / factor, sin / factor])
    a["T_base"] = base.astype(np.float32).reshape(4, HALVES, P, LD).transpose(2, 0, 1, 3)
    q = np.arange(P)[:, None, None]
    key = np.arange(REACH)[None, None, :] - WINDOW
    seen = (key <= q) & (key >= q - WINDOW) & ((np.arange(HALVES)[None, :, None] > 0) | (key >= 0))
    a["T_band"] = np.where(seen, 0.0, MASKED).astype(mybir.dt.np(BF16))
```

```python
from contextlib import ExitStack

import numpy as np
import concourse.bass as bass
from concourse import mybir

ALU = mybir.AluOpType
ACT = mybir.ActivationFunctionType
AX = mybir.AxisListType
F32 = mybir.dt.float32
BF16 = mybir.dt.bfloat16
U32 = mybir.dt.uint32

P = 128
D = 128
B, SEQ = 8, 256
TILES = B * SEQ // P
HALVES = SEQ // P
HEADS, DK = 16, 8
EPS = 1e-5
MASKED = -1e30


class Signals:

    def __init__(self, nc, ctx, stage, seeded=False, **per):
        names = list(per) + ["apart"] * ("apart" not in per)
        self.sems = {name: ctx.enter_context(nc.semaphore(stage + "_" + name)) for name in names}
        self.per = per
        self.base = {name: int(seeded) for name in per}

    def __getitem__(self, name):
        return self.sems[name]

    def __call__(self, name, step, k=0):
        return self.sems[name], step * self.per[name] + (self.base[name] + k)

    def use(self, per):
        assert set(per) <= set(self.sems)
        self.per = per

    def seed(self, eng):
        for sem in self.sems.values():
            eng.sem_inc(sem, 1)

    def apart(self, eng, name, step, k):
        eng.wait_ge(*self(name, step, k))
        self.settle(eng)

    def settle(self, eng):
        eng.sem_inc(self.sems["apart"], 1)

    def ended(self, steps, names=None):
        for name in names or self.per:
            self.base[name] += self.per[name] * steps


class Chain:

    def __init__(self, eng, signals, name, step):
        self.eng, self.signals, self.name, self.step, self.n = eng, signals, name, step, 0

    def __call__(self, ins):
        ins.then_inc(self.signals[self.name], 1)
        self.n += 1
        self.eng.wait_ge(*self.signals(self.name, self.step, self.n))

    def apart(self, ins):
        ins.then_inc(self.signals[self.name], 1)
        self.n += 1
        self.signals.apart(self.eng, self.name, self.step, self.n)

    def done(self):
        assert self.n == self.signals.per[self.name], (self.name, self.n)


class Chip:

    def __init__(self, nc, ctx, dram, loop_names):
        self.nc, self.ctx, self.dram = nc, ctx, dram
        self.tag = ""
        self.loop = Signals(nc, ctx, "loop", seeded=True, **dict.fromkeys(loop_names, 0))
        self.ffn = Signals(nc, ctx, "ffn", seeded=True, **STACK_FFN)
        self.once = Signals(nc, ctx, "once", **dict.fromkeys(["loaded", "set", "reduced", "chain"] + [f"experts{n}" for n in range(LOADS)], 0))
        self.layer = Signals(nc, ctx, "layer", **STACK_LAYER)
        self.x = ctx.enter_context(nc.sbuf_tensor("x_all", [P, TILES, D], F32))
        self.ident = ctx.enter_context(nc.sbuf_tensor("ident", [P, P], F32))
        self.minus_half = ctx.enter_context(nc.sbuf_tensor("minus_half", [P, 1], F32))


NORM_SIGNALS = dict(norm_chain=1, moments=1, var=1, rstd=1, xn=1, xT_psum=1, xT=1)


class Norm:
    def __init__(self, chip, ctx, tiles, turned=True):
        self.tiles = tiles
        sb = lambda name, shape: ctx.enter_context(chip.nc.sbuf_tensor(chip.tag + "norm_" + name, shape, F32))
        self.stats = sb("stats", [P, tiles, 6])
        self.moments = sb("moments", [P, tiles, 2])
        self.var = sb("var", [P, tiles])
        self.rstd = sb("rstd", [P, tiles])
        if not turned:
            return
        self.xn = sb("xn", [P, tiles, D])
        self.xT = sb("xT", [P, tiles * P])
        self.psum = ctx.enter_context(chip.nc.psum_tensor(chip.tag + "norm_psum", [P, 512], F32))


def norm_vector(nc, dve, sig, m, step, source, target, used, which="", settled=()):
    T = m.tiles
    for t in range(T):
        ins = nc.vector.bn_stats(m.stats[:, t, :], source(t))
    ins.then_inc(sig["norm_chain" + which], 1)
    sig.apart(dve, "norm_chain" + which, step, 1)
    for t in range(T):
        ins = nc.vector.bn_aggr(m.moments[:, t, :], m.stats[:, t, :])
    ins.then_inc(sig["moments" + which], 1)
    dve.wait_ge(*sig("moments" + which, step, 1))
    nc.vector.tensor_scalar(m.var[:, :], m.moments[:, :, 1], EPS, None, ALU.add).then_inc(sig["var" + which], 1)
    dve.wait_ge(*sig("rstd" + which, step, 1))
    for name in used:
        dve.wait_ge(*sig(name, step))
    for wait in settled:
        dve.wait_ge(*wait)
    for t in range(T):
        ins = nc.vector.tensor_scalar(target(t), source(t), m.moments[:, t, 0:1], m.rstd[:, t:t + 1],
                                      ALU.subtract, ALU.mult)
    ins.then_inc(sig["xn" + which], 1)


def norm_rstd(nc, pool, sig, chip, m, step, which=""):
    pool.wait_ge(*sig("var" + which, step, 1))
    nc.gpsimd.tensor_tensor(m.rstd[:, :], m.var[:, :], chip.minus_half[:, :].to_broadcast([P, m.tiles]), ALU.pow)\
      .then_inc(sig["rstd" + which], 1)


def norm_transpose(nc, pe, sig, chip, m, step):
    pe.wait_ge(*sig("xn", step, 1))
    pe.wait_ge(*sig("xT", step))
    for t in range(m.tiles):
        ins = nc.tensor.transpose(m.psum[:, t * P:(t + 1) * P], m.xn[:, t, :], chip.ident[:, :])
    ins.then_inc(sig["xT_psum"], 1)


def norm_xT(nc, act, sig, m, step, xT_used):
    act.wait_ge(*sig("xT_psum", step, 1))
    for name in xT_used:
        act.wait_ge(*sig(name, step))
    nc.scalar.activation(m.xT[:, :], m.psum[:, 0:m.tiles * P], ACT.Copy).then_inc(sig["xT"], 1)


def x_tile(chip, step, tiles):
    return lambda t: chip.x[:, bass.ds(step * tiles + t, 1), :].rearrange("p a d -> p (a d)")


TWO_PI = 2 * np.pi
TWO_PI_1 = 6.28125
TWO_PI_2 = float(np.float32(np.round((TWO_PI - TWO_PI_1) * 2 ** 20) / 2 ** 20))
TWO_PI_3 = TWO_PI - TWO_PI_1 - TWO_PI_2
ROUNDER = 1.5 * 2 ** 23
PI_BELOW = 3.1415925


def setup_l1_angles(chip, cossin):
    nc = chip.nc
    with ExitStack() as ctx:
        sb = lambda name, shape: ctx.enter_context(nc.sbuf_tensor("angle_" + name, shape, F32))
        parts, angle, turns = sb("parts", [P, 4, D]), sb("sum", [P, 2, D]), sb("turns", [P, 2, D])
        sig = chip.once
        sig.use(dict(loaded=64, chain=10, reduced=1, set=1))
        block = ctx.enter_context(nc.Block())

        @block.sync
        def _(sp):
            for n, name in enumerate(["L1_ffn_theta", "L1_ffn_phi", "L1_ffn_theta_noise", "L1_ffn_phi_noise"]):
                sp.dma_start(parts[:, n, :], chip.dram[name]).then_inc(sig["loaded"], 16)

        @block.vector
        def _(dve):
            chain = Chain(dve, sig, "chain", 0)
            dve.wait_ge(*sig("loaded", 1))
            chain(nc.vector.tensor_tensor(angle[:, :, :], parts[:, 0:2, :], parts[:, 2:4, :], ALU.add))
            chain(nc.vector.tensor_scalar(turns[:, 0, :], angle[:, 0, :], 1 / TWO_PI, 0.25, ALU.mult, ALU.add))
            chain(nc.vector.tensor_scalar(turns[:, 1, :], angle[:, 1, :], 1 / TWO_PI, None, ALU.mult))
            chain(nc.vector.tensor_scalar(turns[:, :, :], turns[:, :, :], ROUNDER, None, ALU.add))
            chain(nc.vector.tensor_scalar(turns[:, :, :], turns[:, :, :], ROUNDER, None, ALU.subtract))
            for part in (TWO_PI_1, TWO_PI_2, TWO_PI_3):
                chain(nc.vector.scalar_tensor_tensor(angle[:, :, :], turns[:, :, :], -part, angle[:, :, :], ALU.mult, ALU.add))
            chain(nc.vector.tensor_scalar(angle[:, 0, :], angle[:, 0, :], np.pi / 2, None, ALU.add))
            chain(nc.vector.tensor_scalar(angle[:, :, :], angle[:, :, :], PI_BELOW, -PI_BELOW, ALU.min, ALU.max))
            chain.done()
            nc.vector.engine_nop().then_inc(sig["reduced"], 1)

        @block.scalar
        def _(act):
            act.wait_ge(*sig("reduced", 1))
            nc.scalar.activation(cossin[:, :, :], angle[:, :, :], ACT.Sin).then_inc(sig["set"], 1)
            act.wait_ge(*sig("set", 1))
    sig.ended(1)


def stage_l1_ffn(chip, cossin):
    nc, sig = chip.nc, chip.loop
    sig.use(L1_FFN_SIGNALS)
    T = 4
    with ExitStack() as ctx:
        m = Norm(chip, ctx, T)
        squares = ctx.enter_context(nc.sbuf_tensor(chip.tag + "squares", [P, T, 2, D], F32))
        norm2 = ctx.enter_context(nc.sbuf_tensor(chip.tag + "norm2", [P, T, D], F32))
        waves = ctx.enter_context(nc.psum_tensor(chip.tag + "waves", [P, T, 2, D], F32))
        block = ctx.enter_context(nc.Block())
        steps = TILES // T

        @block.vector
        def _(dve):
            with dve.Fori(0, steps) as step:
                norm_vector(nc, dve, sig, m, step, x_tile(chip, step, T), lambda t: m.xn[:, t, :], ["xT_psum"])
                dve.wait_ge(*sig("squares", step, 1))
                nc.vector.tensor_tensor(norm2[:, :, :], squares[:, :, 0, :], squares[:, :, 1, :], ALU.add)\
                  .then_inc(sig["norm2"], 1)
                dve.wait_ge(*sig("root", step, 1))
                x = chip.x[:, bass.ds(step * T, T), :]
                nc.vector.scalar_tensor_tensor(x, norm2[:, :, :], 0.5, x, ALU.mult, ALU.add).then_inc(sig["x"], 1)
                dve.wait_ge(*sig("x", step, 1))

        @block.scalar
        def _(act):
            with act.Fori(0, steps) as step:
                norm_xT(nc, act, sig, m, step, ["waves"])
                act.wait_ge(*sig("waves", step, 1))
                act.wait_ge(*sig("norm2", step))
                nc.scalar.activation(squares[:, :, :, :], waves[:, :, :, :], ACT.Square).then_inc(sig["squares"], 1)
                act.wait_ge(*sig("norm2", step, 1))
                nc.scalar.activation(norm2[:, :, :], norm2[:, :, :], ACT.Sqrt).then_inc(sig["root"], 1)

        @block.gpsimd
        def _(pool):
            with pool.Fori(0, steps) as step:
                norm_rstd(nc, pool, sig, chip, m, step)

        @block.tensor
        def _(pe):
            with pe.Fori(0, steps) as step:
                norm_transpose(nc, pe, sig, chip, m, step)
                pe.wait_ge(*sig("xT", step, 1))
                pe.wait_ge(*sig("squares", step))
                for t in range(T):
                    ins = nc.tensor.matmul(waves[:, t, :, :], m.xT[:, t * P:(t + 1) * P], cossin[:, :, :],
                                           start=True, stop=True)
                ins.then_inc(sig["waves"], 1)
    sig.ended(steps)


L1_FFN_SIGNALS = dict(NORM_SIGNALS, waves=1, squares=1, norm2=1, root=1, x=1)


EXPERTS = 8
TOKEN_TILES = 4
LOADS = 4


def moe_signals(gated, chunks):
    per = dict(NORM_SIGNALS, logits=1, routed=1, top=1, gap=1, exp_gap=1, h_psum=EXPERTS * chunks,
               hidden=EXPERTS * chunks, o_psum=EXPERTS, mixed=EXPERTS, x=1 if gated else 2, route_chain=10)
    if gated:
        per.update(silu=EXPERTS * chunks)
    else:
        per.update(rwT_psum=1, rwT=1, bias_psum=1, moments2=1, var2=1, rstd2=1, out_chain=5, )
    return per


def stage_moe(chip, level):
    nc, T = chip.nc, TOKEN_TILES
    sig, loaded = chip.loop, chip.once
    gated = level == 3
    F = 256 if gated else 512
    chunks, width = F // P, T * P
    banks = 2
    steps = TILES // T
    dram = chip.dram
    sig.use(moe_signals(gated, chunks))
    loaded.use(moe_loads(level))
    with ExitStack() as ctx:
        sb = lambda name, shape, dt=F32: ctx.enter_context(nc.sbuf_tensor(chip.tag + name, shape, dt))
        ps = lambda name, shape: ctx.enter_context(nc.psum_tensor(chip.tag + name, shape, F32))
        m = Norm(chip, ctx, T)
        w_up = sb("w_up", [P, EXPERTS, F])
        w_up2 = sb("w_up2", [P, EXPERTS, F]) if gated else None
        w_down = sb("w_down", [P, EXPERTS, chunks, D])
        w_gate = sb("w_gate", [P, EXPERTS])
        iota = sb("iota", [P, EXPERTS])
        if not gated:
            b_gate, b_up, b_down = sb("b_gate", [P, EXPERTS]), sb("b_up", [P, EXPERTS, chunks]), sb("b_down", [EXPERTS, D])
            gamma, beta = sb("gamma", [P, D]), sb("beta", [P, D])
            rwT = sb("rwT", [EXPERTS, width])
            stats2, moments2, var2, rstd2 = sb("stats2", [P, T, 6]), sb("moments2", [P, T, 2]), sb("var2", [P, T]), sb("rstd2", [P, T])
        hidden = sb("hidden", [P, 2, chunks, width])
        silu = sb("silu", [P, 2, width]) if gated else None
        logits, top = sb("logits", [P, T, EXPERTS]), sb("top", [P, T, 8])
        index, indexf = sb("index", [P, T, 8], U32), sb("indexf", [P, T, 8])
        gap, weights = sb("gap", [P, T, 1]), sb("weights", [P, T, 2])
        pick, route = sb("pick", [P, T, EXPERTS]), sb("route", [P, T, EXPERTS])
        mix = sb("mix", [P, T, D])
        logits_psum = ps("logits_psum", [P, 512])
        h_psum = [ps(f"h_psum{n}", [P, width]) for n in range(banks)]
        h2_psum = [ps(f"h2_psum{n}", [P, width]) for n in range(banks)] if gated else None
        o_psum = [ps(f"o_psum{n}", [P, T, D]) for n in range(2)]
        lg = logits_psum[:, 0:T * EXPERTS].rearrange("p (t e) -> p t e", t=T)
        x_of = lambda step: chip.x[:, bass.ds(step * T, T), :]
        block = ctx.enter_context(nc.Block())

        @block.sync
        def _(sp):
            names = [("w_gate", w_gate), ("iota", iota)]
            if not gated:
                names += [("b_gate", b_gate), ("b_up", b_up), ("b_down", b_down), ("gamma", gamma), ("beta", beta)]
            for name, tile in names:
                src = dram["iota"] if name == "iota" else dram[f"L{level}_{name}"]
                sp.dma_start(tile[:], src).then_inc(loaded["loaded"], 16)
            for n in range(LOADS):
                e = slice(n * EXPERTS // LOADS, (n + 1) * EXPERTS // LOADS)
                sp.dma_start(w_up[:, e, :], dram[f"L{level}_w_up"][:, e, :]).then_inc(loaded[f"experts{n}"], 16)
                if gated:
                    sp.dma_start(w_up2[:, e, :], dram[f"L{level}_w_up2"][:, e, :]).then_inc(loaded[f"experts{n}"], 16)
                sp.dma_start(w_down[:, e, :, :], dram[f"L{level}_w_down"][:, e, :, :]).then_inc(loaded[f"experts{n}"], 16)

        @block.tensor
        def _(pe):
            pe.wait_ge(*loaded("loaded", 1))
            with pe.Fori(0, steps) as step:
                if not gated:
                    pe.wait_ge(*sig("rwT", step))
                norm_transpose(nc, pe, sig, chip, m, step)
                pe.wait_ge(*sig("xT", step, 1))
                pe.wait_ge(*sig("top", step))
                for t in range(T):
                    ins = nc.tensor.matmul(lg[:, t, :], m.xT[:, t * P:(t + 1) * P], w_gate[:, :], start=True, stop=True)
                ins.then_inc(sig["logits"], 1)

                def down(e):
                    pe.wait_ge(*sig("hidden", step, (e + 1) * chunks))
                    pe.wait_ge(*sig("mixed", step, max(e - 1, 0)))
                    for t in range(T):
                        for c in range(chunks):
                            ins = nc.tensor.matmul(o_psum[e % 2][:, t, :], hidden[:, e % 2, c, t * P:(t + 1) * P],
                                                   w_down[:, e, c, :], start=c == 0, stop=c == chunks - 1)
                    ins.then_inc(sig["o_psum"], 1)

                for e in range(EXPERTS):
                    pe.wait_ge(*loaded(f"experts{e * LOADS // EXPERTS}", 1))
                    for c in range(chunks):
                        n = e * chunks + c
                        pe.wait_ge(*sig("hidden", step, max(n - banks + 1, 0)))
                        ins = nc.tensor.matmul(h_psum[n % banks][:, :], w_up[:, e, c * P:(c + 1) * P], m.xT[:, :],
                                               start=True, stop=True)
                        if gated:
                            ins = nc.tensor.matmul(h2_psum[n % banks][:, :], w_up2[:, e, c * P:(c + 1) * P], m.xT[:, :],
                                                   start=True, stop=True)
                        ins.then_inc(sig["h_psum"], 1)
                    if e:
                        down(e - 1)
                down(EXPERTS - 1)
                if not gated:
                    pe.wait_ge(*sig("routed", step, 1))
                    for t in range(T):
                        ins = nc.tensor.transpose(m.psum[0:EXPERTS, t * P:(t + 1) * P], route[:, t, :], chip.ident[:, :])
                    ins.then_inc(sig["rwT_psum"], 1)
                    pe.wait_ge(*sig("rwT", step, 1))
                    pe.wait_ge(*sig("mixed", step, EXPERTS - 1))
                    for t in range(T):
                        ins = nc.tensor.matmul(o_psum[0][:, t, :], rwT[:, t * P:(t + 1) * P], b_down[:, :], start=True, stop=True)
                    ins.then_inc(sig["bias_psum"], 1)

        @block.scalar
        def _(act):
            act.wait_ge(*loaded("loaded", 1))
            with act.Fori(0, steps) as step:
                norm_xT(nc, act, sig, m, step, ["h_psum", "logits"])
                act.wait_ge(*sig("gap", step, 1))
                nc.scalar.activation(weights[:, :, 1:2], gap[:, :, :], ACT.Exp).then_inc(sig["exp_gap"], 1)
                for e in range(EXPERTS):
                    if not gated:
                        act.wait_ge(*sig("o_psum", step, max(e - 1, 0)))
                    for c in range(chunks):
                        n = e * chunks + c
                        act.wait_ge(*sig("h_psum", step, n + 1))
                        if gated:
                            act.wait_ge(*sig("hidden", step, max(n - 1, 0)))
                            nc.scalar.activation(silu[:, n % 2, :], h_psum[n % banks][:, :], ACT.Silu)\
                              .then_inc(sig["silu"], 1)
                        else:
                            nc.scalar.activation(hidden[:, e % 2, c, :], h_psum[n % banks][:, :], ACT.Relu,
                                                 bias=b_up[:, e, c:c + 1]).then_inc(sig["hidden"], 1)
                if not gated:
                    act.wait_ge(*sig("rwT_psum", step, 1))
                    act.wait_ge(*sig("bias_psum", step))
                    nc.scalar.activation(rwT[:, :], m.psum[0:EXPERTS, :], ACT.Copy).then_inc(sig["rwT"], 1)

        @block.gpsimd
        def _(pool):
            with pool.Fori(0, steps) as step:
                norm_rstd(nc, pool, sig, chip, m, step)
                if not gated:
                    pool.wait_ge(*sig("var2", step, 1))
                    nc.gpsimd.tensor_tensor(rstd2[:, :], var2[:, :], chip.minus_half[:, :].to_broadcast([P, T]), ALU.pow)\
                      .then_inc(sig["rstd2"], 1)

        @block.vector
        def _(dve):
            dve.wait_ge(*loaded("loaded", 1))
            with dve.Fori(0, steps) as step:
                norm_vector(nc, dve, sig, m, step, x_tile(chip, step, T), lambda t: m.xn[:, t, :], ["xT_psum"])
                chain = Chain(dve, sig, "route_chain", step)
                dve.wait_ge(*sig("logits", step, 1))
                if gated:
                    ins = nc.vector.tensor_copy(logits[:, :, :], lg)
                else:
                    ins = nc.vector.tensor_tensor(logits[:, :, :], lg, b_gate[:, :].rearrange("p (a e) -> p a e", a=1).to_broadcast([P, T, EXPERTS]), ALU.add)
                ins.then_inc(sig["top"], 1)
                sig.apart(dve, "top", step, 1)
                for t in range(T):
                    ins = nc.vector.max(top[:, t, :], logits[:, t, :])
                chain.apart(ins)
                for t in range(T):
                    ins = nc.vector.max_index(index[:, t, :], top[:, t, :], logits[:, t, :])
                chain(ins)
                nc.vector.tensor_tensor(gap[:, :, :], top[:, :, 1:2], top[:, :, 0:1], ALU.subtract).then_inc(sig["gap"], 1)
                chain(nc.vector.tensor_copy(indexf[:, :, :], index[:, :, :]))
                dve.wait_ge(*sig("exp_gap", step, 1))
                chain(nc.vector.tensor_scalar(weights[:, :, 0:1], weights[:, :, 1:2], 1.0, None, ALU.add))
                chain(nc.vector.reciprocal(weights[:, :, 0:1], weights[:, :, 0:1]))
                chain(nc.vector.tensor_tensor(weights[:, :, 1:2], weights[:, :, 1:2], weights[:, :, 0:1], ALU.mult))
                every = [P, T, EXPERTS]
                ids = iota[:, :].rearrange("p (a e) -> p a e", a=1).to_broadcast(every)
                chain(nc.vector.tensor_tensor(route[:, :, :], ids, indexf[:, :, 0:1].to_broadcast(every), ALU.is_equal))
                chain(nc.vector.tensor_tensor(pick[:, :, :], ids, indexf[:, :, 1:2].to_broadcast(every), ALU.is_equal))
                chain(nc.vector.tensor_tensor(route[:, :, :], route[:, :, :], weights[:, :, 0:1].to_broadcast(every), ALU.mult))
                chain(nc.vector.tensor_tensor(pick[:, :, :], pick[:, :, :], weights[:, :, 1:2].to_broadcast(every), ALU.mult))
                nc.vector.tensor_tensor(route[:, :, :], route[:, :, :], pick[:, :, :], ALU.add).then_inc(sig["routed"], 1)
                dve.wait_ge(*sig("routed", step, 1))

                def mix_in(e):
                    dve.wait_ge(*sig("o_psum", step, e + 1))
                    if e:
                        dve.wait_ge(*sig("mixed", step, e))
                    for t in range(T):
                        if e == 0:
                            ins = nc.vector.tensor_scalar(mix[:, t, :], o_psum[0][:, t, :], route[:, t, e:e + 1], None, ALU.mult)
                        else:
                            ins = nc.vector.scalar_tensor_tensor(mix[:, t, :], o_psum[e % 2][:, t, :], route[:, t, e:e + 1],
                                                                 mix[:, t, :], ALU.mult, ALU.add)
                    ins.then_inc(sig["mixed"], 1)

                for e in range(EXPERTS):
                    if gated:
                        dve.wait_ge(*sig("o_psum", step, max(e - 1, 0)))
                        for c in range(chunks):
                            n = e * chunks + c
                            dve.wait_ge(*sig("silu", step, n + 1))
                            nc.vector.tensor_tensor(hidden[:, e % 2, c, :], silu[:, n % 2, :], h2_psum[n % banks][:, :],
                                                    ALU.mult).then_inc(sig["hidden"], 1)
                        if e:
                            mix_in(e - 1)
                    else:
                        mix_in(e)
                if gated:
                    mix_in(EXPERTS - 1)
                    dve.wait_ge(*sig("mixed", step, EXPERTS))
                    nc.vector.scalar_tensor_tensor(x_of(step), mix[:, :, :], 0.5, x_of(step), ALU.mult, ALU.add).then_inc(sig["x"], 1)
                else:
                    out = Chain(dve, sig, "out_chain", step)
                    row = [P, T, D]
                    dve.wait_ge(*sig("mixed", step, EXPERTS))
                    dve.wait_ge(*sig("bias_psum", step, 1))
                    out(nc.vector.tensor_tensor(mix[:, :, :], mix[:, :, :], o_psum[0][:, :, :], ALU.add))
                    out(nc.vector.tensor_tensor(mix[:, :, :], mix[:, :, :], m.xn[:, :, :], ALU.add))
                    for t in range(T):
                        ins = nc.vector.bn_stats(stats2[:, t, :], mix[:, t, :])
                    out.apart(ins)
                    for t in range(T):
                        ins = nc.vector.bn_aggr(moments2[:, t, :], stats2[:, t, :])
                    ins.then_inc(sig["moments2"], 1)
                    dve.wait_ge(*sig("moments2", step, 1))
                    nc.vector.tensor_scalar(var2[:, :], moments2[:, :, 1], EPS, None, ALU.add).then_inc(sig["var2"], 1)
                    dve.wait_ge(*sig("rstd2", step, 1))
                    for t in range(T):
                        ins = nc.vector.tensor_scalar(mix[:, t, :], mix[:, t, :], moments2[:, t, 0:1], rstd2[:, t:t + 1],
                                                      ALU.subtract, ALU.mult)
                    out(ins)
                    out(nc.vector.tensor_tensor(mix[:, :, :], mix[:, :, :], gamma[:, :].rearrange("p (a d) -> p a d", a=1).to_broadcast(row), ALU.mult))
                    nc.vector.tensor_tensor(mix[:, :, :], mix[:, :, :], beta[:, :].rearrange("p (a d) -> p a d", a=1).to_broadcast(row), ALU.add)\
                      .then_inc(sig["x"], 1)
                    dve.wait_ge(*sig("x", step, 1))
                    nc.vector.scalar_tensor_tensor(x_of(step), mix[:, :, :], 0.5, x_of(step), ALU.mult, ALU.add).then_inc(sig["x"], 1)
                    out.done()
                dve.wait_ge(*sig("x", step, 1 if gated else 2))
                chain.done()
    sig.ended(steps)
    loaded.ended(1)


def moe_loads(level):
    small = 2 if level == 3 else 7
    return dict(loaded=16 * small, **{f"experts{n}": 16 * (3 if level == 3 else 2) for n in range(LOADS)})


GROUPS, BAND = 4, 32
AUG = DK + 1
PAIRS = HEADS // 2
ATTN_LOADS = {0: 11, 2: 13, 3: 11}


BESIDE = (1, 3, 0, 2, 5, 7, 4, 6)


def attention_signals(level):
    per = dict(NORM_SIGNALS, proj=GROUPS, proj_read=GROUPS, q_alone=GROUPS, k_alone=GROUPS, v_psum=1, v=1, scores=PAIRS, probs=PAIRS,
               ctx_psum=1, context=1, ctxT_psum=1, ctxT=1, out_psum=1, x=2, ctx_chain=1)
    if level == 3:
        per.update(rope=GROUPS, rope_chain=2 * GROUPS, den_scores=PAIRS, den_probs=PAIRS, den=PAIRS)
    else:
        per.update(max_scores=PAIRS, negmax=PAIRS, negmaxT=2, q_aug=2)
    if level == 2:
        per.update(norm_chain_a=1, moments_a=1, var_a=1, rstd_a=1, xn_a=1, residual=1)
    return per


def stage_attention(chip, level):
    nc, sig, once = chip.nc, chip.loop, chip.once
    causal, softmax = level != 2, level != 3
    scale = float(DK) ** -0.5
    dram = chip.dram
    T = HALVES
    sig.use(attention_signals(level))
    once.use(dict(loaded=16 * ATTN_LOADS[level], set=4 if softmax else 3))
    drained = "negmax" if softmax else "den_probs"
    with ExitStack() as ctx:
        sb = lambda name, shape, dt=F32: ctx.enter_context(nc.sbuf_tensor(chip.tag + name, shape, dt))
        ps = lambda name, shape: ctx.enter_context(nc.psum_tensor(chip.tag + name, shape, F32))
        m = Norm(chip, ctx, T)
        tiles = {"wq": sb("wq", [P, GROUPS, P]), "wk": sb("wk", [P, GROUPS, P]), "wv": sb("wv", [P, D]), "wo": sb("wo", [P, D]),
                 "bo": sb("bo", [P, D]), "ident_bf": sb("ident_bf", [P, P], BF16), "mask": sb("mask", [P, P], BF16),
                 "maskT": sb("maskT", [P, P], BF16)}
        if softmax:
            tiles.update(bq=sb("bq", [P, GROUPS]), bk=sb("bk", [P, GROUPS]), bv=sb("bv", [P, D]))
        else:
            tiles.update(wq_swap=sb("wq_swap", [P, GROUPS, P]), wk_swap=sb("wk_swap", [P, GROUPS, P]),
                         rope=sb("rope", [P, 2, SEQ]))
        if level == 2:
            tiles.update(gamma=sb("gamma", [P, 1]), beta=sb("beta", [P, 1]))
            x1 = sb("x1", [P, 2, T, D])
        assert len(tiles) == ATTN_LOADS[level]
        wq, wk, wv, wo, bo, ident_bf, mask, maskT = (tiles[n] for n in ("wq", "wk", "wv", "wo", "bo", "ident_bf", "mask", "maskT"))
        qk = sb("qk", [P, 2, 2, GROUPS, SEQ])
        q_alone = sb("q_alone", [P, GROUPS, GROUPS, SEQ])
        k_alone = sb("k_alone", [P, 2, GROUPS, GROUPS, SEQ])
        turned = None if softmax else sb("turned", [P, 2, 2, GROUPS, SEQ])
        turn = None if softmax else sb("turn", [P, 2, 2, SEQ])
        v = sb("v", [P, 2, T, HEADS, AUG])
        negmax = sb("negmax", [P, T, GROUPS, P]) if softmax else None
        probs = sb("probs", [P, T, HEADS, SEQ])
        den_exp = None if softmax else sb("den_exp", [P, 2, 2, T, SEQ])
        den = None if softmax else sb("den", [P, 2, T, HEADS])
        rden, context, ctxT = sb("rden", [P, T, HEADS, 1]), sb("context", [P, T, D]), sb("ctxT", [P, SEQ])
        scores = ps("scores", [P, GROUPS, T, SEQ])
        pv = ps("pv", [P, T, HEADS, AUG])
        v_psum = ps("v_psum", [P, T, D])
        vo = ps("vo", [P, T, D])
        banks = lambda n: slice(2 * (n % 2), 2 * (n % 2) + 2)
        of_pair = lambda tile, n: tile[:, :, 2 * n:2 * n + 2, :].rearrange("p t h s -> p h t s")
        bank_of = lambda g: (2 if g < 2 else 0) + (g % 2 if softmax else 0)
        block = ctx.enter_context(nc.Block())

        def run(eng, front, back, settle=False):
            front(0, 0)
            if settle:
                sig.settle(eng)
            with eng.Fori(0, B // 2 - 1) as pair:
                for parity in range(2):
                    back(pair * 2 + parity, parity, pair * 2 + (parity + 1))
            back(B - 2, 0, B - 1)
            back(B - 1, 1, None)

        @block.sync
        def _(sp):
            for name, tile in tiles.items():
                src = dram[name] if name in ("ident_bf", "mask", "maskT") else dram[f"A{level}_{name}"]
                sp.dma_start(tile[:], src).then_inc(once["loaded"], 16)

        @block.tensor
        def _(pe):
            def score(n, stationary, moving, mask_of):
                g = n // 2
                for j in (2 * (n % 2), 2 * (n % 2) + 1):
                    for t in range(T):
                        first, end = span(t, mask_of)
                        ins = nc.tensor.matmul(scores[:, j, t, first:end], stationary[:, j, g, t * P:(t + 1) * P],
                                               moving[:, g, first:end], start=True, stop=mask_of is None,
                                               skip_group_check=True)
                        if mask_of is not None:
                            ins = nc.tensor.matmul(scores[:, j, t, t * P:(t + 1) * P], ident_bf[:, :], mask_of[:, :],
                                                   start=False, stop=True, skip_group_check=True)
                return ins

            def span(t, mask_of):
                if mask_of is None:
                    return 0, SEQ
                return (0, (t + 1) * P) if mask_of is mask else (t * P, SEQ)

            def project_v(ahead):
                pe.wait_ge(*sig("xT", ahead, 1))
                pe.wait_ge(*sig("v", ahead))
                for t in range(T):
                    ins = nc.tensor.matmul(v_psum[:, t, :], m.xT[:, t * P:(t + 1) * P], wv[:, :], start=True, stop=True)
                ins.then_inc(sig["v_psum"], 1)

            def project(ahead, g):
                projections = [wq, wk] if softmax else [wq, wk, tiles["wq_swap"], tiles["wk_swap"]]
                if not softmax and g % 2 == 1:
                    pe.wait_ge(*sig("rope", ahead, g))
                for n, w in enumerate(projections):
                    ins = nc.tensor.matmul(scores[:, bank_of(g) + n // 2, n % 2, :], w[:, g, :], m.xT[:, :],
                                           start=True, stop=True)
                ins.then_inc(sig["proj"], 1)

            def projected(ahead, groups):
                pe.wait_ge(*sig("proj_read", ahead, groups))
                if not softmax:
                    pe.wait_ge(*sig("rope", ahead, groups))

            def front_score(ahead, parity, i):
                if i % 4 == 0:
                    pe.wait_ge(*sig("q_alone", ahead, i // 2 + 2))
                if softmax:
                    score(BESIDE[i], q_alone, qk[:, parity, 1], mask if causal else None).then_inc(sig["max_scores"], 1)
                else:
                    score(BESIDE[i], q_alone, qk[:, 0, 1], None).then_inc(sig["den_scores"], 1)

            def turn_negmax(ahead, half):
                pe.wait_ge(*sig("negmax", ahead, 4 * half + 4))
                pe.wait_ge(*sig("q_aug", ahead, half))
                for g in (2 * half, 2 * half + 1):
                    for t in range(T):
                        at = (g % 2) * SEQ + t * P
                        ins = nc.tensor.transpose(m.psum[:, at:at + P], negmax[:, t, g, :], chip.ident[:, :])
                ins.then_inc(sig["negmaxT"], 1)

            def back_score(step, parity, n):
                if n % 4 == 0:
                    if softmax:
                        pe.wait_ge(*sig("q_aug", step, n // 4 + 1))
                    else:
                        pe.wait_ge(*sig("rope", step, GROUPS))
                if n % 2 == 0:
                    pe.wait_ge(*sig("k_alone", step, n // 2 + 1))
                score(n, k_alone[:, parity], (qk if softmax else turned)[:, parity, 0], maskT if causal else None)\
                  .then_inc(sig["scores"], 1)

            def weigh(step, parity, n):
                pe.wait_ge(*sig("probs", step, n + 1))
                if n == 0:
                    pe.wait_ge(*sig("v", step, 1))
                    pe.wait_ge(*sig("context", step))
                columns = slice(0, AUG if softmax else DK)
                for h in (2 * n, 2 * n + 1):
                    for qt in range(T):
                        for kt in range(qt + 1 if causal else T):
                            last = kt == (qt if causal else T - 1)
                            ins = nc.tensor.matmul(pv[:, qt, h, columns], probs[:, kt, h, qt * P:(qt + 1) * P],
                                                   v[:, parity, kt, h, columns], start=kt == 0, stop=last)
                return ins

            def front(ahead, parity):
                norm_transpose(nc, pe, sig, chip, m, ahead)
                project_v(ahead)
                for g in range(GROUPS):
                    project(ahead, g)
                projected(ahead, GROUPS)
                for i in range(PAIRS):
                    if i > 0:
                        pe.wait_ge(*sig(drained, ahead, i))
                    front_score(ahead, parity, i)
                if softmax:
                    for half in range(2):
                        turn_negmax(ahead, half)

            def back(step, parity, ahead):
                pe.wait_ge(*sig(drained, step, PAIRS))
                pe.wait_ge(*sig("probs", step))
                for n in range(PAIRS):
                    i = 2 * (n - 4)
                    if n >= 2 and (ahead is None or n == 2):
                        pe.wait_ge(*sig("probs", step, n - 1))
                    elif n == 3:
                        projected(ahead, 2)
                    elif n >= 4:
                        pe.wait_ge(*sig("probs", step, n))
                        front_score(ahead, 1 - parity, i)
                        if n > 4:
                            pe.wait_ge(*sig(drained, ahead, i))
                    back_score(step, parity, n)
                    if n > 0:
                        weigh(step, parity, n - 1)
                    if ahead is None:
                        continue
                    if n == 1:
                        pe.wait_ge(*sig("ctxT", step))
                        norm_transpose(nc, pe, sig, chip, m, ahead)
                    elif n == 2:
                        project_v(ahead)
                        for g in (0, 1):
                            project(ahead, g)
                    elif n == 3:
                        for g in (2, 3):
                            project(ahead, g)
                        projected(ahead, GROUPS)
                    elif n >= 4:
                        pe.wait_ge(*sig(drained, ahead, i + 1))
                        front_score(ahead, 1 - parity, i + 1)
                        if n == 6 and softmax:
                            turn_negmax(ahead, 0)
                weigh(step, parity, PAIRS - 1).then_inc(sig["ctx_psum"], 1)
                if ahead is not None and softmax:
                    turn_negmax(ahead, 1)
                    pe.wait_ge(*sig("q_aug", ahead, 2))
                pe.wait_ge(*sig("context", step, 1))
                for t in range(T):
                    ins = nc.tensor.transpose(m.psum[:, t * P:(t + 1) * P], context[:, t, :], chip.ident[:, :])
                ins.then_inc(sig["ctxT_psum"], 1)
                pe.wait_ge(*sig("ctxT", step, 1))
                pe.wait_ge(*sig("x", step))
                for t in range(T):
                    ins = nc.tensor.matmul(vo[:, t, :], ctxT[:, t * P:(t + 1) * P], wo[:, :], start=True, stop=True)
                ins.then_inc(sig["out_psum"], 1)

            pe.wait_ge(*once("loaded", 1))
            pe.wait_ge(*once("set", 1))
            run(pe, front, back, settle=True)

        @block.scalar
        def _(act):
            def xT(ahead):
                act.wait_ge(*sig("xT_psum", ahead, 1))
                act.wait_ge(*sig("proj", ahead))
                if level == 2:
                    ins = nc.scalar.activation(m.xT[:, :], m.psum[:, 0:SEQ], ACT.Identity, bias=tiles["beta"][:, 0:1],
                                               scale=tiles["gamma"][:, 0:1])
                else:
                    ins = nc.scalar.activation(m.xT[:, :], m.psum[:, 0:SEQ], ACT.Copy)
                ins.then_inc(sig["xT"], 1)

            def read_projection(ahead, parity, g, settled):
                act.wait_ge(*sig("proj", ahead, g + 1))
                act.wait_ge(*sig("scores" if softmax else "den_scores", settled))
                act.wait_ge(*sig("q_alone", ahead))
                act.wait_ge(*sig("k_alone", ahead))
                for n in range(2):
                    if softmax:
                        ins = nc.scalar.activation(qk[:, parity, n, g, :], scores[:, bank_of(g), n, :], ACT.Identity,
                                                   bias=tiles["bq" if n == 0 else "bk"][:, g:g + 1])
                    else:
                        ins = nc.scalar.activation(qk[:, 0, n, g, :], scores[:, bank_of(g), n, :], ACT.Copy)
                ins.then_inc(sig["proj_read"], 1)

            def denominators(ahead, i):
                act.wait_ge(*sig("den_scores", ahead, i + 1))
                act.wait_ge(*sig("den", ahead, max(i - 1, 0)))
                nc.scalar.activation(den_exp[:, i % 2], scores[:, banks(BESIDE[i]), :, :], ACT.Exp, scale=scale)\
                  .then_inc(sig["den_probs"], 1)

            def exponential(step, n):
                act.wait_ge(*sig("scores", step, n + 1))
                act.wait_ge(*sig("ctx_psum", step))
                for t in range(T) if causal else [slice(0, T)]:
                    first = t * P if causal else 0
                    ins = nc.scalar.activation(of_pair(probs, n)[:, :, t, first:SEQ], scores[:, banks(n), t, first:SEQ],
                                               ACT.Exp, scale=scale)
                ins.then_inc(sig["probs"], 1)

            def front(ahead, parity):
                xT(ahead)
                for g in range(GROUPS):
                    read_projection(ahead, parity, g, ahead)
                if not softmax:
                    for i in range(PAIRS):
                        denominators(ahead, i)

            def back(step, parity, ahead):
                for n in range(PAIRS):
                    with_front = ahead is not None
                    if with_front and n >= 4 and not softmax:
                        denominators(ahead, 2 * (n - 4))
                    exponential(step, n)
                    if with_front and n == 1:
                        xT(ahead)
                    elif with_front and n in (2, 3):
                        for g in (2 * (n - 2), 2 * (n - 2) + 1):
                            read_projection(ahead, 1 - parity, g, step if softmax else ahead)
                    elif with_front and n >= 4 and not softmax:
                        denominators(ahead, 2 * (n - 4) + 1)
                act.wait_ge(*sig("ctxT_psum", step, 1))
                act.wait_ge(*sig("out_psum", step))
                nc.scalar.activation(ctxT[:, :], m.psum[:, 0:SEQ], ACT.Copy).then_inc(sig["ctxT"], 1)

            act.wait_ge(*once("loaded", 1))
            run(act, front, back)

        @block.gpsimd
        def _(pool):
            def front(ahead, parity, settled=None):
                if level == 2:
                    norm_rstd(nc, pool, sig, chip, m, ahead, "_a")
                norm_rstd(nc, pool, sig, chip, m, ahead)
                source = (qk if softmax else turned)[:, parity, 1]
                for g in range(GROUPS):
                    pool.wait_ge(*sig("proj_read" if softmax else "rope", ahead, g + 1))
                    pool.wait_ge(*sig("scores", ahead if settled is None else settled))
                    sig.settle(pool)
                    for j in range(GROUPS):
                        band = slice(BAND * j, BAND * (j + 1))
                        ins = nc.gpsimd.tensor_copy(k_alone[band, parity, j, g, :], source[band, g, :])
                    ins.then_inc(sig["k_alone"], 1)
                pool.wait_ge(*sig("k_alone", ahead, GROUPS))

            def back(step, parity, ahead):
                if ahead is not None:
                    front(ahead, 1 - parity, step)

            nc.gpsimd.memset(k_alone[:], 0.0).then_inc(once["set"], 1)
            pool.wait_ge(*once("set", 1))
            run(pool, front, back)

        @block.vector
        def _(dve):
            def norm(ahead, parity, settled):
                tile = lambda t: x_of(ahead)[:, t, :]
                if level == 2:
                    norm_vector(nc, dve, sig, m, ahead, tile, lambda t: x1[:, parity, t, :], [], "_a", [sig("x", settled)])
                    dve.wait_ge(*sig("xn_a", ahead, 1))
                    tile = lambda t: x1[:, parity, t, :]
                norm_vector(nc, dve, sig, m, ahead, tile, lambda t: m.xn[:, t, :], ["xT_psum"])

            def x_of(step):
                if isinstance(step, int):
                    return chip.x[:, step * T:(step + 1) * T, :]
                return chip.x[:, bass.ds(step * T, T), :]

            def copy_v(ahead, parity, settled):
                dve.wait_ge(*sig("v_psum", ahead, 1))
                dve.wait_ge(*sig("ctx_psum", settled))
                vh = v_psum[:, :, :].rearrange("p t (h c) -> p t h c", c=DK)
                for t in range(T):
                    if softmax:
                        ins = nc.vector.tensor_tensor(v[:, parity, t, :, 0:DK], vh[:, t],
                                                      tiles["bv"][:, :].rearrange("p (h c) -> p h c", c=DK), ALU.add)
                    else:
                        ins = nc.vector.tensor_copy(v[:, parity, t, :, 0:DK], vh[:, t])
                ins.then_inc(sig["v"], 1)

            def rotate(ahead, parity, g, settled):
                rope = tiles["rope"]
                cos, sin = (rope[:, n:n + 1, :].to_broadcast([P, 2, SEQ]) for n in range(2))
                dve.wait_ge(*sig("proj", ahead, g + 1))
                dve.wait_ge(*sig("proj_read", ahead, g + 1))
                dve.wait_ge(*sig("rope", ahead, g))
                dve.wait_ge(*sig("scores", settled))
                dve.wait_ge(*sig("k_alone", ahead))
                nc.vector.tensor_tensor(turn[:, 0, :, :], scores[:, bank_of(g), :, :], cos, ALU.mult).then_inc(sig["rope_chain"], 1)
                nc.vector.tensor_tensor(turn[:, 1, :, :], scores[:, bank_of(g) + 1, :, :], sin, ALU.mult).then_inc(sig["rope_chain"], 1)
                dve.wait_ge(*sig("rope_chain", ahead, 2 * g + 2))
                nc.vector.tensor_tensor(turned[:, parity, :, g, :], turn[:, 0, :, :], turn[:, 1, :, :], ALU.add)\
                  .then_inc(sig["rope"], 1)

            def copy_q(ahead, parity, g):
                dve.wait_ge(*sig("proj_read", ahead, g + 1))
                dve.wait_ge(*sig("max_scores" if softmax else "den_scores", ahead))
                source = qk[:, parity if softmax else 0, 0]
                for j in range(GROUPS):
                    band = slice(BAND * j, BAND * (j + 1))
                    ins = nc.vector.tensor_copy(q_alone[band, j, g, :], source[band, g, :])
                ins.then_inc(sig["q_alone"], 1)

            def reduce(ahead, parity, i, settled):
                n = BESIDE[i]
                if softmax:
                    dve.wait_ge(*sig("max_scores", ahead, i + 1))
                    dve.wait_ge(*sig("negmaxT", ahead))
                    places = negmax[:, :, n // 2, :].rearrange("p t (j r) -> p j t r", r=BAND)[:, banks(n), :, DK]
                    for t in range(T) if causal else [slice(0, T)]:
                        keys = (t + 1) * P if causal else SEQ
                        ins = nc.vector.tensor_reduce(places[:, :, t], scores[:, banks(n), t, 0:keys], AX.X, ALU.max,
                                                      negate=True)
                    ins.then_inc(sig["negmax"], 1)
                else:
                    dve.wait_ge(*sig("den_probs", ahead, i + 1))
                    dve.wait_ge(*sig("ctx_chain", settled))
                    nc.vector.tensor_reduce(den[:, parity, :, 2 * n:2 * n + 2].rearrange("p t h -> p h t"), den_exp[:, i % 2],
                                            AX.X, ALU.add).then_inc(sig["den"], 1)

            def add_negmax(ahead, parity, half):
                dve.wait_ge(*sig("negmaxT", ahead, half + 1))
                dve.wait_ge(*sig("q_alone", ahead, GROUPS))
                q2 = qk[:, parity, 0, 2 * half:2 * half + 2, :]
                nc.vector.tensor_tensor(q2, m.psum[:, :].rearrange("p (g s) -> p g s", g=2), q2, ALU.add)\
                  .then_inc(sig["q_aug"], 1)

            def front(ahead, parity):
                norm(ahead, parity, ahead)
                copy_v(ahead, parity, ahead)
                for g in range(GROUPS):
                    if not softmax:
                        rotate(ahead, parity, g, ahead)
                    copy_q(ahead, parity, g)
                for i in range(PAIRS):
                    reduce(ahead, parity, i, ahead)
                if softmax:
                    for half in range(2):
                        add_negmax(ahead, parity, half)

            def back(step, parity, ahead):
                if ahead is not None:
                    norm(ahead, 1 - parity, step)
                    copy_v(ahead, 1 - parity, step)
                    for g in range(GROUPS):
                        if not softmax:
                            rotate(ahead, 1 - parity, g, step)
                        copy_q(ahead, 1 - parity, g)
                    for i in range(PAIRS):
                        reduce(ahead, 1 - parity, i, step)
                        if i == 5 and softmax:
                            add_negmax(ahead, 1 - parity, 0)
                dve.wait_ge(*sig("ctx_psum", step, 1))
                sums = pv[:, :, :, DK:AUG] if softmax else den[:, parity].rearrange("p t (h o) -> p t h o", o=1)
                nc.vector.reciprocal(rden[:, :, :, :], sums).then_inc(sig["ctx_chain"], 1)
                dve.wait_ge(*sig("ctx_chain", step, 1))
                dve.wait_ge(*sig("ctxT_psum", step))
                ch = context[:, :, :].rearrange("p t (h c) -> p t h c", c=DK)
                for t in range(T):
                    ins = nc.vector.tensor_tensor(ch[:, t], pv[:, t, :, 0:DK], rden[:, t].to_broadcast([P, HEADS, DK]), ALU.mult)
                ins.then_inc(sig["context"], 1)
                if ahead is not None and softmax:
                    add_negmax(ahead, 1 - parity, 1)
                dve.wait_ge(*sig("out_psum", step, 1))
                xs = x_of(step)
                nc.vector.tensor_tensor(xs, vo[:, :, :], xs, ALU.add).then_inc(sig["x"], 1)
                dve.wait_ge(*sig("x", step, 1))
                if level == 2:
                    nc.vector.tensor_tensor(xs, xs, x1[:, parity, :, :], ALU.add).then_inc(sig["residual"], 1)
                    dve.wait_ge(*sig("residual", step, 1))
                nc.vector.tensor_tensor(xs, xs, bo[:, :].rearrange("p (a d) -> p a d", a=1).to_broadcast([P, T, D]), ALU.add)\
                  .then_inc(sig["x"], 1)
                dve.wait_ge(*sig("x", step, 2))

            nc.vector.memset(v[:, :, :, :, :], 1.0).then_inc(once["set"], 1)
            nc.vector.memset(q_alone[:], 0.0).then_inc(once["set"], 1)
            if softmax:
                nc.vector.memset(negmax[:, :, :, :], 0.0).then_inc(once["set"], 1)
            dve.wait_ge(*once("set", 1))
            dve.wait_ge(*once("loaded", 1))
            run(dve, front, back, settle=True)
    sig.ended(B)
    once.ended(1)


RW_HEADS, HS = 2, 64
LORA_R, TD_R = 32, 64
MIXES = 5
PAIR = 2
ROUNDS = HS // PAIR
RW_SIGNALS = dict(NORM_SIGNALS, mix_chain=3 + MIXES, lora_psum=1, lora=1, miu_psum=1, mixed=1, td_psum=1, kvrg_psum=1,
                  td_tanh=1, w_psum=1, act_chain=1, decay=1, kvr=1, g_exp=1, ruk=1, bonus_psum=1, gate=1, gate_chain=2,
                  bonus=1, vb=ROUNDS, kv=ROUNDS, scan=ROUNDS, prod=ROUNDS, y_acc=ROUNDS, yT=1, y_tok=1, yn_stats=1,
                  yn_moments=1, yn_var=1, yn_rstd=1, yn=1, ynT_psum=1, ynT=1, gated=1, out_psum=1, x=1)
RW_LOADS = 16
PE_PLACES, DVE_PLACES, POOL_PLACE = (2, 6, 8, 13, 15, 18), (1, 4, 10, 16, 20), 1


def stage_rwkv(chip):
    nc, dram, sig, once = chip.nc, chip.dram, chip.loop, chip.once
    sig.use(RW_SIGNALS)
    once.use(dict(loaded=16 * (RW_LOADS + 1), set=3))
    T = HALVES
    with ExitStack() as ctx:
        sb = lambda name, shape, dt=F32: ctx.enter_context(nc.sbuf_tensor(chip.tag + name, shape, dt))
        ps = lambda name, shape: ctx.enter_context(nc.psum_tensor(chip.tag + name, shape, F32))
        m = Norm(chip, ctx, T)
        tiles = {"miu_x": sb("miu_x", [P, 1]), "lambda": sb("lambda", [P, MIXES]), "A": sb("A", [P, MIXES * LORA_R]),
                 "B": sb("B", [LORA_R, MIXES, D]), "td_miu": sb("td_miu", [P, 1]), "td_A": sb("td_A", [P, TD_R]),
                 "td_B": sb("td_B", [TD_R, D]), "u": sb("u", [P, 1]), "wr": sb("wr", [P, D]), "wk": sb("wk", [P, D]),
                 "wv": sb("wv", [P, D]), "wg": sb("wg", [P, D]), "wo": sb("wo", [P, D]), "gamma": sb("gamma", [P, 1]),
                 "beta": sb("beta", [P, 1]), "head_ones": sb("head_ones", [P, P])}
        assert len(tiles) == RW_LOADS
        spread = sb("spread", [P, HS, P])
        gather = sb("gather", [P, P + HS - 1])
        delta, xm, lora = sb("delta", [P, SEQ]), sb("xm", [P, SEQ]), sb("lora", [LORA_R, MIXES, SEQ])
        mix, td = sb("mix", [P, MIXES, SEQ]), sb("td", [TD_R, SEQ])
        expw, rT, ruk, expg = sb("expw", [P, SEQ]), sb("rT", [P, SEQ]), sb("ruk", [P, SEQ]), sb("expg", [P, SEQ])
        decays = sb("decay", [P, 2, PAIR, SEQ])
        kTs, vTs, r_nexts = sb("kT", [P, 2, SEQ]), sb("vT", [P, 2, SEQ]), sb("r_next", [P, 2, SEQ])
        bonuses, gates = sb("bonus", [P, 2, SEQ]), sb("gate", [P, 2, SEQ])
        kv, state, prod = sb("kv", [P, 2, PAIR, SEQ]), sb("state", [P, 2, PAIR, SEQ]), sb("prod", [P, 2, PAIR, SEQ])
        yT, yn, ynT, gated = sb("yT", [P, SEQ]), sb("yn", [P, T, D]), sb("ynT", [P, SEQ]), sb("gated", [P, SEQ])
        y_stats, y_moments = sb("y_stats", [P, T * RW_HEADS, 6]), sb("y_moments", [P, T * RW_HEADS, 2])
        y_var, y_rstd = sb("y_var", [P, T * RW_HEADS]), sb("y_rstd", [P, T * RW_HEADS])
        work = ps("work", [P, 4, 2, SEQ])
        vb = [ps(f"vb{n}", [P, PAIR, SEQ]) for n in range(2)]
        y_psum = ps("y", [P, 512])
        block = ctx.enter_context(nc.Block())
        lora_psum = work[0:LORA_R, 0:3, :, :].rearrange("p b a s -> p (b a) s")[:, 0:MIXES, :]
        miu_psum = work[:, 0:3, :, :].rearrange("p b a s -> p (b a) s")[:, 0:MIXES, :]
        one = lambda v: v.rearrange("p (a s) -> p a s", a=1)

        def run(eng, pieces, front, back):
            for piece in range(pieces):
                front(0, 0, piece, 0)
            sig.settle(eng)
            with eng.Fori(0, B // 2 - 1) as pair:
                for parity in range(2):
                    back(pair * 2 + parity, parity, pair * 2 + (parity + 1))
            back(B - 2, 0, B - 1)
            back(B - 1, 1, None)

        @block.sync
        def _(sp):
            for name, tile in tiles.items():
                sp.dma_start(tile[:], dram["RW_" + name]).then_inc(once["loaded"], 16)
            sp.dma_start(gather[:, :], dram["RW_gather"]).then_inc(once["loaded"], 16)

        @block.tensor
        def _(pe):
            pe.wait_ge(*once("loaded", 1))
            pe.wait_ge(*once("set", 1))
            def front(ahead, parity, piece, settled):
                if piece == 0:
                    norm_transpose(nc, pe, sig, chip, m, ahead)
                elif piece == 1:
                    pe.wait_ge(*sig("mixed", ahead))
                    pe.wait_ge(*sig("x", settled))
                    pe.wait_ge(*sig("ynT", settled))
                    pe.wait_ge(*sig("mix_chain", ahead, 3))
                    for f in range(MIXES):
                        ins = nc.tensor.matmul(lora_psum[:, f, :], tiles["A"][:, f * LORA_R:(f + 1) * LORA_R], xm[:, :],
                                               start=True, stop=True)
                    ins.then_inc(sig["lora_psum"], 1)
                elif piece == 2:
                    pe.wait_ge(*sig("lora", ahead, 1))
                    for f in range(MIXES):
                        ins = nc.tensor.matmul(miu_psum[:, f, :], tiles["B"][:, f, :], lora[:, f, :], start=True, stop=True)
                    ins.then_inc(sig["miu_psum"], 1)
                elif piece == 3:
                    pe.wait_ge(*sig("mixed", ahead, 1))
                    nc.tensor.matmul(work[0:TD_R, 0, 0, :], tiles["td_A"][:, :], mix[:, 0, :], start=True, stop=True)\
                      .then_inc(sig["td_psum"], 1)
                    for n, name in enumerate(("wk", "wv", "wr", "wg")):
                        ins = nc.tensor.matmul(work[:, 1 + n // 2, n % 2, :], tiles[name][:, :], mix[:, 1 + n, :], start=True, stop=True)
                    ins.then_inc(sig["kvrg_psum"], 1)
                elif piece == 4:
                    pe.wait_ge(*sig("td_tanh", ahead, 1))
                    pe.wait_ge(*sig("bonus", ahead))
                    nc.tensor.matmul(work[:, 3, 0, :], tiles["td_B"][:, :], td[:, :], start=True, stop=True).then_inc(sig["w_psum"], 1)
                else:
                    pe.wait_ge(*sig("ruk", ahead, 1))
                    pe.wait_ge(*sig("act_chain", ahead, 1))
                    nc.tensor.matmul(work[:, 3, 1, :], tiles["head_ones"][:, :], ruk[:, :], start=True, stop=True)\
                      .then_inc(sig["bonus_psum"], 1)

            def spread_v(step, parity, n):
                pe.wait_ge(*sig("kv", step, max(n - 1, 0)))
                for a in range(PAIR):
                    ins = nc.tensor.matmul(vb[n % 2][:, a, :], spread[:, PAIR * n + a, :], vTs[:, parity, :], start=True, stop=True)
                ins.then_inc(sig["vb"], 1)

            def back(step, parity, ahead):
                pe.wait_ge(*sig("kvr", step, 1))
                spread_v(step, parity, 0)
                spread_v(step, parity, 1)
                pe.wait_ge(*sig("yT", step))
                for n in range(ROUNDS):
                    if ahead is not None and n in PE_PLACES:
                        front(ahead, 1 - parity, PE_PLACES.index(n), step)
                    if n + 2 < ROUNDS:
                        spread_v(step, parity, n + 2)
                    pe.wait_ge(*sig("prod", step, n + 1))
                    for a in range(PAIR):
                        at = HS - 1 - (PAIR * n + a)
                        ins = nc.tensor.matmul(y_psum[:, 0:SEQ], gather[:, at:at + P], prod[:, n % 2, a, :],
                                               start=n == 0 and a == 0, stop=n == ROUNDS - 1 and a == PAIR - 1)
                    ins.then_inc(sig["y_acc"], 1)
                pe.wait_ge(*sig("yT", step, 1))
                for t in range(T):
                    ins = nc.tensor.transpose(work[:, 0, t, 0:P], yT[:, t * P:(t + 1) * P], chip.ident[:, :])
                ins.then_inc(sig["y_tok"], 1)
                pe.wait_ge(*sig("yn", step, 1))
                if ahead is not None:
                    pe.wait_ge(*sig("kvr", ahead, 1))
                for t in range(T):
                    ins = nc.tensor.transpose(work[:, 1, 0, t * P:(t + 1) * P], yn[:, t, :], chip.ident[:, :])
                ins.then_inc(sig["ynT_psum"], 1)
                pe.wait_ge(*sig("gated", step, 1))
                for t in range(T):
                    ins = nc.tensor.matmul(work[:, 0, t, 0:D], gated[:, t * P:(t + 1) * P], tiles["wo"][:, :], start=True, stop=True)
                ins.then_inc(sig["out_psum"], 1)

            run(pe, len(PE_PLACES), front, back)

        @block.scalar
        def _(act):
            act.wait_ge(*once("loaded", 1))
            act.wait_ge(*once("set", 1))
            def front(ahead, parity, piece, settled):
                norm_xT(nc, act, sig, m, ahead, ["mixed"])
                act.wait_ge(*sig("lora_psum", ahead, 1))
                nc.scalar.activation(lora[:, :, :], lora_psum, ACT.Tanh).then_inc(sig["lora"], 1)
                act.wait_ge(*sig("td_psum", ahead, 1))
                nc.scalar.activation(td[:, :], work[0:TD_R, 0, 0, :], ACT.Tanh).then_inc(sig["td_tanh"], 1)
                act.wait_ge(*sig("kvrg_psum", ahead, 1))
                act.wait_ge(*sig("y_acc", settled))
                nc.scalar.activation(kTs[:, parity, :], work[:, 1, 0, :], ACT.Copy)
                nc.scalar.activation(vTs[:, parity, :], work[:, 1, 1, :], ACT.Copy)
                nc.scalar.activation(r_nexts[:, parity, 0:SEQ - 1], work[:, 2, 0, 1:SEQ], ACT.Copy)
                nc.scalar.activation(rT[:, :], work[:, 2, 0, :], ACT.Copy).then_inc(sig["kvr"], 1)
                act.wait_ge(*sig("gate", ahead))
                nc.scalar.activation(expg[:, :], work[:, 2, 1, :], ACT.Exp, scale=-1.0).then_inc(sig["g_exp"], 1)
                act.wait_ge(*sig("w_psum", ahead, 1))
                nc.scalar.activation(expw[:, :], work[:, 3, 0, :], ACT.Exp, bias=tiles["td_miu"][:, 0:1]).then_inc(sig["act_chain"], 1)
                act.wait_ge(*sig("act_chain", ahead, 1))
                for a in range(PAIR):
                    ins = nc.scalar.activation(decays[:, parity, a, 1:SEQ], expw[:, 1:SEQ], ACT.Exp, scale=-1.0)
                ins.then_inc(sig["decay"], 1)

            def back(step, parity, ahead):
                if ahead is not None:
                    front(ahead, 1 - parity, 0, step)
                act.wait_ge(*sig("ynT_psum", step, 1))
                act.wait_ge(*sig("gated", step))
                nc.scalar.activation(ynT[:, :], work[:, 1, 0, :], ACT.Identity, bias=tiles["beta"][:, 0:1],
                                     scale=tiles["gamma"][:, 0:1]).then_inc(sig["ynT"], 1)

            run(act, 1, front, back)

        @block.gpsimd
        def _(pool):
            def front(ahead, parity, piece, settled):
                norm_rstd(nc, pool, sig, chip, m, ahead)

            def back(step, parity, ahead):
                pool.wait_ge(*sig("kvr", step, 1))
                for n in range(ROUNDS):
                    if ahead is not None and n == POOL_PLACE:
                        front(ahead, 1 - parity, 0, step)
                    pool.wait_ge(*sig("scan", step, n + 1))
                    pool.wait_ge(*sig("y_acc", step, max(n - 1, 0)))
                    nc.gpsimd.tensor_tensor(prod[:, n % 2, :, :], state[:, n % 2, :, :],
                                            one(r_nexts[:, parity, :]).to_broadcast([P, PAIR, SEQ]), ALU.mult).then_inc(sig["prod"], 1)
                pool.wait_ge(*sig("yn_var", step, 1))
                nc.gpsimd.tensor_tensor(y_rstd[:, :], y_var[:, :], chip.minus_half[:, :].to_broadcast([P, T * RW_HEADS]), ALU.pow)\
                  .then_inc(sig["yn_rstd"], 1)

            run(pool, 1, front, back)

        @block.vector
        def _(dve):
            dve.wait_ge(*once("loaded", 1))
            nc.vector.memset(r_nexts[:, :, SEQ - 1:SEQ], 0.0).then_inc(once["set"], 1)
            nc.vector.memset(decays[:, :, :, 0:1], 0.0).then_inc(once["set"], 1)
            nc.vector.tensor_copy(spread[:, :, :].rearrange("p v (h k) -> p v h k", h=RW_HEADS),
                                  chip.ident[:, :].rearrange("p (h v o) -> p v h o", h=RW_HEADS, o=1).to_broadcast([P, HS, RW_HEADS, HS]))\
              .then_inc(once["set"], 1)
            def x_of(step):
                if isinstance(step, int):
                    return chip.x[:, step * T:(step + 1) * T, :]
                return chip.x[:, bass.ds(step * T, T), :]

            def front(ahead, parity, piece, settled):
                if piece == 0:
                    norm_vector(nc, dve, sig, m, ahead, lambda t: x_of(ahead)[:, t, :], lambda t: m.xn[:, t, :], ["xT_psum"])
                elif piece == 1:
                    chain = Chain(dve, sig, "mix_chain", ahead)
                    dve.wait_ge(*sig("xT", ahead, 1))
                    nc.vector.tensor_scalar(delta[:, 0:1], m.xT[:, 0:1], -1.0, None, ALU.mult).then_inc(sig["mix_chain"], 1)
                    chain.n += 1
                    chain(nc.vector.tensor_tensor(delta[:, 1:SEQ], m.xT[:, 0:SEQ - 1], m.xT[:, 1:SEQ], ALU.subtract))
                    chain(nc.vector.scalar_tensor_tensor(xm[:, :], delta[:, :], tiles["miu_x"][:, 0:1], m.xT[:, :], ALU.mult, ALU.add))
                elif piece == 2:
                    dve.wait_ge(*sig("miu_psum", ahead, 1))
                    dve.wait_ge(*sig("kvrg_psum", ahead))
                    for f in range(MIXES):
                        ins = nc.vector.scalar_tensor_tensor(mix[:, f, :], miu_psum[:, f, :], tiles["lambda"][:, f:f + 1], delta[:, :],
                                                             ALU.add, ALU.mult)
                        ins.then_inc(sig["mix_chain"], 1)
                    dve.wait_ge(*sig("mix_chain", ahead, 3 + MIXES))
                    nc.vector.tensor_tensor(mix[:, :, :], mix[:, :, :], one(m.xT[:, :]).to_broadcast([P, MIXES, SEQ]), ALU.add)\
                      .then_inc(sig["mixed"], 1)
                elif piece == 3:
                    dve.wait_ge(*sig("kvr", ahead, 1))
                    nc.vector.scalar_tensor_tensor(ruk[:, :], rT[:, :], tiles["u"][:, 0:1], kTs[:, parity, :], ALU.mult, ALU.mult)\
                      .then_inc(sig["ruk"], 1)
                    gate = gates[:, parity, :]
                    chain = Chain(dve, sig, "gate_chain", ahead)
                    dve.wait_ge(*sig("g_exp", ahead, 1))
                    dve.wait_ge(*sig("gated", settled))
                    chain(nc.vector.tensor_scalar(gate, expg[:, :], 1.0, None, ALU.add))
                    chain(nc.vector.reciprocal(gate, gate))
                    nc.vector.tensor_tensor(gate, work[:, 2, 1, :], gate, ALU.mult).then_inc(sig["gate"], 1)
                    chain.done()
                else:
                    dve.wait_ge(*sig("bonus_psum", ahead, 1))
                    dve.wait_ge(*sig("yT", settled))
                    nc.vector.tensor_tensor(bonuses[:, parity, :], work[:, 3, 1, :], vTs[:, parity, :], ALU.mult).then_inc(sig["bonus"], 1)

            def back(step, parity, ahead):
                dve.wait_ge(*sig("decay", step, 1))
                for n in range(ROUNDS):
                    if ahead is not None and n in DVE_PLACES:
                        front(ahead, 1 - parity, DVE_PLACES.index(n), step)
                    dve.wait_ge(*sig("vb", step, n + 1))
                    dve.wait_ge(*sig("scan", step, max(n - 1, 0)))
                    nc.vector.tensor_tensor(kv[:, n % 2, :, :], vb[n % 2][:, :, :], one(kTs[:, parity, :]).to_broadcast([P, PAIR, SEQ]), ALU.mult)\
                      .then_inc(sig["kv"], 1)
                    dve.wait_ge(*sig("kv", step, n + 1))
                    dve.wait_ge(*sig("prod", step, max(n - 1, 0)))
                    flat = lambda tile: tile.rearrange("p a s -> p (a s)")
                    nc.vector.tensor_tensor_scan(flat(state[:, n % 2, :, :]), flat(decays[:, parity, :, :]), flat(kv[:, n % 2, :, :]), 0.0,
                                                 ALU.mult, ALU.add).then_inc(sig["scan"], 1)
                dve.wait_ge(*sig("y_acc", step, ROUNDS))
                dve.wait_ge(*sig("bonus", step, 1))
                nc.vector.tensor_copy(yT[:, 0:1], bonuses[:, parity, 0:1])
                nc.vector.tensor_tensor(yT[:, 1:SEQ], y_psum[:, 0:SEQ - 1], bonuses[:, parity, 1:SEQ], ALU.add).then_inc(sig["yT"], 1)
                dve.wait_ge(*sig("y_tok", step, 1))
                for n in range(T * RW_HEADS):
                    ins = nc.vector.bn_stats(y_stats[:, n, :], work[:, 0, n // 2, (n % 2) * HS:(n % 2 + 1) * HS])
                ins.then_inc(sig["yn_stats"], 1)
                sig.apart(dve, "yn_stats", step, 1)
                for n in range(T * RW_HEADS):
                    ins = nc.vector.bn_aggr(y_moments[:, n, :], y_stats[:, n, :])
                ins.then_inc(sig["yn_moments"], 1)
                dve.wait_ge(*sig("yn_moments", step, 1))
                nc.vector.tensor_scalar(y_var[:, :], y_moments[:, :, 1], EPS * RW_HEADS, None, ALU.add).then_inc(sig["yn_var"], 1)
                dve.wait_ge(*sig("yn_rstd", step, 1))
                for n in range(T * RW_HEADS):
                    half = slice((n % 2) * HS, (n % 2 + 1) * HS)
                    ins = nc.vector.tensor_scalar(yn[:, n // 2, half], work[:, 0, n // 2, half], y_moments[:, n, 0:1],
                                                  y_rstd[:, n:n + 1], ALU.subtract, ALU.mult)
                ins.then_inc(sig["yn"], 1)
                dve.wait_ge(*sig("ynT", step, 1))
                dve.wait_ge(*sig("gate", step, 1))
                nc.vector.tensor_tensor(gated[:, :], ynT[:, :], gates[:, parity, :], ALU.mult).then_inc(sig["gated"], 1)
                dve.wait_ge(*sig("out_psum", step, 1))
                xs = x_of(step)
                nc.vector.tensor_tensor(xs, work[:, 0, :, 0:D], xs, ALU.add).then_inc(sig["x"], 1)
                dve.wait_ge(*sig("x", step, 1))

            run(dve, len(DVE_PLACES), front, back)
    sig.ended(B)
    once.ended(1)


DEPTH = 6
LH, LD = 16, 64
INNER = LH * LD
WINDOW = 32
REACH = P + WINDOW
LPAIRS = LH // 2
FF = 341
FF_CHUNKS = 3
FF_TILES = 4
FF_STEPS = TILES // FF_TILES
CHUNKS = 4

STACK_ATTENTION = dict(z_copy=1, zT_psum=1, xsT=1, proj=CHUNKS + HALVES, square=CHUNKS, norm2=CHUNKS, half_turns=CHUNKS,
                       turn_sum=CHUNKS, clamped=CHUNKS, rnorm=CHUNKS, qk=CHUNKS, qkT_psum=2 * CHUNKS, qkT=2 * CHUNKS,
                       v=HALVES, scores=LPAIRS, negmax=LPAIRS, shifted=LPAIRS, probs=LPAIRS, probsT_psum=LPAIRS,
                       probsT=LPAIRS, pv=LPAIRS, rsum=LPAIRS, context=LPAIRS, ctxT_psum=4, ctxT=4, out_psum=1, z=1)
STACK_AHEAD = ("z_copy", "zT_psum", "xsT", "proj", "square", "norm2", "half_turns", "turn_sum", "clamped", "rnorm", "qk",
               "qkT_psum", "qkT", "v")
STACK_FFN = dict(f_copy=1, fzT_psum=1, fxsT=1, fxs_psum=1, norm_chain=1, moments=1, var=1, rstd=1, xn=1,
                 fxnT_psum=1, fxnT=1, h_psum=FF_CHUNKS, gelu=FF_CHUNKS, hidden=FF_CHUNKS, f_psum=1, zf=2)
STACK_LAYER = dict(tables=1, qkv_weights=32, out_weights=16, ffn_weights=64)
FF_PIECES = 3 + FF_CHUNKS + 1


def beside(n):
    total = (FF_STEPS - 1) * FF_PIECES
    return range(n * total // LPAIRS, (n + 1) * total // LPAIRS)


def stage_stack(chip):
    nc, dram, att, ffn, layer_sig, once = chip.nc, chip.dram, chip.loop, chip.ffn, chip.layer, chip.once
    att.use(STACK_ATTENTION)
    once.use(dict(set=3, loaded=48))
    with ExitStack() as ctx:
        sb = lambda name, shape, dt=F32: ctx.enter_context(nc.sbuf_tensor(chip.tag + name, shape, dt))
        z = sb("z", [P, TILES, D])
        wqkv, wo = sb("wqkv", [P, 3 * INNER]), sb("wo", [P, LPAIRS, D])
        rows, base, tables = sb("rows", [P, 4, 1, LD]), sb("base", [P, 4, HALVES, LD]), sb("tables", [P, 4, HALVES, LD])
        w1, w2, b2 = sb("w1", [P, 2 * FF]), sb("w2", [P, FF_CHUNKS, D]), sb("b2", [P, 1, D])
        cols = sb("cols", [P, 2 * FF_CHUNKS + 2])
        ident_bf, band = sb("ident_bf", [P, P], BF16), sb("band", [P, HALVES, REACH], BF16)
        zc, xsT = sb("zc", [P, HALVES, D]), sb("xsT", [P, SEQ])
        square = sb("square", [P, 2, INNER])
        halves = sb("halves", [P, 2, 2, INNER])
        qk = sb("qk", [P, CHUNKS, INNER])
        norm2, clamped, rnorm = sb("norm2", [P, CHUNKS, LH]), sb("clamped", [P, CHUNKS, LH]), sb("rnorm", [P, CHUNKS, LH])
        qkT = sb("qkT", [P, 2, LPAIRS, SEQ])
        v, v_near = sb("v", [P, HALVES, LH, LD + 1]), sb("v_near", [WINDOW, LH, LD + 1])
        negmax = sb("negmax", [P, 2, 2, HALVES, 1])
        shifted, probs = sb("shifted", [P, 2, 2, HALVES, REACH]), sb("probs", [P, 2, 2, HALVES, REACH])
        probsT, near = sb("probsT", [P, 2, 2, HALVES, P]), sb("near", [WINDOW, 2, 2, WINDOW])
        rsum = sb("rsum", [P, 2, 2, HALVES, 1])
        context, ctxT = sb("context", [P, HALVES, INNER]), sb("ctxT", [P, LPAIRS, SEQ])
        fz, fxsT = sb("fz", [P, FF_TILES, D]), sb("fxsT", [P, 2, SEQ])
        stats, moments = sb("stats", [P, FF_TILES, 6]), sb("moments", [P, FF_TILES, 2])
        var, rstd = sb("var", [P, FF_TILES]), sb("rstd", [P, FF_TILES])
        fxn, fxnT = sb("fxn", [P, FF_TILES, D]), sb("fxnT", [P, FF_TILES * P])
        gelu, hidden = sb("gelu", [P, 2, FF_TILES * P]), sb("hidden", [P, FF_CHUNKS, FF_TILES * P])
        wide = ctx.enter_context(nc.psum_tensor(chip.tag + "wide", [P, 2, 512], F32))
        score_psum = ctx.enter_context(nc.psum_tensor(chip.tag + "score_psum", [P, 2, 512], F32))
        flip = [ctx.enter_context(nc.psum_tensor(f"{chip.tag}flip{n}", [P, 512], F32)) for n in range(2)]
        acc = [ctx.enter_context(nc.psum_tensor(f"{chip.tag}acc{n}", [P, 512], F32)) for n in range(2)]
        tiles4 = lambda bank: bank[:, :].rearrange("p (t d) -> p t d", d=D)
        pv_of = lambda n: acc[n % 2][:, 0:4 * (LD + 1)].rearrange("p (h t c) -> p h t c", h=2, t=HALVES)
        near_psum = lambda n: acc[n % 2][0:WINDOW, 4 * (LD + 1):4 * (LD + 1) + 2 * WINDOW].rearrange("p (h q) -> p h q", h=2)
        scores = score_psum[:, :, 0:HALVES * REACH].rearrange("p h (t k) -> p h t k", t=HALVES)
        turn_flip = lambda n: flip[0 if n in (5, 7) else 1]
        ctx_flip = lambda n: flip[(n + 1) % 2]

        m = Norm(chip, ctx, FF_TILES, turned=False)
        first = chip.ffn
        first.use(dict(norm_chain=1, moments=1, var=1, rstd=1, xn=1))
        with nc.Block() as block:
            @block.gpsimd
            def _(pool):
                with pool.Fori(0, FF_STEPS) as step:
                    norm_rstd(nc, pool, first, chip, m, step)

            @block.vector
            def _(dve):
                with dve.Fori(0, FF_STEPS) as step:
                    norm_vector(nc, dve, first, m, step, x_tile(chip, step, FF_TILES),
                                lambda t: z[:, bass.ds(step * FF_TILES + t, 1), :].rearrange("p a d -> p (a d)"), [])
                    dve.wait_ge(*first("xn", step, 1))
                nc.vector.memset(xsT[64:P, 0:1], 0.0).then_inc(once["set"], 1)
                nc.vector.memset(fxsT[64:P, :, 0:1], 0.0).then_inc(once["set"], 1)
                nc.vector.memset(v_near[:, :, LD:LD + 1], 1.0)
                nc.vector.memset(v[:, :, :, LD:LD + 1], 1.0).then_inc(once["set"], 1)
                dve.wait_ge(*once("set", 1))

            @block.sync
            def _(sp):
                sp.dma_start(base[:, :, :, :], dram["T_base"]).then_inc(once["loaded"], 16)
                sp.dma_start(ident_bf[:, :], dram["ident_bf"]).then_inc(once["loaded"], 16)
                sp.dma_start(band[:, :, :], dram["T_band"]).then_inc(once["loaded"], 16)
                sp.wait_ge(*once("loaded", 1))

        first.ended(FF_STEPS)
        once.ended(1)
        ffn.use(STACK_FFN)
        block = ctx.enter_context(nc.Block())

        @block.sync
        def _(sp):
            def load(layer, names, done):
                tiles = dict(wqkv=wqkv, rows=rows, wo=wo, w1=w1, w2=w2, cols=cols, b2=b2)
                for name in names:
                    sp.dma_start(tiles[name][:], layer_view(dram["T_" + name], layer)).then_inc(layer_sig[done], 16)

            load(0, ("wqkv", "rows"), "qkv_weights")
            load(0, ("wo",), "out_weights")
            load(0, ("w1", "w2", "cols", "b2"), "ffn_weights")
            if DEPTH > 1:
                with sp.Fori(0, DEPTH - 1) as layer:
                    sp.wait_ge(*att("proj", (layer + 1) * B))
                    att.settle(sp)
                    sp.wait_ge(*layer_sig("tables", layer, 1))
                    att.settle(sp)
                    load(layer + 1, ("wqkv", "rows"), "qkv_weights")
                    sp.wait_ge(*att("out_psum", (layer + 1) * B))
                    att.settle(sp)
                    load(layer + 1, ("wo",), "out_weights")
                    sp.wait_ge(*ffn("zf", (layer + 1) * FF_STEPS))
                    att.settle(sp)
                    load(layer + 1, ("w1", "w2", "cols", "b2"), "ffn_weights")
            sp.wait_ge(*att("proj", DEPTH * B))
            sp.wait_ge(*layer_sig("tables", DEPTH - 1, 1))
            load(DEPTH, ("wqkv", "rows"), "qkv_weights")

        @block.tensor
        def _(pe):
            def turn_z(ahead, settled):
                pe.wait_ge(*att("z_copy", ahead, 1))
                pe.wait_ge(*att("qkT", ahead))
                pe.wait_ge(*att("ctxT", settled))
                for t in range(HALVES):
                    ins = nc.tensor.transpose(flip[1][:, t * P:(t + 1) * P], zc[:, t, :], chip.ident[:, :])
                ins.then_inc(att["zT_psum"], 1)

            def project(ahead, n):
                if n == 0:
                    pe.wait_ge(*att("xsT", ahead, 1))
                    pe.wait_ge(*att("v", ahead))
                elif n <= CHUNKS:
                    pe.wait_ge(*att("half_turns", ahead, n))
                else:
                    pe.wait_ge(*att("v", ahead, 1))
                for c in range(2):
                    at = (n // HALVES) * INNER + c * 512
                    ins = nc.tensor.matmul(wide[:, c, :], xsT[:, (n % HALVES) * P:(n % HALVES + 1) * P],
                                           wqkv[:, at:at + 512], start=True, stop=True)
                ins.then_inc(att["proj"], 1)

            def turn_qk(ahead, n):
                chunk, part = n % CHUNKS, n // CHUNKS
                pe.wait_ge(*att("qk", ahead, chunk + 1))
                if n > 0 and n != 5:
                    pe.wait_ge(*att("qkT", ahead, n if n <= CHUNKS else n - 1))
                for i in range(4):
                    pair = 4 * part + i
                    ins = nc.tensor.transpose(turn_flip(n)[:, i * P:(i + 1) * P], qk[:, chunk, pair * P:(pair + 1) * P],
                                              chip.ident[:, :])
                ins.then_inc(att["qkT_psum"], 1)

            def score(step, n):
                pe.wait_ge(*att("shifted", step, n))
                if n % 4 == 0:
                    pe.wait_ge(*att("qkT", step, n + 4))
                for h in range(2):
                    nc.tensor.matmul(score_psum[:, h, 0:HALVES * REACH], ident_bf[:, :],
                                     band[:, :, :].rearrange("p t k -> p (t k)"), start=True, stop=False,
                                     skip_group_check=True)
                for t in range(HALVES):
                    for h in range(2):
                        of_head = slice(h * LD, (h + 1) * LD)
                        first_key, at = (0, WINDOW) if t == 0 else (P - WINDOW, REACH)
                        ins = nc.tensor.matmul(score_psum[:, h, at:HALVES * REACH if t else REACH],
                                               qkT[of_head, 0, n, t * P:(t + 1) * P],
                                               qkT[of_head, 1, n, first_key:(t + 1) * P],
                                               start=False, stop=t == HALVES - 1, skip_group_check=True)
                ins.then_inc(att["scores"], 1)

            def turn_probs(step, n):
                pe.wait_ge(*att("probs", step, n + 1))
                pe.wait_ge(*att("probsT", step, n))
                if n == 0:
                    pe.wait_ge(*att("qkT", step, 2 * CHUNKS))
                    pe.wait_ge(*att("ctxT", step))
                    pe.wait_ge(*att("context", step))
                elif n == 1:
                    pe.wait_ge(*att("z", step))
                else:
                    pe.wait_ge(*att("context", step, n - 1))
                for h in range(2):
                    for t in range(HALVES):
                        nc.tensor.transpose(flip[0][:, (2 * h + t) * P:(2 * h + t + 1) * P],
                                            probs[:, n % 2, h, t, WINDOW:REACH], chip.ident[:, :])
                    ins = nc.tensor.transpose(near_psum(n)[:, h, :], probs[0:WINDOW, n % 2, h, 1, 0:WINDOW],
                                              chip.ident[0:WINDOW, 0:WINDOW])
                ins.then_inc(att["probsT_psum"], 1)

            def weigh(step, n):
                pe.wait_ge(*att("probsT", step, n + 1))
                if n == 0:
                    pe.wait_ge(*att("v", step, HALVES))
                for h in range(2):
                    head = 2 * n + h
                    for t in range(HALVES):
                        nc.tensor.matmul(pv_of(n)[:, h, t, :], probsT[:, n % 2, h, t, :], v[:, t, head, :],
                                         start=True, stop=t == 0, skip_group_check=True)
                    ins = nc.tensor.matmul(pv_of(n)[0:WINDOW, h, 1, :], near[:, n % 2, h, :], v_near[:, head, :],
                                           start=False, stop=True, skip_group_check=True)
                ins.then_inc(att["pv"], 1)

            def turn_context(step, n, ahead=None):
                pe.wait_ge(*att("context", step, 2 * n + 2))
                if n > 1:
                    pe.wait_ge(*att("ctxT", step, n - 1))
                elif ahead is not None:
                    pe.wait_ge(*att("qkT", ahead, 7 + n))
                for i in range(2):
                    for t in range(HALVES):
                        c = 2 * n + i
                        ins = nc.tensor.transpose(ctx_flip(n)[:, (2 * i + t) * P:(2 * i + t + 1) * P],
                                                  context[:, t, c * P:(c + 1) * P], chip.ident[:, :])
                ins.then_inc(att["ctxT_psum"], 1)

            def output(step):
                for n in range(4):
                    pe.wait_ge(*att("ctxT", step, n + 1))
                    for c in (2 * n, 2 * n + 1):
                        for t in range(HALVES):
                            ins = nc.tensor.matmul(acc[1][:, t * P:(t + 1) * P], ctxT[:, c, t * P:(t + 1) * P], wo[:, c, :],
                                                   start=c == 0 and t == 0, stop=c == LPAIRS - 1, skip_group_check=True)
                ins.then_inc(att["out_psum"], 1)

            def ffn_piece(step, n, banks):
                left, right = banks[:, 0, :], banks[:, 1, :]
                if n == 0:
                    pe.wait_ge(*ffn("f_copy", step, 1))
                    pe.wait_ge(*ffn("zf", step))
                    for t in range(FF_TILES):
                        ins = nc.tensor.transpose(left[:, t * P:(t + 1) * P], fz[:, t, :], chip.ident[:, :])
                    ins.then_inc(ffn["fzT_psum"], 1)
                elif n == 1:
                    pe.wait_ge(*ffn("fxsT", step, 1))
                    for t in range(FF_TILES):
                        ins = nc.tensor.transpose(right[:, t * P:(t + 1) * P], fxsT[:, t // 2, (t % 2) * P:(t % 2 + 1) * P],
                                                  chip.ident[:, :])
                    ins.then_inc(ffn["fxs_psum"], 1)
                elif n == 2:
                    pe.wait_ge(*ffn("xn", step, 1))
                    for t in range(FF_TILES):
                        ins = nc.tensor.transpose(left[:, t * P:(t + 1) * P], fxn[:, t, :], chip.ident[:, :])
                    ins.then_inc(ffn["fxnT_psum"], 1)
                elif n < FF_PIECES - 1:
                    c = n - 3
                    width = min(P, FF - c * P)
                    if c == 0:
                        pe.wait_ge(*ffn("fxnT", step, 1))
                    else:
                        pe.wait_ge(*ffn("hidden", step, c))
                    for half in range(2):
                        at = half * FF + c * P
                        ins = nc.tensor.matmul(banks[0:width, half, :], w1[:, at:at + width], fxnT[:, :],
                                               start=True, stop=True)
                    ins.then_inc(ffn["h_psum"], 1)
                else:
                    pe.wait_ge(*ffn("hidden", step, FF_CHUNKS))
                    for t in range(FF_TILES):
                        for c in range(FF_CHUNKS):
                            width = min(P, FF - c * P)
                            ins = nc.tensor.matmul(left[:, t * P:(t + 1) * P], hidden[0:width, c, t * P:(t + 1) * P],
                                                   w2[0:width, c, :], start=c == 0, stop=c == FF_CHUNKS - 1)
                    ins.then_inc(ffn["f_psum"], 1)

            pe.wait_ge(*layer_sig("qkv_weights", 0, 32))
            turn_z(0, 0)
            for n in range(CHUNKS + HALVES):
                project(0, n)
            for n in range(2 * CHUNKS):
                turn_qk(0, n)
            with pe.Fori(0, DEPTH) as layer:
                start = layer * B
                pe.wait_ge(*layer_sig("out_weights", layer, 16))
                pe.wait_ge(*ffn("zf", layer * FF_STEPS))
                score(start, 0)
                att.settle(pe)
                with pe.Fori(0, B - 1) as b:
                    step = layer * B + b
                    ahead = step + 1
                    for n in range(LPAIRS):
                        if n + 1 < LPAIRS:
                            score(step, n + 1)
                        if n > 0:
                            weigh(step, n - 1)
                        if n == 0:
                            turn_z(ahead, step)
                        if n >= CHUNKS:
                            turn_qk(ahead, n - CHUNKS)
                        turn_probs(step, n)
                        if n <= CHUNKS:
                            project(ahead, n)
                    score(ahead, 0)
                    turn_qk(ahead, 4)
                    weigh(step, LPAIRS - 1)
                    for n in range(5, 8):
                        turn_qk(ahead, n)
                    for n in range(4):
                        turn_context(step, n, ahead)
                        if n == 1:
                            project(ahead, CHUNKS + 1)
                    output(step)
                last, ahead = start + (B - 1), start + B
                f_start = layer * FF_STEPS
                pe.wait_ge(*layer_sig("ffn_weights", layer, 64))
                pe.wait_ge(*att("v", ahead))
                for n in range(LPAIRS):
                    pieces = beside(n)
                    if n + 1 < LPAIRS:
                        score(last, n + 1)
                    ffn_piece(f_start + pieces[0] // FF_PIECES, pieces[0] % FF_PIECES, wide)
                    if n > 0:
                        weigh(last, n - 1)
                    ffn_piece(f_start + pieces[1] // FF_PIECES, pieces[1] % FF_PIECES, wide)
                    turn_probs(last, n)
                    for piece in pieces[2:]:
                        ffn_piece(f_start + piece // FF_PIECES, piece % FF_PIECES, wide)
                weigh(last, LPAIRS - 1)
                for n in range(4):
                    turn_context(last, n)
                output(last)
                f_last = f_start + (FF_STEPS - 1)
                pe.wait_ge(*layer_sig("qkv_weights", layer + 1, 32))
                pe.wait_ge(*att("shifted", ahead))
                ffn_piece(f_last, 0, score_psum)
                turn_z(ahead, ahead)
                ffn_piece(f_last, 1, score_psum)
                project(ahead, 0)
                ffn_piece(f_last, 2, score_psum)
                ffn_piece(f_last, 3, score_psum)
                project(ahead, 1)
                ffn_piece(f_last, 4, score_psum)
                ffn_piece(f_last, 5, score_psum)
                project(ahead, 2)
                ffn_piece(f_last, 6, score_psum)
                project(ahead, 3)
                project(ahead, 4)
                turn_qk(ahead, 0)
                project(ahead, 5)
                for n in range(1, 2 * CHUNKS):
                    turn_qk(ahead, n)

        @block.scalar
        def _(act):
            def shifted_copy(target, bank, done):
                nc.scalar.activation(target[0:64], bank[0:64], ACT.Copy)
                tokens = len(target.shape) - 1
                if tokens == 1:
                    ins = nc.scalar.activation(target[64:P, 1:SEQ], bank[64:P, 0:SEQ - 1], ACT.Copy)
                else:
                    ins = nc.scalar.activation(target[64:P, :, 1:SEQ], bank[64:P, :, 0:SEQ - 1], ACT.Copy)
                ins.then_inc(done, 1)

            def shifted_z(ahead):
                act.wait_ge(*att("zT_psum", ahead, 1))
                act.wait_ge(*att("proj", ahead))
                shifted_copy(xsT[:, :], flip[1][:, 0:SEQ], att["xsT"])

            def squares(ahead, n):
                act.wait_ge(*att("proj", ahead, n + 1))
                act.wait_ge(*att("norm2", ahead, max(n - 1, 0)))
                nc.scalar.activation(square[:, n % 2, :], wide[:, :, :].rearrange("p a n -> p (a n)"), ACT.Square)\
                  .then_inc(att["square"], 1)

            def copy_v(ahead, t):
                act.wait_ge(*att("proj", ahead, CHUNKS + t + 1))
                if t == 0:
                    act.wait_ge(*att("pv", ahead))
                heads = lambda rows: wide[rows, :, :].rearrange("p a (h d) -> p (a h) d", d=LD)
                if t == 0:
                    nc.scalar.activation(v_near[:, :, 0:LD], heads(slice(P - WINDOW, P)), ACT.Copy)
                nc.scalar.activation(v[:, t, :, 0:LD], heads(slice(0, P)), ACT.Copy)\
                  .then_inc(att["v"], 1)

            def copy_qkT(ahead, n, scored):
                chunk, part = n % CHUNKS, n // CHUNKS
                act.wait_ge(*att("qkT_psum", ahead, n + 1))
                act.wait_ge(*scored)
                target = qkT[:, chunk // 2, 4 * part:4 * part + 4, (chunk % 2) * P:(chunk % 2 + 1) * P]
                nc.scalar.activation(target, tiles4(turn_flip(n)), ACT.Copy).then_inc(att["qkT"], 1)

            def exponential(step, n):
                act.wait_ge(*att("shifted", step, n + 1))
                act.wait_ge(*att("probsT_psum", step, max(n - 1, 0)))
                nc.scalar.activation(probs[:, n % 2], shifted[:, n % 2], ACT.Exp).then_inc(att["probs"], 1)

            def copy_probsT(step, n):
                act.wait_ge(*att("probsT_psum", step, n + 1))
                act.wait_ge(*att("pv", step, max(n - 1, 0)))
                nc.scalar.activation(probsT[:, n % 2].rearrange("p h t q -> p (h t) q"), tiles4(flip[0]), ACT.Copy)
                nc.scalar.activation(near[:, n % 2], near_psum(n), ACT.Copy).then_inc(att["probsT"], 1)

            def copy_ctxT(step, n):
                if n == 0:
                    act.wait_ge(*att("out_psum", step))
                act.wait_ge(*att("ctxT_psum", step, n + 1))
                nc.scalar.activation(ctxT[:, 2 * n:2 * n + 2, :], ctx_flip(n)[:, :].rearrange("p (c s) -> p c s", c=2), ACT.Copy)\
                  .then_inc(att["ctxT"], 1)

            def ffn_piece(step, n, banks):
                if n == 0:
                    act.wait_ge(*ffn("fzT_psum", step, 1))
                    act.wait_ge(*ffn("fxs_psum", step))
                    shifted_copy(fxsT[:, :, :], banks[:, 0, :].rearrange("p (b s) -> p b s", b=2), ffn["fxsT"])
                elif n == 2:
                    act.wait_ge(*ffn("fxnT_psum", step, 1))
                    act.wait_ge(*ffn("h_psum", step))
                    nc.scalar.activation(fxnT[:, :], banks[:, 0, :], ACT.Identity, scale=cols[:, 2 * FF_CHUNKS:2 * FF_CHUNKS + 1],
                                         bias=cols[:, 2 * FF_CHUNKS + 1:2 * FF_CHUNKS + 2]).then_inc(ffn["fxnT"], 1)
                elif 3 <= n < FF_PIECES - 1:
                    c = n - 3
                    width = min(P, FF - c * P)
                    act.wait_ge(*ffn("h_psum", step, c + 1))
                    act.wait_ge(*ffn("hidden", step, max(c - 1, 0)))
                    nc.scalar.activation(gelu[0:width, c % 2, :], banks[0:width, 1, :], ACT.Gelu,
                                         bias=cols[0:width, FF_CHUNKS + c:FF_CHUNKS + c + 1]).then_inc(ffn["gelu"], 1)

            shifted_z(0)
            for n in range(CHUNKS):
                squares(0, n)
            for t in range(HALVES):
                copy_v(0, t)
            for n in range(2 * CHUNKS):
                copy_qkT(0, n, att("scores", 0))
            with act.Fori(0, DEPTH) as layer:
                start = layer * B
                exponential(start, 0)
                with act.Fori(0, B - 1) as b:
                    step = layer * B + b
                    ahead = step + 1
                    for n in range(LPAIRS):
                        if n == 0:
                            shifted_z(ahead)
                        if n >= CHUNKS:
                            copy_qkT(ahead, n - CHUNKS, att("scores", step, 4))
                        copy_probsT(step, n)
                        if n + 1 < LPAIRS:
                            exponential(step, n + 1)
                        if n < CHUNKS:
                            squares(ahead, n)
                    copy_qkT(ahead, 4, att("scores", step, LPAIRS))
                    exponential(ahead, 0)
                    for n in range(5, 8):
                        copy_qkT(ahead, n, att("scores", step, LPAIRS))
                    copy_v(ahead, 0)
                    for n in range(4):
                        copy_ctxT(step, n)
                        if n == 1:
                            copy_v(ahead, 1)
                last, ahead = start + (B - 1), start + B
                f_start = layer * FF_STEPS
                act.wait_ge(*layer_sig("ffn_weights", layer, 64))
                for n in range(LPAIRS):
                    pieces = beside(n)
                    for piece in pieces[:2]:
                        ffn_piece(f_start + piece // FF_PIECES, piece % FF_PIECES, wide)
                    copy_probsT(last, n)
                    if n + 1 < LPAIRS:
                        exponential(last, n + 1)
                    for piece in pieces[2:]:
                        ffn_piece(f_start + piece // FF_PIECES, piece % FF_PIECES, wide)
                for n in range(4):
                    copy_ctxT(last, n)
                f_last = f_start + (FF_STEPS - 1)
                ffn_piece(f_last, 0, score_psum)
                shifted_z(ahead)
                squares(ahead, 0)
                ffn_piece(f_last, 2, score_psum)
                ffn_piece(f_last, 3, score_psum)
                squares(ahead, 1)
                ffn_piece(f_last, 4, score_psum)
                ffn_piece(f_last, 5, score_psum)
                squares(ahead, 2)
                squares(ahead, 3)
                copy_v(ahead, 0)
                copy_qkT(ahead, 0, att("scores", ahead))
                copy_v(ahead, 1)
                for n in range(1, 2 * CHUNKS):
                    copy_qkT(ahead, n, att("scores", ahead))

        @block.gpsimd
        def _(pool):
            def rotate_and_scale(ahead):
                pool.wait_ge(*att("qkT_psum", ahead))
                for n in range(CHUNKS):
                    pool.wait_ge(*att("half_turns", ahead, n + 1))
                    nc.gpsimd.tensor_tensor(qk[:, n, :], halves[:, n % 2, 0, :], halves[:, n % 2, 1, :], ALU.add)\
                      .then_inc(att["turn_sum"], 1)
                    pool.wait_ge(*att("clamped", ahead, n + 1))
                    if n == 0:
                        pool.wait_ge(*att("qk", ahead))
                    nc.gpsimd.tensor_tensor(rnorm[:, n, :], clamped[:, n, :], chip.minus_half[:, :].to_broadcast([P, LH]), ALU.pow)\
                      .then_inc(att["rnorm"], 1)
                    pool.wait_ge(*att("rnorm", ahead, n + 1))
                    pool.wait_ge(*att("turn_sum", ahead, n + 1))
                    heads = qk[:, n, :].rearrange("p (h d) -> p h d", d=LD)
                    nc.gpsimd.tensor_tensor(heads, heads, rnorm[:, n, :].rearrange("p (h o) -> p h o", o=1).to_broadcast([P, LH, LD]),
                                            ALU.mult).then_inc(att["qk"], 1)

            rotate_and_scale(0)
            with pool.Fori(0, DEPTH) as layer:
                with pool.Fori(0, B - 1) as b:
                    rotate_and_scale(layer * B + b + 1)
                with pool.Fori(0, FF_STEPS) as s:
                    step = layer * FF_STEPS + s
                    pool.wait_ge(*ffn("var", step, 1))
                    nc.gpsimd.tensor_tensor(rstd[:, :], var[:, :], chip.minus_half[:, :].to_broadcast([P, FF_TILES]), ALU.pow)\
                      .then_inc(ffn["rstd"], 1)
                rotate_and_scale(layer * B + B)

        @block.vector
        def _(dve):
            def copy_z(ahead, b):
                dve.wait_ge(*att("zT_psum", ahead))
                nc.vector.tensor_copy(zc[:, :, :], z[:, bass.ds(b * HALVES, HALVES), :]).then_inc(att["z_copy"], 1)

            def rotate(ahead, n):
                dve.wait_ge(*att("proj", ahead, n + 1))
                if n == 0:
                    dve.wait_ge(*att("rnorm", ahead))
                dve.wait_ge(*att("square", ahead, n + 1))
                dve.wait_ge(*att("turn_sum", ahead, max(n - 1, 0)))
                which, t = n // 2, n % 2
                heads = wide[:, :, :].rearrange("p a (h d) -> p (a h) d", d=LD)
                out = halves[:, n % 2].rearrange("p k (h d) -> p k h d", d=LD)
                cos = tables[:, 2 * which, t:t + 1, :]
                sin = tables[:, 2 * which + 1, t:t + 1, :]
                nc.vector.tensor_tensor(out[:, 0], heads, cos.to_broadcast([P, LH, LD]), ALU.mult)
                for half in range(2):
                    to, of = (slice(0, LD // 2), slice(LD // 2, LD))[::1 if half == 0 else -1]
                    ins = nc.vector.tensor_tensor(out[:, 1, :, to], heads[:, :, of], sin[:, :, to].to_broadcast([P, LH, LD // 2]),
                                                  ALU.mult)
                ins.then_inc(att["half_turns"], 1)

            def norms(ahead, n):
                nc.vector.tensor_reduce(norm2[:, n, :], square[:, n % 2, :].rearrange("p (h d) -> p h d", d=LD), AX.X, ALU.add)\
                  .then_inc(att["norm2"], 1)
                dve.wait_ge(*att("norm2", ahead, n + 1))
                nc.vector.tensor_scalar(clamped[:, n, :], norm2[:, n, :], 1e-24, None, ALU.max).then_inc(att["clamped"], 1)

            def shift(step, n):
                dve.wait_ge(*att("scores", step, n + 1))
                dve.wait_ge(*att("shifted", step, max(n - 1, 0)))
                nc.vector.tensor_reduce(negmax[:, n % 2, :, :, 0], scores, AX.X, ALU.max, negate=True)\
                  .then_inc(att["negmax"], 1)
                dve.wait_ge(*att("negmax", step, n + 1))
                dve.wait_ge(*att("probs", step, max(n - 1, 0)))
                nc.vector.tensor_tensor(shifted[:, n % 2], scores, negmax[:, n % 2].to_broadcast([P, 2, HALVES, REACH]), ALU.add)\
                  .then_inc(att["shifted"], 1)

            def divide(step, n):
                dve.wait_ge(*att("pv", step, n + 1))
                dve.wait_ge(*att("context", step, max(n - 1, 0)))
                nc.vector.reciprocal(rsum[:, n % 2], pv_of(n)[:, :, :, LD:LD + 1]).then_inc(att["rsum"], 1)
                dve.wait_ge(*att("rsum", step, n + 1))
                if n == 0:
                    dve.wait_ge(*att("ctxT_psum", step))
                to = context[:, :, 2 * n * LD:2 * (n + 1) * LD].rearrange("p t (h d) -> p h t d", h=2)
                nc.vector.tensor_tensor(to, pv_of(n)[:, :, :, 0:LD], rsum[:, n % 2].to_broadcast([P, 2, HALVES, LD]), ALU.mult)\
                  .then_inc(att["context"], 1)

            def add_output(step, b):
                z_of = z[:, bass.ds(b * HALVES, HALVES), :]
                dve.wait_ge(*att("out_psum", step, 1))
                nc.vector.tensor_tensor(z_of, tiles4(acc[1])[:, 0:HALVES, :], z_of, ALU.add).then_inc(att["z"], 1)
                dve.wait_ge(*att("z", step, 1))

            def scale_tables(layer):
                dve.wait_ge(*layer_sig("qkv_weights", layer, 32))
                dve.wait_ge(*att("half_turns", layer * B))
                nc.vector.tensor_tensor(tables[:, :, :, :], base[:, :, :, :], rows[:, :, :, :].to_broadcast([P, 4, HALVES, LD]), ALU.mult)\
                  .then_inc(layer_sig["tables"], 1)
                dve.wait_ge(*layer_sig("tables", layer, 1))

            def copy_ff(step, s):
                dve.wait_ge(*ffn("fzT_psum", step))
                nc.vector.tensor_copy(fz[:, :, :], z[:, s * FF_TILES:(s + 1) * FF_TILES, :]).then_inc(ffn["f_copy"], 1)

            def ffn_piece(step, s, n, banks):
                left, right = banks[:, 0, :], banks[:, 1, :]
                if n == 1:
                    dve.wait_ge(*ffn("fxs_psum", step, 1))
                    for t in range(FF_TILES):
                        ins = nc.vector.bn_stats(stats[:, t, :], right[:, t * P:(t + 1) * P])
                    ins.then_inc(ffn["norm_chain"], 1)
                    ffn.apart(dve, "norm_chain", step, 1)
                    for t in range(FF_TILES):
                        ins = nc.vector.bn_aggr(moments[:, t, :], stats[:, t, :])
                    ins.then_inc(ffn["moments"], 1)
                    dve.wait_ge(*ffn("moments", step, 1))
                    nc.vector.tensor_scalar(var[:, :], moments[:, :, 1], EPS, None, ALU.add).then_inc(ffn["var"], 1)
                    dve.wait_ge(*ffn("rstd", step, 1))
                    dve.wait_ge(*ffn("fxnT_psum", step))
                    for t in range(FF_TILES):
                        ins = nc.vector.tensor_scalar(fxn[:, t, :], right[:, t * P:(t + 1) * P], moments[:, t, 0:1],
                                                      rstd[:, t:t + 1], ALU.subtract, ALU.mult)
                    ins.then_inc(ffn["xn"], 1)
                elif 3 <= n < FF_PIECES - 1:
                    c = n - 3
                    width = min(P, FF - c * P)
                    if c == 0:
                        dve.wait_ge(*ffn("f_psum", step))
                    dve.wait_ge(*ffn("gelu", step, c + 1))
                    nc.vector.scalar_tensor_tensor(hidden[0:width, c, :], left[0:width, :], cols[0:width, c:c + 1],
                                                   gelu[0:width, c % 2, :], ALU.add, ALU.mult).then_inc(ffn["hidden"], 1)
                elif n == FF_PIECES - 1:
                    z_of = z[:, s * FF_TILES:(s + 1) * FF_TILES, :]
                    dve.wait_ge(*ffn("f_psum", step, 1))
                    nc.vector.tensor_tensor(z_of, tiles4(left), z_of, ALU.add).then_inc(ffn["zf"], 1)
                    dve.wait_ge(*ffn("zf", step, 1))
                    nc.vector.tensor_tensor(z_of, z_of, b2[:, :, :].to_broadcast([P, FF_TILES, D]), ALU.add).then_inc(ffn["zf"], 1)
                    dve.wait_ge(*ffn("zf", step, 2))
                    if s + 1 < FF_STEPS - 1:
                        copy_ff(step + 1, s + 1)

            copy_z(0, 0)
            scale_tables(0)
            for n in range(CHUNKS):
                rotate(0, n)
                norms(0, n)
            with dve.Fori(0, DEPTH) as layer:
                start = layer * B
                shift(start, 0)
                att.settle(dve)
                with dve.Fori(0, B - 1) as b:
                    step = layer * B + b
                    ahead = step + 1
                    copy_z(ahead, b + 1)
                    for n in range(LPAIRS):
                        if 1 <= n <= CHUNKS:
                            rotate(ahead, n - 1)
                        if n + 1 < LPAIRS:
                            shift(step, n + 1)
                        if n > 0:
                            divide(step, n - 1)
                        if 1 <= n <= CHUNKS:
                            norms(ahead, n - 1)
                    shift(ahead, 0)
                    divide(step, LPAIRS - 1)
                    add_output(step, b)
                last, ahead = start + (B - 1), start + B
                f_start = layer * FF_STEPS
                dve.wait_ge(*layer_sig("ffn_weights", layer, 64))
                copy_ff(f_start, 0)
                for n in range(LPAIRS):
                    pieces = beside(n)
                    if n + 1 < LPAIRS:
                        shift(last, n + 1)
                    ffn_piece(f_start + pieces[0] // FF_PIECES, pieces[0] // FF_PIECES, pieces[0] % FF_PIECES, wide)
                    if n > 0:
                        divide(last, n - 1)
                    for piece in pieces[1:]:
                        ffn_piece(f_start + piece // FF_PIECES, piece // FF_PIECES, piece % FF_PIECES, wide)
                divide(last, LPAIRS - 1)
                add_output(last, B - 1)
                f_last = f_start + (FF_STEPS - 1)
                copy_ff(f_last, FF_STEPS - 1)
                copy_z(ahead, 0)
                scale_tables(layer + 1)
                for n in range(CHUNKS):
                    ffn_piece(f_last, FF_STEPS - 1, (1, 3, 5, 6)[n], score_psum)
                    rotate(ahead, n)
                    norms(ahead, n)
                    if n == 1:
                        ffn_piece(f_last, FF_STEPS - 1, 4, score_psum)
            nc.vector.scalar_tensor_tensor(chip.x[:, :, :], z[:, :, :], 0.5, chip.x[:, :, :], ALU.mult, ALU.add)
    att.ended(DEPTH * B)
    att.ended(1, STACK_AHEAD)
    ffn.ended(DEPTH * FF_STEPS)
    layer_sig.ended(DEPTH)
    layer_sig.ended(1, ("qkv_weights", "tables"))


def layer_view(a, layer):
    part = a[bass.ds(layer, 1)]
    names = " ".join("cde"[:len(a.shape) - 2])
    return part.rearrange(f"a p {names} -> (a p) {names}")


def loop_signals():
    stages = [moe_signals(gated, 1) for gated in (False, True)] + [attention_signals(level) for level in (0, 2, 3)]
    return sorted(set().union(*stages, L1_FFN_SIGNALS, RW_SIGNALS, STACK_ATTENTION))


def program(nc, dram, out, stages):
    with ExitStack() as ctx:
        chip = Chip(nc, ctx, dram, loop_signals())
        cossin = ctx.enter_context(nc.sbuf_tensor("cossin", [P, 2, D], F32))
        begin = chip.once
        begin.use(dict(loaded=32, set=1))
        with nc.Block() as block:
            @block.sync
            def _(sp):
                sp.dma_start(chip.x[:, :, :], dram["x"].rearrange("b (h p) d -> p (b h) d", p=P)).then_inc(begin["loaded"], 16)
                sp.dma_start(chip.ident[:, :], dram["ident"]).then_inc(begin["loaded"], 16)
                sp.wait_ge(*begin("loaded", 1))

            @block.gpsimd
            def _(pool):
                chip.loop.seed(pool)
                chip.ffn.seed(pool)

            @block.vector
            def _(dve):
                nc.vector.memset(chip.minus_half[:, :], -0.5).then_inc(begin["set"], 1)
                dve.wait_ge(*begin("set", 1))
        begin.ended(1)
        setup_l1_angles(chip, cossin)
        for number, (level, part) in enumerate(stages):
            chip.tag = f"stage{number}_"
            if part == "attention" and level == 1:
                stage_rwkv(chip)
            elif part == "attention":
                stage_attention(chip, level)
            elif level == 1:
                stage_l1_ffn(chip, cossin)
            elif level == 2:
                stage_stack(chip)
            else:
                stage_moe(chip, level)
        end = chip.once
        end.use(dict(loaded=16))
        with nc.Block() as block:
            @block.sync
            def _(sp):
                sp.dma_start(out.rearrange("b (h p) d -> p (b h) d", p=P), chip.x[:, :, :]).then_inc(end["loaded"], 16)
                sp.wait_ge(*end("loaded", 1))


STAGES = [(level, part) for level in range(4) for part in ("ffn", "attention", "ffn")]


def kernel(**inputs):
    import concourse.bacc as bacc
    from concourse.bass_utils import run_bass_kernel_spmd

    nc = bacc.Bacc("TRN2", target_bir_lowering=False, num_devices=1)
    arrays, dram = {}, {}
    for name, a in layout(inputs).items():
        a = np.ascontiguousarray(a)
        arrays["in_" + name] = a
        dram[name] = nc.dram_tensor("in_" + name, a.shape, mybir.dt.from_np(a.dtype), kind="ExternalInput").ap()
    out = nc.dram_tensor("out", (B, SEQ, D), F32, kind="ExternalOutput").ap()
    program(nc, dram, out, STAGES)
    r = run_bass_kernel_spmd(nc, [arrays], core_ids=[0])
    return r.results[0]["out"]


def layout(inputs):
    w = {name: np.asarray(a) for name, a in inputs.items()}
    a = {"x": w["L0_attn_embeddings"], "ident": np.eye(P, dtype=np.float32)}
    for name in ("L1_ffn_theta", "L1_ffn_phi", "L1_ffn_theta_noise", "L1_ffn_phi_noise"):
        a[name] = w[name]
    rows = lambda v: np.broadcast_to(v, (P,) + v.shape)
    a["iota"] = rows(np.arange(EXPERTS, dtype=np.float32))
    split = lambda v: v.reshape(v.shape[0], -1, P, v.shape[-1]).transpose(2, 0, 1, 3)
    a["L0_w_gate"], a["L0_b_gate"] = w["L0_ffn_Wr"].T, rows(w["L0_ffn_br"])
    a["L0_w_up"] = w["L0_ffn_W1"].transpose(2, 0, 1)
    a["L0_b_up"] = w["L0_ffn_b1"].reshape(EXPERTS, -1, P).transpose(2, 0, 1)
    a["L0_w_down"] = split(w["L0_ffn_W2"].transpose(0, 2, 1))
    a["L0_b_down"] = w["L0_ffn_b2"]
    a["L0_gamma"], a["L0_beta"] = rows(w["L0_ffn_gamma"]), rows(w["L0_ffn_beta"])
    a["L3_w_gate"] = w["L3_ffn_gate_kernel"]
    a["L3_w_up"], a["L3_w_up2"] = (w[n].transpose(1, 0, 2) for n in ("L3_ffn_w0_kernel", "L3_ffn_w1_kernel"))
    a["L3_w_down"] = split(w["L3_ffn_wo_kernel"])
    attention_layout(w, a, rows)
    rwkv_layout(w, a)
    stack_layout(w, a)
    return a


def attention_layout(w, a, rows):
    bf16 = mybir.dt.np(BF16)
    a["ident_bf"] = np.eye(P, dtype=np.float32).astype(bf16)
    above = np.triu(np.full((P, P), MASKED, np.float32), 1)
    a["mask"], a["maskT"] = above.astype(bf16), np.ascontiguousarray(above.T).astype(bf16)

    def banded(v, ninth=0.0):
        out = np.zeros((v.shape[0], GROUPS, GROUPS, BAND), np.float32)
        out[..., :DK] = v.reshape(v.shape[0], GROUPS, GROUPS, DK)
        out[..., DK] = ninth
        return out.reshape(v.shape[0], GROUPS, P)

    pairs = np.arange(D) ^ 1
    heads = lambda v: v.transpose(1, 0, 2).reshape(D, D)
    q0, k0, v0 = (w["L0_attn_W" + n] for n in "qkv")
    a["A0_wq"], a["A0_wk"], a["A0_wv"] = banded(heads(q0)), banded(heads(k0)), heads(v0)
    a["A0_bq"] = banded(w["L0_attn_bq"].reshape(1, D))[0].T
    a["A0_bk"] = banded(w["L0_attn_bk"].reshape(1, D), 1.0)[0].T
    a["A0_bv"], a["A0_wo"], a["A0_bo"] = rows(w["L0_attn_bv"].reshape(D)), w["L0_attn_Wo"], rows(w["L0_attn_bo"])
    q2, k2, v2 = (w["L2_attn_w_qkv"][:, n * D:(n + 1) * D] for n in range(3))
    bq2, bk2, bv2 = (w["L2_attn_b_qkv"][n * D:(n + 1) * D] for n in range(3))
    a["A2_wq"], a["A2_wk"], a["A2_wv"] = banded(q2), banded(k2), v2
    a["A2_bq"], a["A2_bk"], a["A2_bv"] = banded(bq2.reshape(1, D))[0].T, banded(bk2.reshape(1, D), 1.0)[0].T, rows(bv2)
    a["A2_wo"], a["A2_bo"] = w["L2_attn_w_out"], rows(w["L2_attn_b_out"])
    a["A2_gamma"], a["A2_beta"] = w["L2_attn_ln_gamma"].reshape(D, 1), w["L2_attn_ln_beta"].reshape(D, 1)
    q3, k3, v3 = (w["L3_attn_Wqkv"][:, n * D:(n + 1) * D] for n in range(3))
    a["A3_wq"], a["A3_wk"], a["A3_wv"] = banded(q3), banded(k3), v3
    a["A3_wq_swap"], a["A3_wk_swap"] = banded(q3[:, pairs]), banded(k3[:, pairs])
    a["A3_wo"], a["A3_bo"] = w["L3_attn_Wout"], rows(w["L3_attn_bout"])
    theta = np.power(np.float32(10000.0), (-2.0 * (np.arange(DK // 2, dtype=np.float32) - 1.0) / DK).astype(np.float32))
    angle = (np.arange(SEQ, dtype=np.float32)[:, None] * theta.astype(np.float32)[None, :]).astype(np.float64)
    sign = np.tile([-1.0, 1.0], DK // 2)
    tables = [np.repeat(np.cos(angle), 2, axis=1), np.repeat(np.sin(angle), 2, axis=1) * sign]
    a["A3_rope"] = np.stack([banded(np.tile(t, HEADS).astype(np.float32))[:, 0].T for t in tables], axis=1)


def rwkv_layout(w, a):
    column = lambda v: v.reshape(D, 1)
    a["RW_miu_x"], a["RW_td_miu"], a["RW_u"] = (column(w["L1_attn_" + n]) for n in ("miu_x", "td_miu", "u"))
    a["RW_gamma"], a["RW_beta"] = column(w["L1_attn_gn_gamma"]), column(w["L1_attn_gn_beta"])
    a["RW_lambda"] = w["L1_attn_lambda_"].reshape(MIXES, D).T
    a["RW_A"], a["RW_B"] = w["L1_attn_A_lora"], w["L1_attn_B_lora"].transpose(1, 0, 2)
    a["RW_td_A"], a["RW_td_B"] = w["L1_attn_td_A"], w["L1_attn_td_B"]
    for n in "rkvgo":
        a["RW_w" + n] = w["L1_attn_W" + n].T
    head = np.arange(P) // HS
    a["RW_head_ones"] = (head[:, None] == head[None, :]).astype(np.float32)
    gather = np.zeros((P, P + HS - 1), np.float32)
    gather[np.arange(P), head * HS + HS - 1] = 1.0
    a["RW_gather"] = gather


def stack_layout(w, a):
    t = {n: w["L2_ffn_" + n] for n in ("Wqkv", "q_scale", "k_scale", "Wo", "ln_g", "ln_b", "W1", "b1", "W2", "b2")}
    depth = t["Wqkv"].shape[0]
    a["T_wqkv"] = np.concatenate([t["Wqkv"], t["Wqkv"][-1:]])
    a["T_wo"] = t["Wo"].reshape(depth, LPAIRS, P, D).transpose(0, 2, 1, 3)
    a["T_w1"] = t["W1"]
    w2 = np.zeros((depth, FF_CHUNKS * P, D), np.float32)
    w2[:, :FF] = t["W2"]
    a["T_w2"] = w2.reshape(depth, FF_CHUNKS, P, D).transpose(0, 2, 1, 3)
    b1 = np.zeros((depth, 2, FF_CHUNKS * P), np.float32)
    b1[:, :, :FF] = t["b1"].reshape(depth, 2, FF)
    b1 = b1.reshape(depth, 2 * FF_CHUNKS, P).transpose(0, 2, 1)
    a["T_cols"] = np.concatenate([b1, t["ln_g"][:, :, None], t["ln_b"][:, :, None]], axis=2)
    a["T_b2"] = np.broadcast_to(t["b2"][:, None, None, :], (depth, P, 1, D))
    swap = lambda v: np.roll(v, LD // 2, axis=-1)
    scales = np.stack([t["q_scale"], swap(t["q_scale"]), t["k_scale"], swap(t["k_scale"])], axis=1)
    a["T_rows"] = np.broadcast_to(np.concatenate([scales, scales[-1:]])[:, None, :, None, :], (depth + 1, P, 4, 1, LD))
    half = np.arange(0, LD, 2, dtype=np.float32)
    inv_freq = (1.0 / np.power(np.float32(10000.0), half / LD)).astype(np.float32)
    n = np.arange(SEQ, dtype=np.float32)
    freqs = (n[:, None] * inv_freq[None, :]).astype(np.float64)
    factor = ((half + 0.4 * LD) / (1.4 * LD)).astype(np.float64)[None, :] ** ((n - SEQ // 2) / (WINDOW // 2))[:, None]
    cos, sin, factor = (np.concatenate([v, v], axis=1) for v in (np.cos(freqs), np.sin(freqs), factor))
    sin = sin * np.where(np.arange(LD) < LD // 2, -1.0, 1.0)
    base = np.stack([8 * cos * factor, 8 * sin * factor, cos / factor, sin / factor])
    a["T_base"] = base.astype(np.float32).reshape(4, HALVES, P, LD).transpose(2, 0, 1, 3)
    q = np.arange(P)[:, None, None]
    key = np.arange(REACH)[None, None, :] - WINDOW
    seen = (key <= q) & (key >= q - WINDOW) & ((np.arange(HALVES)[None, :, None] > 0) | (key >= 0))
    a["T_band"] = np.where(seen, 0.0, MASKED).astype(mybir.dt.np(BF16))
```
